# Optimizing a Trainium2 kernel written in Bass

```python
import numpy as np
import jax
import jax.numpy as jnp

def _softmax(x, axis=-1):
    return jax.nn.softmax(x, axis=axis)

def _gelu(x):
    return jax.nn.gelu(x, approximate=True)

def _silu(x):
    return jax.nn.silu(x)

def _sigmoid(x):
    return jax.nn.sigmoid(x)

def _layernorm(x, axis=-1, eps=1e-05):
    m = jnp.mean(x, axis=axis, keepdims=True)
    v = jnp.var(x, axis=axis, keepdims=True)
    return (x - m) / jnp.sqrt(v + eps)

def _scatter_add(tgt, idx, src, axis=0):
    return tgt.at[idx].add(src)

def _segment_sum(src, seg, n):
    return jax.ops.segment_sum(src, seg, n)
kernel_name = 'mk_gnn_resnorm_d4_gnn_r8_32de70'

def setup_inputs(seed: int=0):
    np.random.seed(seed)
    _w = jnp.asarray

    def _rec_inputs():
        import jax
        import jax.numpy as jnp
        _gk = jax.random.key(seed)
        x = -0.000202 + 1 * jax.random.normal(jax.random.fold_in(_gk, 1), (6250, 128), jnp.float32)
        _s = jax.random.randint(jax.random.fold_in(_gk, 2), (100000,), 0, 6250, jnp.int32)
        _d = jax.random.randint(jax.random.fold_in(_gk, 3), (100000,), 0, 6250, jnp.int32)
        _loop = jnp.arange(6250, dtype=jnp.int32)
        src = jnp.concatenate([_s, _d, _loop])
        dst = jnp.concatenate([_d, _s, _loop])
        _o = jnp.argsort(dst, stable=True)
        src = src[_o]
        dst = dst[_o]
        edge_type_32 = jax.random.randint(jax.random.fold_in(_gk, 13), (206250,), 0, 32, jnp.int32)
        edge_weight = jax.random.uniform(jax.random.fold_in(_gk, 14), (206250,), jnp.float32, 0.0, 0.999998)
        edge_weight1 = jax.random.uniform(jax.random.fold_in(_gk, 15), (206250, 1), jnp.float32, 0.0, 0.999998)
        return (x, src, dst, edge_type_32, edge_weight, edge_weight1)
    x, src, dst, edge_type_32, edge_weight, edge_weight1 = _rec_inputs()

    def _L0_gnn_setup():
        import jax, jax.numpy as jnp
        import numpy as np
        N_NODES, N_EDGES = (6250, 100000)
        NODE_D, MSG_D, OUT_D = (128, 128, 128)

        def _linear_params(key, d_in, d_out):
            kw, _ = jax.random.split(key)
            W = jax.random.normal(kw, (d_in, d_out), jnp.float32) * np.float32(1.0 / np.sqrt(d_in))
            b = jnp.zeros((d_out,), jnp.float32)
            return (W, b)
        key = jax.random.key(seed)
        ks = jax.random.split(key, 12)
        node_features = jax.random.normal(ks[0], (N_NODES, NODE_D), jnp.float32)
        src = jax.random.randint(ks[1], (N_EDGES,), 0, N_NODES, dtype=jnp.int32)
        dst = jax.random.randint(ks[2], (N_EDGES,), 0, N_NODES, dtype=jnp.int32)
        W_msg_1, b_msg_1 = _linear_params(ks[3], NODE_D, MSG_D)
        W_msg_2, b_msg_2 = _linear_params(ks[4], MSG_D, MSG_D)
        W_msg_3, b_msg_3 = _linear_params(ks[5], MSG_D, MSG_D)
        W_att_1, b_att_1 = _linear_params(ks[6], 2 * NODE_D, 1)
        W_att_2, b_att_2 = _linear_params(ks[7], 2 * NODE_D, 1)
        W_att_3, b_att_3 = _linear_params(ks[8], 2 * NODE_D, 1)
        W_c1, b_c1 = _linear_params(ks[9], MSG_D + NODE_D, OUT_D)
        W_c2, b_c2 = _linear_params(ks[10], OUT_D, OUT_D)
        return {'node_features': node_features, 'src': src, 'dst': dst, 'W_msg_1': W_msg_1, 'b_msg_1': b_msg_1, 'W_msg_2': W_msg_2, 'b_msg_2': b_msg_2, 'W_msg_3': W_msg_3, 'b_msg_3': b_msg_3, 'W_att_1': W_att_1, 'b_att_1': b_att_1, 'W_att_2': W_att_2, 'b_att_2': b_att_2, 'W_att_3': W_att_3, 'b_att_3': b_att_3, 'W_c1': W_c1, 'b_c1': b_c1, 'W_c2': W_c2, 'b_c2': b_c2}
    _L0_gnn_all = _L0_gnn_setup()
    _L0_gnn_in = {k: v for k, v in _L0_gnn_all.items() if k in ('W_msg_1', 'b_msg_1', 'W_msg_2', 'b_msg_2', 'W_msg_3', 'b_msg_3', 'W_att_1', 'b_att_1', 'W_att_2', 'b_att_2', 'W_att_3', 'b_att_3', 'W_c1', 'b_c1', 'W_c2', 'b_c2')}
    del _L0_gnn_all

    def _L1_gnn_setup():
        import jax, jax.numpy as jnp
        import numpy as np
        N_NODES = 6250
        N_EDGES = 100000
        HIDDEN = 128
        LN_EPS = 1e-05

        def _layernorm(x, gamma, beta):
            mu = jnp.mean(x, axis=-1, keepdims=True)
            var = jnp.mean(jnp.square(x - mu), axis=-1, keepdims=True)
            return (x - mu) * jax.lax.rsqrt(var + LN_EPS) * gamma + beta
        key = jax.random.key(seed)
        k1, k2, k3, k4 = jax.random.split(key, 4)
        node_states = jax.random.normal(k1, (N_NODES, HIDDEN), dtype=jnp.float32)
        edge_index = jax.random.randint(k2, (2, N_EDGES), 0, N_NODES, dtype=jnp.int64)
        W_proj = jax.random.normal(k3, (HIDDEN, HIDDEN), dtype=jnp.float32) / np.sqrt(HIDDEN)
        w_edge = jax.random.normal(k4, (2 * HIDDEN,), dtype=jnp.float32) / np.sqrt(2 * HIDDEN)
        ln_gamma = jnp.ones((HIDDEN,), dtype=jnp.float32)
        ln_beta = jnp.zeros((HIDDEN,), dtype=jnp.float32)
        return {'node_states': node_states, 'edge_index': edge_index, 'W_proj': W_proj, 'w_edge': w_edge, 'ln_gamma': ln_gamma, 'ln_beta': ln_beta}
    _L1_gnn_all = _L1_gnn_setup()
    _L1_gnn_in = {k: v for k, v in _L1_gnn_all.items() if k in ('W_proj', 'w_edge', 'ln_gamma', 'ln_beta')}
    del _L1_gnn_all

    def _L2_gnn_setup():
        import jax, jax.numpy as jnp
        import numpy as np
        N, E, D, F, R, B = (6250, 200000, 128, 128, 32, 8)
        key = jax.random.key(seed)
        ks = jax.random.split(key, 9)
        h = jax.random.normal(ks[0], (N, D), dtype=jnp.float32)
        src = jax.random.randint(ks[1], (E,), 0, N, dtype=jnp.int32)
        dst = jax.random.randint(ks[2], (E,), 0, N, dtype=jnp.int32)
        etype = jax.random.randint(ks[3], (E,), 0, R, dtype=jnp.int32)
        norm = jax.random.uniform(ks[4], (E, 1), dtype=jnp.float32)
        weight = jax.random.normal(ks[5], (B, D, F), dtype=jnp.float32) * (2.0 / (D + F)) ** 0.5
        w_comp = jax.random.normal(ks[6], (R, B), dtype=jnp.float32) * (2.0 / (R + B)) ** 0.5
        loop_weight = jax.random.normal(ks[7], (D, F), dtype=jnp.float32) * (2.0 / (D + F)) ** 0.5
        h_bias = jnp.zeros((F,), dtype=jnp.float32)
        return {'h': h, 'src': src, 'dst': dst, 'etype': etype, 'norm': norm, 'weight': weight, 'w_comp': w_comp, 'loop_weight': loop_weight, 'h_bias': h_bias}
    _L2_gnn_all = _L2_gnn_setup()
    _L2_gnn_in = {k: v for k, v in _L2_gnn_all.items() if k in ('weight', 'w_comp', 'loop_weight', 'h_bias')}
    del _L2_gnn_all

    def _L3_gnn_setup():
        import jax, jax.numpy as jnp
        import numpy as np
        N_NODES = 6250
        N_EDGES = 75000
        D_IN = 128
        D_OUT = 128
        BN_EPS = 1e-05

        def _gcn_forward(x, edge_index, edge_weight, W, b, gamma, beta):
            n = x.shape[0]
            loop = jnp.arange(n, dtype=edge_index.dtype)
            src = jnp.concatenate([edge_index[0], loop])
            dst = jnp.concatenate([edge_index[1], loop])
            w = jnp.concatenate([edge_weight, jnp.ones((n,), dtype=x.dtype)])
            deg = jax.ops.segment_sum(w, dst, num_segments=n)
            dinv = jnp.where(deg > 0, jax.lax.rsqrt(deg), 0.0)
            norm = w * dinv[src] * dinv[dst]
            xw = x @ W
            msgs = xw[src] * norm[:, None]
            out = jax.ops.segment_sum(msgs, dst, num_segments=n) + b
            mean = jnp.mean(out, axis=0)
            var = jnp.mean(jnp.square(out - mean), axis=0)
            out = (out - mean) * jax.lax.rsqrt(var + BN_EPS) * gamma + beta
            return jax.nn.relu(out)
        key = jax.random.key(seed)
        ks = jax.random.split(key, 7)
        x = jax.random.normal(ks[0], (N_NODES, D_IN), dtype=jnp.float32)
        edge_index = jax.random.randint(ks[1], (2, N_EDGES), 0, N_NODES, dtype=jnp.int64)
        edge_weight = jax.random.uniform(ks[2], (N_EDGES,), dtype=jnp.float32)
        W = jax.random.normal(ks[3], (D_IN, D_OUT), dtype=jnp.float32) / np.sqrt(D_IN)
        b = jnp.zeros((D_OUT,), dtype=jnp.float32)
        gamma = jnp.ones((D_OUT,), dtype=jnp.float32)
        beta = jnp.zeros((D_OUT,), dtype=jnp.float32)
        return {'x': x, 'edge_index': edge_index, 'edge_weight': edge_weight, 'W': W, 'b': b, 'gamma': gamma, 'beta': beta}
    _L3_gnn_all = _L3_gnn_setup()
    _L3_gnn_in = {k: v for k, v in _L3_gnn_all.items() if k in ('W', 'b', 'gamma', 'beta')}
    del _L3_gnn_all
    return {'x': x, 'src': src, 'dst': dst, 'edge_type_32': edge_type_32, 'edge_weight': edge_weight, 'edge_weight1': edge_weight1, 'L0_gnn_W_msg_1': _L0_gnn_in['W_msg_1'], 'L0_gnn_b_msg_1': _L0_gnn_in['b_msg_1'], 'L0_gnn_W_msg_2': _L0_gnn_in['W_msg_2'], 'L0_gnn_b_msg_2': _L0_gnn_in['b_msg_2'], 'L0_gnn_W_msg_3': _L0_gnn_in['W_msg_3'], 'L0_gnn_b_msg_3': _L0_gnn_in['b_msg_3'], 'L0_gnn_W_att_1': _L0_gnn_in['W_att_1'], 'L0_gnn_b_att_1': _L0_gnn_in['b_att_1'], 'L0_gnn_W_att_2': _L0_gnn_in['W_att_2'], 'L0_gnn_b_att_2': _L0_gnn_in['b_att_2'], 'L0_gnn_W_att_3': _L0_gnn_in['W_att_3'], 'L0_gnn_b_att_3': _L0_gnn_in['b_att_3'], 'L0_gnn_W_c1': _L0_gnn_in['W_c1'], 'L0_gnn_b_c1': _L0_gnn_in['b_c1'], 'L0_gnn_W_c2': _L0_gnn_in['W_c2'], 'L0_gnn_b_c2': _L0_gnn_in['b_c2'], 'L1_gnn_W_proj': _L1_gnn_in['W_proj'], 'L1_gnn_w_edge': _L1_gnn_in['w_edge'], 'L1_gnn_ln_gamma': _L1_gnn_in['ln_gamma'], 'L1_gnn_ln_beta': _L1_gnn_in['ln_beta'], 'L2_gnn_weight': _L2_gnn_in['weight'], 'L2_gnn_w_comp': _L2_gnn_in['w_comp'], 'L2_gnn_loop_weight': _L2_gnn_in['loop_weight'], 'L2_gnn_h_bias': _L2_gnn_in['h_bias'], 'L3_gnn_W': _L3_gnn_in['W'], 'L3_gnn_b': _L3_gnn_in['b'], 'L3_gnn_gamma': _L3_gnn_in['gamma'], 'L3_gnn_beta': _L3_gnn_in['beta']}

def reference(x, src, dst, edge_type_32, edge_weight, edge_weight1, L0_gnn_W_msg_1, L0_gnn_b_msg_1, L0_gnn_W_msg_2, L0_gnn_b_msg_2, L0_gnn_W_msg_3, L0_gnn_b_msg_3, L0_gnn_W_att_1, L0_gnn_b_att_1, L0_gnn_W_att_2, L0_gnn_b_att_2, L0_gnn_W_att_3, L0_gnn_b_att_3, L0_gnn_W_c1, L0_gnn_b_c1, L0_gnn_W_c2, L0_gnn_b_c2, L1_gnn_W_proj, L1_gnn_w_edge, L1_gnn_ln_gamma, L1_gnn_ln_beta, L2_gnn_weight, L2_gnn_w_comp, L2_gnn_loop_weight, L2_gnn_h_bias, L3_gnn_W, L3_gnn_b, L3_gnn_gamma, L3_gnn_beta):
    import jax
    import jax.numpy as jnp

    def _L0_gnn_ref(node_features, src, dst, W_msg_1, b_msg_1, W_msg_2, b_msg_2, W_msg_3, b_msg_3, W_att_1, b_att_1, W_att_2, b_att_2, W_att_3, b_att_3, W_c1, b_c1, W_c2, b_c2):
        import jax, jax.numpy as jnp
        import numpy as np
        N_NODES, N_EDGES = (6250, 100000)
        NODE_D, MSG_D, OUT_D = (128, 128, 128)

        def _linear_params(key, d_in, d_out):
            kw, _ = jax.random.split(key)
            W = jax.random.normal(kw, (d_in, d_out), jnp.float32) * np.float32(1.0 / np.sqrt(d_in))
            b = jnp.zeros((d_out,), jnp.float32)
            return (W, b)
        h = node_features
        N = h.shape[0]
        hs = h[src]
        hd = h[dst]
        e = jnp.concatenate([hs, hd], axis=1)
        a1 = jnp.exp(jax.nn.relu(e @ W_att_1 + b_att_1))
        a2 = jnp.exp(jax.nn.relu(e @ W_att_2 + b_att_2))
        a3 = jnp.exp(jax.nn.relu(e @ W_att_3 + b_att_3))
        att1 = jax.ops.segment_sum(a1, dst, num_segments=N)
        att2 = jax.ops.segment_sum(a2, dst, num_segments=N)
        att3 = jax.ops.segment_sum(a3, dst, num_segments=N)
        avg_a = (a1 / att1[dst] + a2 / att2[dst] + a3 / att3[dst]) / 3.0
        m = avg_a * jax.nn.relu(jax.nn.relu(jax.nn.relu(hs @ W_msg_1 + b_msg_1) @ W_msg_2 + b_msg_2) @ W_msg_3 + b_msg_3)
        deg = jax.ops.segment_sum(jnp.ones((src.shape[0], 1), h.dtype), dst, num_segments=N)
        h_neigh = jax.ops.segment_sum(m, dst, num_segments=N) / jnp.maximum(deg, 1.0)
        hc = jnp.concatenate([h, h_neigh], axis=1)
        out = jax.nn.relu(hc @ W_c1 + b_c1) @ W_c2 + b_c2
        return out

    def _L1_gnn_ref(node_states, edge_index, W_proj, w_edge, ln_gamma, ln_beta):
        import jax, jax.numpy as jnp
        import numpy as np
        N_NODES = 6250
        N_EDGES = 100000
        HIDDEN = 128
        LN_EPS = 1e-05

        def _layernorm(x, gamma, beta):
            mu = jnp.mean(x, axis=-1, keepdims=True)
            var = jnp.mean(jnp.square(x - mu), axis=-1, keepdims=True)
            return (x - mu) * jax.lax.rsqrt(var + LN_EPS) * gamma + beta
        src, dst = (edge_index[0], edge_index[1])
        n = node_states.shape[0]
        d = node_states.shape[1]
        h = node_states @ W_proj.T
        a_src = h @ w_edge[:d]
        a_dst = h @ w_edge[d:]
        scores = jax.nn.leaky_relu(a_src[src] + a_dst[dst], negative_slope=0.2)
        scores = scores - jnp.max(scores)
        attn = jnp.exp(scores)
        denom = jax.ops.segment_sum(attn, dst, num_segments=n) + 1e-06
        weights = attn / denom[dst]
        messages = h[src] * weights[:, None]
        agg = jax.ops.segment_sum(messages, dst, num_segments=n)
        out = _layernorm(agg + node_states, ln_gamma, ln_beta)
        return jax.nn.gelu(out, approximate=False)

    def _L2_gnn_ref(h, src, dst, etype, norm, weight, w_comp, loop_weight, h_bias):
        import jax, jax.numpy as jnp
        import numpy as np
        N, E, D, F, R, B = (6250, 200000, 128, 128, 32, 8)
        n_nodes, d_in = h.shape
        n_rels = w_comp.shape[0]
        W_rel = jnp.einsum('rb,bdf->rdf', w_comp, weight)
        seg = etype * n_nodes + dst
        agg = jax.ops.segment_sum(h[src] * norm, seg, num_segments=n_rels * n_nodes)
        agg = agg.reshape(n_rels, n_nodes, d_in)
        node_repr = jnp.einsum('rnd,rdf->nf', agg, W_rel)
        node_repr = node_repr + h_bias + h @ loop_weight
        return jax.nn.relu(node_repr)

    def _L3_gnn_ref(x, edge_index, edge_weight, W, b, gamma, beta):
        import jax, jax.numpy as jnp
        import numpy as np
        N_NODES = 6250
        N_EDGES = 75000
        D_IN = 128
        D_OUT = 128
        BN_EPS = 1e-05

        def _gcn_forward(x, edge_index, edge_weight, W, b, gamma, beta):
            n = x.shape[0]
            loop = jnp.arange(n, dtype=edge_index.dtype)
            src = jnp.concatenate([edge_index[0], loop])
            dst = jnp.concatenate([edge_index[1], loop])
            w = jnp.concatenate([edge_weight, jnp.ones((n,), dtype=x.dtype)])
            deg = jax.ops.segment_sum(w, dst, num_segments=n)
            dinv = jnp.where(deg > 0, jax.lax.rsqrt(deg), 0.0)
            norm = w * dinv[src] * dinv[dst]
            xw = x @ W
            msgs = xw[src] * norm[:, None]
            out = jax.ops.segment_sum(msgs, dst, num_segments=n) + b
            mean = jnp.mean(out, axis=0)
            var = jnp.mean(jnp.square(out - mean), axis=0)
            out = (out - mean) * jax.lax.rsqrt(var + BN_EPS) * gamma + beta
            return jax.nn.relu(out)
        return _gcn_forward(x, edge_index, edge_weight, W, b, gamma, beta)
    edge_index = jnp.stack([src, dst])
    x = _layernorm(x + _L0_gnn_ref(x, src, dst, L0_gnn_W_msg_1, L0_gnn_b_msg_1, L0_gnn_W_msg_2, L0_gnn_b_msg_2, L0_gnn_W_msg_3, L0_gnn_b_msg_3, L0_gnn_W_att_1, L0_gnn_b_att_1, L0_gnn_W_att_2, L0_gnn_b_att_2, L0_gnn_W_att_3, L0_gnn_b_att_3, L0_gnn_W_c1, L0_gnn_b_c1, L0_gnn_W_c2, L0_gnn_b_c2), axis=-1)
    x = _layernorm(x + _L1_gnn_ref(x, edge_index, L1_gnn_W_proj, L1_gnn_w_edge, L1_gnn_ln_gamma, L1_gnn_ln_beta), axis=-1)
    x = _layernorm(x + _L2_gnn_ref(x, src, dst, edge_type_32, edge_weight1, L2_gnn_weight, L2_gnn_w_comp, L2_gnn_loop_weight, L2_gnn_h_bias), axis=-1)
    x = _layernorm(x + _L3_gnn_ref(x, edge_index, edge_weight, L3_gnn_W, L3_gnn_b, L3_gnn_gamma, L3_gnn_beta), axis=-1)
    return x

_drawn_inputs = setup_inputs


def setup_inputs(seed=0):
    import zlib

    import numpy as np

    out = dict(_drawn_inputs(seed))
    spreads = {'L0_gnn_b_msg_1': (0.0, 0.8),
     'L0_gnn_b_msg_2': (0.0, 2.0),
     'L0_gnn_b_msg_3': (0.0, 2.0),
     'L0_gnn_b_c1': (0.0, 0.1),
     'L0_gnn_b_c2': (0.0, 0.1),
     'L1_gnn_ln_gamma': (1.0, 0.2),
     'L1_gnn_ln_beta': (0.0, 0.1),
     'L2_gnn_h_bias': (0.0, 0.1),
     'L3_gnn_b': (0.0, 2.0),
     'L3_gnn_gamma': (1.0, 0.2),
     'L3_gnn_beta': (0.0, 0.1)}
    factors = {'L0_gnn_W_msg_1': 8.0,
     'L0_gnn_W_msg_2': 8.0,
     'L0_gnn_W_msg_3': 8.0,
     'L0_gnn_W_att_1': 8.0,
     'L0_gnn_W_att_2': 8.0,
     'L0_gnn_W_att_3': 8.0,
     'L1_gnn_w_edge': 8.0}
    for name, (base, spread) in spreads.items():
        noise = np.random.default_rng([zlib.crc32(name.encode()), seed]).standard_normal(out[name].shape)
        drawn = base * np.exp(spread * noise) if base else spread * noise
        out[name] = jnp.asarray(drawn.astype(out[name].dtype))
    for name, factor in factors.items():
        out[name] = (out[name] * factor).astype(out[name].dtype)
    return out
```

```python
from contextlib import ExitStack

import numpy as np

import concourse.bass as bass
from concourse import mybir

F32 = mybir.dt.float32
BF16 = mybir.dt.bfloat16
I32 = mybir.dt.int32
U16 = mybir.dt.uint16
U8 = mybir.dt.uint8
ALU = mybir.AluOpType
ACT = mybir.ActivationFunctionType
AX = mybir.AxisListType

P = 128
N = 6250
E = 206250
D = 128
WIN = 32
NODE_TILES = -(-N // P)
NPAD = NODE_TILES * P
WINDOWS = NPAD // WIN
GRP = 4
RING = 4 * GRP
TILES = -(-((E + (P - 1) * WINDOWS) // P) // RING) * RING
GROUPS = TILES // GRP
CHUNKS = -(-TILES // P)
TCOLS = CHUNKS * P
ROW = 1650
ROWS = E // ROW
EPAD = (ROWS + 1) * ROW
PAD_DST = 8192
FAR = 64.0
RELS, BASES = 32, 8
TROW = 132


def bcast_mid(ap, n):
    return ap.unsqueeze(1).to_broadcast([ap.shape[0], n, ap.shape[1]])


def bcast_last(ap, n):
    return ap.unsqueeze(2).to_broadcast([ap.shape[0], ap.shape[1], n])


def build_identity(nc, pool, ident, zeroed, ready):
    pool.memset(ident[:], 0.0).then_inc(zeroed, 1)
    pool.wait_ge(zeroed, 1)
    pool.affine_select(out=ident[:], in_=ident[:], compare_op=ALU.not_equal, fill=1.0, base=0,
                       pattern=[[-1, P]], channel_multiplier=1).then_inc(ready, 1)


def build_edge_tiles(nc, sh, fields_in, fields, types_tiled, weights_dram, norms_dram, win_dram,
                     src_all, rel_all, win_all):
    with ExitStack() as ctx:
        def sb(name, shape, dt=F32):
            return ctx.enter_context(nc.sbuf_tensor(name, shape, dt))

        def sem(name):
            return ctx.enter_context(nc.semaphore(name))

        pad_i = sb("pad_i", [1, ROW], I32)
        pad_z = sb("pad_z", [1, ROW], I32)
        ident = sb("ident_e", [P, P])
        last_i = sb("last_i", [ROWS, 1], I32)
        last_f = sb("last_f", [ROWS, 1])
        thr_row = sb("thr_row", [ROWS, 2 * P + 1])
        below = sb("below", [ROWS, 2 * P + 1])
        ones_col = sb("ones_col", [P, 1])
        ones_sq = sb("ones_sq", [P, P])
        tri = sb("tri", [P, P])
        thr_col = sb("thr_col", [P, 4])
        row_i = sb("row_i", [P, 4], I32)
        row_f = sb("row_f", [P, 4])
        edge_rows = sb("edge_rows", [P, 4, ROW], I32)
        less = sb("less", [P, ROW])
        partial = sb("partial", [P, 4])
        bound = sb("bound", [P, 4])
        count_i = sb("count_i", [P, 2], I32)
        ntile_i = sb("ntile_i", [P, 2], I32)
        ntile = sb("ntile", [P, 2])
        first = sb("first", [P, 2])
        end = sb("end", [P, 2])
        tile_row = sb("tile_row", [P, TCOLS])
        member = sb("member", [P, 2, TCOLS])
        per_win = sb("per_win", [P, 2, 3])
        tile_col = sb("tile_col", [P, CHUNKS])
        got = sb("got", [P, CHUNKS, 3])
        used_off = sb("used_off", [P, CHUNKS])
        off_f = sb("off_f", [P, CHUNKS])
        off_i = sb("off_i", [P, CHUNKS], I32)
        win32 = sb("win32", [P, CHUNKS])
        win_t = sb("win_t", [CHUNKS, P], U8)
        off_c = sb("off_c", [P, 1], I32)
        raw_i = sb("raw_i", [P, 3, P], I32)
        raw_f = sb("raw_f", [P, 2, P])
        src_f = sb("src_f", [P, P])
        rel_f = sb("rel_f", [P, P])
        type_f = sb("type_f", [P, P])
        w_all = sb("w_all", [P, TCOLS])
        n_all = sb("n_all", [P, TCOLS])
        ps_rows = ctx.enter_context(nc.psum_tensor("ps_rows", [P, 4], F32))
        ps_first = ctx.enter_context(nc.psum_tensor("ps_first", [P, 2], F32))
        ps_got = ctx.enter_context(nc.psum_tensor("ps_got", [P, CHUNKS * 3], F32))
        ps_win = ctx.enter_context(nc.psum_tensor("ps_win", [CHUNKS, P], F32))
        ps_t = ctx.enter_context(nc.psum_tensor("ps_t", [P, 4 * P], F32))

        pads_set, padded, last_in = sem("pads_set"), sem("padded"), sem("last_in")
        const, zeroed, ident_ok = sem("const"), sem("zeroed_e"), sem("ident_e_ok")
        dve_step, rows_mm, rows_in = sem("dve_step"), sem("rows_mm"), sh.rows_in
        below_ok, row_ok, ntile_ok, first_mm = sem("below_ok"), sem("row_ok"), sem("ntile_ok"), sem("first_mm")
        member_ok, got_mm, winf_ok = sem("member_ok"), sem("got_mm"), sem("winf_ok")
        win_tr, win_u8, win_out, win_in = sem("win_tr"), sem("win_u8"), sem("win_out"), sem("win_in")
        off_ok, off_go, fetched = sem("off_ok"), sem("off_go"), sh.fetched
        conv_ok, turned, laid = sem("conv_ok"), sem("turned"), sem("laid")
        types_out, laid_out = sem("types_out"), sem("laid_out")
        block = ctx.enter_context(nc.Block())

        @block.sync
        def _(sp):
            for k, (src, dst) in enumerate(zip(fields_in, fields)):
                sp.dma_start(dst[0:E].rearrange("(a b) -> a b", a=330),
                             src.rearrange("(a b) -> a b", a=330)).then_inc(padded, 16)
            sp.wait_ge(pads_set, 2)
            for k, dst in enumerate(fields):
                fill = pad_i if k == 1 else pad_z
                fill = fill[:] if dst.dtype == I32 else fill[:].bitcast(F32)
                sp.dma_start(dst[E:EPAD].rearrange("(a b) -> a b", a=1), fill).then_inc(padded, 16)
            sp.dma_start(last_i[:], fields_in[1].rearrange("(a b) -> a b", b=ROW)[:, ROW - 1:ROW],
                         allow_slow_non_contiguous=True).then_inc(last_in, 16)
            sp.wait_ge(win_u8, 1)
            sp.dma_start(win_dram.rearrange("(a b) -> a b", b=P), win_t[:]).then_inc(win_out, 16)
            sp.wait_ge(win_out, 16)
            sp.dma_start(win_all[:], win_dram.rearrange("(a b) -> a b", a=1)).then_inc(win_in, 16)
            with sp.Fori(0, CHUNKS) as c:
                sp.wait_ge(conv_ok, c + 1)
                sp.dma_start(types_tiled[bass.ds(c * P, P), :], type_f[:]).then_inc(types_out, 16)
            sp.wait_ge(laid, CHUNKS)
            sp.dma_start(weights_dram, w_all[:]).then_inc(laid_out, 16)
            sp.dma_start(norms_dram, n_all[:]).then_inc(laid_out, 16)
            sp.wait_ge(laid_out, 32)
            sp.wait_ge(types_out, 16 * CHUNKS)
            sp.wait_ge(win_in, 16)

        @block.gpsimd
        def _(pool):
            build_identity(nc, pool, ident, zeroed, ident_ok)
            pool.memset(pad_i[:], PAD_DST).then_inc(pads_set, 1)
            pool.memset(pad_z[:], 0).then_inc(pads_set, 1)
            pool.memset(ones_col[:], 1.0)
            pool.memset(ones_sq[:], 1.0).then_inc(zeroed, 1)
            pool.iota(thr_row[:], pattern=[[WIN, 2 * P + 1]], base=0, channel_multiplier=0,
                      allow_small_or_imprecise_dtypes=True)
            for c in range(2):
                for s in range(2):
                    pool.iota(thr_col[:, 2 * c + s:2 * c + s + 1], pattern=[[1, 1]],
                              base=WIN * (P * c + s), channel_multiplier=WIN,
                              allow_small_or_imprecise_dtypes=True)
            pool.iota(tile_row[:], pattern=[[1, TCOLS]], base=0, channel_multiplier=0,
                      allow_small_or_imprecise_dtypes=True)
            pool.iota(tile_col[:], pattern=[[P, CHUNKS]], base=0, channel_multiplier=1,
                      allow_small_or_imprecise_dtypes=True)
            for c in range(2):
                pool.iota(per_win[:, c, 1:2], pattern=[[1, 1]], base=P * c, channel_multiplier=1,
                          allow_small_or_imprecise_dtypes=True)
                pool.memset(per_win[:, c, 2:3], 1.0)
            pool.wait_ge(zeroed, 2)
            pool.affine_select(out=tri[:], in_=ones_sq[:], compare_op=ALU.is_gt, fill=0.0, base=0,
                               pattern=[[1, P]], channel_multiplier=-1).then_inc(const, 1)
            pool.wait_ge(padded, 160)
            pool.wait_ge(row_ok, 1)
            for k in range(4):
                pool.indirect_dma_start(
                    out=edge_rows[:, k, :], out_offset=None,
                    in_=fields[1].rearrange("(a b) -> a b", b=ROW),
                    in_offset=bass.IndirectOffsetOnAxis(ap=row_i[:, k:k + 1], axis=0),
                ).then_inc(rows_in, 16)
            pool.wait_ge(rows_in, 64)
            with pool.Fori(0, CHUNKS) as c:
                pool.wait_ge(off_ok, c + 1)
                pool.sem_inc(off_go, 1)
                for k, field in enumerate(fields):
                    to = raw_i[:, k, :] if k < 3 else raw_f[:, k - 3, :]
                    pool.indirect_dma_start(
                        out=to, out_offset=None, in_=field.rearrange("(a b) -> a b", b=1),
                        in_offset=bass.IndirectOffsetOnAxis(ap=off_c[:, 0:1], axis=0),
                    ).then_inc(fetched[k], 16)

        @block.tensor
        def _(pe):
            pe.wait_ge(ident_ok, 1)
            pe.wait_ge(const, 1)
            pe.wait_ge(below_ok, 1)
            for c in range(2):
                for s in range(2):
                    mm = pe.matmul(ps_rows[:, 2 * c + s:2 * c + s + 1],
                                   below[:, P * c + s:P * c + s + P], ones_col[0:ROWS, :],
                                   start=True, stop=True)
            mm.then_inc(rows_mm, 1)
            pe.wait_ge(ntile_ok, 1)
            pe.matmul(ps_first[:, 0:1], tri[:], ntile[:, 0:1], start=True, stop=True)
            pe.matmul(ps_first[:, 1:2], tri[:], ntile[:, 1:2], start=True, stop=False)
            pe.matmul(ps_first[:, 1:2], ones_sq[:], ntile[:, 0:1], start=False,
                      stop=True).then_inc(first_mm, 1)
            pe.wait_ge(member_ok, 1)
            for k in range(CHUNKS):
                for c in range(2):
                    mm = pe.matmul(ps_got[:, 3 * k:3 * k + 3], member[:, c, P * k:P * k + P],
                                   per_win[:, c, :], start=c == 0, stop=c == 1)
            mm.then_inc(got_mm, 1)
            pe.wait_ge(winf_ok, 1)
            pe.transpose(ps_win[:], used_off[:], ident[:]).then_inc(win_tr, 1)
            with pe.Fori(0, CHUNKS) as c:
                pe.wait_ge(fetched[3], 16 * c + 16)
                pe.wait_ge(fetched[4], 16 * c + 16)
                pe.wait_ge(conv_ok, c + 1)
                pe.wait_ge(laid, c)
                pe.transpose(ps_t[:, 0:P], src_f[:], ident[:])
                pe.transpose(ps_t[:, P:2 * P], rel_f[:], ident[:])
                pe.transpose(ps_t[:, 2 * P:3 * P], raw_f[:, 0, :], ident[:])
                pe.transpose(ps_t[:, 3 * P:4 * P], raw_f[:, 1, :], ident[:]).then_inc(turned, 1)

        @block.vector
        def _(v):
            step = [0]

            def then(ins):
                step[0] += 1
                ins.then_inc(dve_step, 1)
                v.wait_ge(dve_step, step[0])

            v.wait_ge(last_in, 16)
            v.wait_ge(const, 1)
            then(v.tensor_copy(last_f[:], last_i[:]))
            v.tensor_scalar(below[:], thr_row[:], last_f[:, 0:1], None,
                            op0=ALU.is_gt).then_inc(below_ok, 1)
            v.wait_ge(rows_mm, 1)
            v.tensor_copy(row_i[:], ps_rows[:]).then_inc(row_ok, 1)
            then(v.tensor_copy(row_f[:], ps_rows[:]))
            v.wait_ge(rows_in, 64)
            for k in range(4):
                then(v.tensor_scalar(less[:], edge_rows[:, k, :], thr_col[:, k:k + 1], 0.0,
                                     op0=ALU.is_lt, op1=ALU.add, accum_out=partial[:, k:k + 1]))
            then(v.scalar_tensor_tensor(out=bound[:], in0=row_f[:], scalar=float(ROW),
                                        in1=partial[:], op0=ALU.mult, op1=ALU.add))
            b = bound[:].rearrange("p (c s) -> p c s", s=2)
            then(v.scalar_tensor_tensor(out=count_i[:], in0=b[:, :, 1], scalar=float(P - 1),
                                        in1=b[:, :, 0], op0=ALU.add, op1=ALU.subtract))
            then(v.tensor_scalar(ntile_i[:], count_i[:], 7, None, op0=ALU.arith_shift_right))
            then(v.tensor_copy(ntile[:], ntile_i[:]))
            v.sem_inc(ntile_ok, 1)
            v.wait_ge(first_mm, 1)
            then(v.tensor_copy(first[:], ps_first[:]))
            then(v.tensor_tensor(end[:], first[:], ntile[:], ALU.add))
            v.scalar_tensor_tensor(out=per_win[:, :, 0], in0=first[:], scalar=-float(P),
                                   in1=b[:, :, 0], op0=ALU.mult, op1=ALU.add)
            for c in range(2):
                then(v.tensor_scalar(member[:, c, :], tile_row[:], first[:, c:c + 1], None,
                                     op0=ALU.is_ge))
                then(v.scalar_tensor_tensor(out=member[:, c, :], in0=tile_row[:],
                                            scalar=end[:, c:c + 1], in1=member[:, c, :],
                                            op0=ALU.is_lt, op1=ALU.mult))
            v.sem_inc(member_ok, 1)
            v.wait_ge(got_mm, 1)
            then(v.tensor_copy(got[:].rearrange("p a b -> p (a b)"), ps_got[:]))
            then(v.tensor_scalar(used_off[:], tile_col[:], float(P), -float(E), op0=ALU.mult,
                                 op1=ALU.add))
            then(v.tensor_tensor(used_off[:], used_off[:], got[:, :, 2], ALU.mult))
            then(v.scalar_tensor_tensor(out=off_f[:], in0=used_off[:], scalar=float(E),
                                        in1=got[:, :, 0], op0=ALU.add, op1=ALU.add))
            then(v.tensor_copy(off_i[:], off_f[:]))
            then(v.tensor_scalar(win32[:], got[:, :, 1], float(WIN), None, op0=ALU.mult))
            then(v.tensor_copy(used_off[:], got[:, :, 1]))
            v.sem_inc(winf_ok, 1)
            v.wait_ge(win_tr, 1)
            v.tensor_copy(win_t[:], ps_win[:]).then_inc(win_u8, 1)
            base = step[0]
            with v.Fori(0, CHUNKS) as c:
                for k in range(5):
                    v.wait_ge(fetched[k], 16 * c)
                v.wait_ge(types_out, 16 * c)
                v.tensor_copy(off_c[:], off_i[:, bass.ds(c, 1)]).then_inc(off_ok, 1)
                for k in range(3):
                    v.wait_ge(fetched[k], 16 * c + 16)
                v.tensor_copy(src_f[:], raw_i[:, 0, :])
                v.tensor_copy(type_f[:], raw_i[:, 2, :])
                v.tensor_scalar(rel_f[:], raw_i[:, 1, :], win32[:, bass.ds(c, 1)], None,
                                op0=ALU.subtract).then_inc(dve_step, 1)
                v.wait_ge(dve_step, base + c + 1)
                v.tensor_scalar(rel_f[:], rel_f[:], FAR, None, op0=ALU.min).then_inc(conv_ok, 1)
                v.wait_ge(turned, c + 1)
                v.tensor_copy(src_all[:, bass.ds(c * P, P)], ps_t[:, 0:P])
                v.tensor_copy(rel_all[:, bass.ds(c * P, P)], ps_t[:, P:2 * P])
                v.tensor_copy(w_all[:, bass.ds(c * P, P)], ps_t[:, 2 * P:3 * P])
                v.tensor_copy(n_all[:, bass.ds(c * P, P)], ps_t[:, 3 * P:4 * P]).then_inc(laid, 1)


BT = 7
BATCHES = NODE_TILES // BT
BN = BT * P
BW = BN // WIN
HALVES = ((0, 512), (512, BN))
AROW = D + 1
LN_EPS = 1e-5
SEM_END = 256


def at_least(eng, sem, value):
    if not isinstance(value, int) or value > 0:
        eng.wait_ge(sem, value)


def row_of(vec, parts=P):
    return vec.rearrange("(a b) -> a b", a=1).to_broadcast([parts, vec.shape[0]])


class Shared:
    pass


def scope(nc, ctx):
    def sb(name, shape, dt=F32):
        return ctx.enter_context(nc.sbuf_tensor(name, shape, dt))

    def ps(name, shape, dt=F32):
        return ctx.enter_context(nc.psum_tensor(name, shape, dt))

    def sem(name):
        return ctx.enter_context(nc.semaphore(name))

    return sb, ps, sem


def zero_semaphores(nc, sh):
    with nc.Block() as block:
        @block.gpsimd
        def _(pool):
            pool.sem_clear(range(sh.first_sem, SEM_END))


def build_constants(nc, sh, x, xpad):
    with ExitStack() as ctx:
        sb, ps, sem = scope(nc, ctx)
        zero_rows = sb("zero_rows", [NPAD - N, D])
        zeroed, ident_ok, iota_ok = sem("zeroed"), sem("ident_ok"), sem("iota_ok")
        placed, copied = sem("placed"), sem("copied")
        block = ctx.enter_context(nc.Block())

        @block.gpsimd
        def _(pool):
            build_identity(nc, pool, sh.ident, zeroed, ident_ok)
            pool.iota(sh.iota[:], pattern=[[1, WIN]], base=0, channel_multiplier=0,
                      allow_small_or_imprecise_dtypes=True)
            pool.memset(sh.ones[:], 1.0)
            pool.memset(sh.eps[:], LN_EPS)
            pool.memset(zero_rows[:], 0.0).then_inc(zeroed, 1)

        @block.vector
        def _(v):
            v.memset(sh.place[:], 0.0).then_inc(placed, 1)
            v.wait_ge(placed, 1)
            v.wait_ge(ident_ok, 1)
            for k in range(4):
                for q in range(4):
                    rows = slice(WIN * k, WIN * k + WIN)
                    v.tensor_copy(sh.place[rows, q, WIN * q:WIN * q + WIN], sh.ident[rows, rows])

        @block.sync
        def _(sp):
            sp.dma_start(xpad[0:N, :], x).then_inc(copied, 16)
            sp.wait_ge(zeroed, 2)
            sp.dma_start(xpad[N:NPAD, :], zero_rows[:]).then_inc(copied, 16)
            sp.wait_ge(copied, 32)


def batch_rows(dram, i):
    return dram[bass.ds(i * BN, BN), :].rearrange("(j p) f -> p j f", p=P)


def attention_tables(nc, sh, w):
    with ExitStack() as ctx:
        sb, ps, sem = scope(nc, ctx)
        at = [0]

        def carve(width, parts=P):
            view = sh.acc[0:parts, at[0]:at[0] + width]
            at[0] += width
            return view

        x_rows = carve(BN).rearrange("p (j f) -> p j f", f=D)
        xT, m1, m2 = carve(BN), carve(BN), carve(BN)
        biased = carve(BN).rearrange("p (j f) -> p j f", f=D)
        table = carve(BT * TROW).rearrange("p (j f) -> p j f", f=TROW)
        wm = carve(3 * D).rearrange("p (k f) -> p k f", f=D)
        b_col = carve(2)
        b3_row = carve(D)
        w_att = carve(6).rearrange("p (s k) -> p s k", s=2)
        b_att = carve(3)
        w_dst = carve(3 * P).rearrange("p (k f) -> p k f", f=P)
        psA, psB, psC, psD = (ps(f"ps{c}", [P, 1024]) for c in "ABCD")
        params, dst_rep, ones_in, x_in = sem("params"), sem("dst_rep"), sem("ones_in"), sem("x_in")
        x_T, x_Tsb, h1, h1sb, h2, h2sb = (sem(n) for n in ("x_T", "x_Tsb", "h1", "h1sb", "h2", "h2sb"))
        h3, dst, dst_sb, biased_ok, feat_ok, src_ok, stored = (
            sem(n) for n in ("h3", "dst", "dst_sb", "biased_ok", "feat_ok", "src_ok", "stored"))
        block = ctx.enter_context(nc.Block())

        @block.sync
        def _(sp):
            for k in range(3):
                sp.dma_start(wm[:, k, :], w[f"L0_gnn_W_msg_{k + 1}"]).then_inc(params, 16)
                for s in range(2):
                    sp.dma_start(w_att[:, s, k:k + 1],
                                 w[f"L0_gnn_W_att_{k + 1}"][s * D:(s + 1) * D, :]).then_inc(params, 16)
                sp.dma_start(b_att[:, k:k + 1], row_of(w[f"L0_gnn_b_att_{k + 1}"])).then_inc(params, 16)
            for k in range(2):
                sp.dma_start(b_col[:, k:k + 1], w[f"L0_gnn_b_msg_{k + 1}"].rearrange("(a b) -> a b", b=1)
                             ).then_inc(params, 16)
            sp.dma_start(b3_row, row_of(w["L0_gnn_b_msg_3"])).then_inc(params, 16)
            with sp.Fori(0, BATCHES) as i:
                sp.wait_ge(x_T, i)
                sp.dma_start(x_rows, batch_rows(sh.xpad, i)).then_inc(x_in, 16)
                sp.wait_ge(feat_ok, i + 1)
                sp.wait_ge(src_ok, i + 1)
                sp.dma_start(batch_rows(sh.table, i), table).then_inc(stored, 16)
            sp.wait_ge(stored, 16 * BATCHES)

        @block.tensor
        def _(pe):
            pe.wait_ge(params, 15 * 16)
            pe.wait_ge(dst_rep, 1)
            with pe.Fori(0, BATCHES) as i:
                pe.wait_ge(x_in, 16 * i + 16)
                pe.wait_ge(dst_sb, 3 * i)
                for j in range(BT):
                    mm = pe.transpose(psA[:, P * j:P * j + P], x_rows[:, j, :], sh.ident[:])
                mm.then_inc(x_T, 1)
                for src_ok_, lhs, rhs, out, done in ((x_Tsb, wm[:, 0, :], xT, psB, h1),
                                                     (h1sb, wm[:, 1, :], m1, psC, h2)):
                    pe.wait_ge(src_ok_, i + 1)
                    for a, b in HALVES:
                        mm = pe.matmul(out[:, a:b], lhs, rhs[:, a:b], start=True, stop=True)
                    mm.then_inc(done, 1)
                for k, (out, free) in enumerate(((psA, x_Tsb), (psB, h1sb), (psC, h2sb))):
                    pe.wait_ge(free, i + 1)
                    for a, b in HALVES:
                        mm = pe.matmul(out[:, a:b], w_dst[:, k, :], xT[:, a:b], start=True, stop=True)
                    mm.then_inc(dst, 1)
                pe.wait_ge(biased_ok, i)
                pe.wait_ge(src_ok, i)
                for j in range(BT):
                    pe.matmul(psD[:, P * j:P * j + P], m2[:, P * j:P * j + P], wm[:, 2, :],
                              start=True, stop=True)
                for j in range(BT):
                    mm = pe.matmul(psD[:, BN + 3 * j:BN + 3 * j + 3], xT[:, P * j:P * j + P],
                                   w_att[:, 0, :], start=True, stop=True)
                mm.then_inc(h3, 1)

        @block.scalar
        def _(act):
            act.wait_ge(params, 15 * 16)
            with act.Fori(0, BATCHES) as i:
                act.wait_ge(h1, i + 1)
                act.activation(m1, psB[:, 0:BN], ACT.Relu, bias=b_col[:, 0:1]).then_inc(h1sb, 1)
                act.wait_ge(h2, i + 1)
                act.activation(m2, psC[:, 0:BN], ACT.Relu, bias=b_col[:, 1:2]).then_inc(h2sb, 1)
                for k, out in enumerate((psA, psB, psC)):
                    act.wait_ge(dst, 3 * i + k + 1)
                    to = sh.dst_terms[:, bass.ds(i * BW * 3 * WIN, BW * 3 * WIN)].rearrange(
                        "p (w k d) -> p w k d", k=3, d=WIN)[:, :, k, :]
                    act.copy(to, out[:, 0:BN].rearrange("p (w d) -> p w d", d=WIN)).then_inc(dst_sb, 1)
                act.wait_ge(biased_ok, i + 1)
                act.wait_ge(stored, 16 * i)
                act.activation(table[:, :, 0:D], biased, ACT.Relu).then_inc(feat_ok, 1)

        @block.vector
        def _(v):
            v.wait_ge(params, 15 * 16)
            v.tensor_copy(w_dst, bcast_last(w_att[:, 1, :], P)).then_inc(dst_rep, 1)
            v.memset(table[:, :, D:D + 1], 1.0)
            with v.Fori(0, BATCHES) as i:
                v.wait_ge(x_T, i + 1)
                v.wait_ge(h3, i)
                v.tensor_copy(xT, psA[:, 0:BN]).then_inc(x_Tsb, 1)
                v.wait_ge(h3, i + 1)
                v.wait_ge(feat_ok, i)
                v.tensor_tensor(biased, psD[:, 0:BN].rearrange("p (j f) -> p j f", f=D),
                                bcast_mid(b3_row, BT), ALU.add).then_inc(biased_ok, 1)
                v.wait_ge(stored, 16 * i)
                v.tensor_tensor(table[:, :, D + 1:D + 4],
                                psD[:, BN:BN + 3 * BT].rearrange("p (j k) -> p j k", k=3),
                                bcast_mid(b_att, BT), ALU.add).then_inc(src_ok, 1)


def window_slice(table, window, width, count=1):
    cols = table[:, bass.ds(window * width, width * count)]
    return cols if count == 1 else cols.rearrange("p (w c) -> p w c", c=width)


class TileWindows:

    def __init__(self, v, sh, name):
        self.v, self.sh = v, sh
        self.regs = [v.alloc_register(f"{name}_window{t}") for t in range(RING)]

    def load(self, i, q):
        first, last = {0: (0, RING - GRP), 3: (RING - GRP, RING)}.get(q, (0, 0))
        if last:
            self.v.load(self.regs[first:last],
                        self.sh.win_all[0:1, bass.ds(i * RING + first, last - first)])

    def load_all(self, i):
        self.v.load(self.regs, self.sh.win_all[0:1, bass.ds(i * RING, RING)])

    def of(self, q):
        return [self.v.snap(r, min_val=0, max_val=WINDOWS - 1)
                for r in self.regs[GRP * q:GRP * q + GRP]]


def gather_rows(pool, table, rows, index_ready, granted, sh, n, q):
    pool.wait_ge(index_ready, n + 1)
    pool.sem_inc(granted, 1)
    for u in range(GRP):
        slot = GRP * q + u
        pool.indirect_dma_start(
            out=rows[:, slot, :], out_offset=None, in_=table[:, :],
            in_offset=bass.IndirectOffsetOnAxis(ap=sh.index[:, slot:slot + 1], axis=0),
        ).then_inc(sh.gathered[slot], 16)


def wait_gathered(eng, sh, layer, i, q):
    for slot in range(GRP * q, GRP * q + GRP):
        eng.wait_ge(sh.gathered[slot], (layer * (GROUPS // 4) + 1 + i) * 16)


def stage_indices(act, sh, index_ready, summed, n, q):
    at_least(act, summed, n - 3)
    act.copy(sh.index[:, GRP * q:GRP * q + GRP],
             sh.src_all[:, bass.ds(n * GRP, GRP)]).then_inc(index_ready, 1)


def attention_edges(nc, sh):
    with ExitStack() as ctx:
        sb, ps, sem = scope(nc, ctx)
        rows = sb("rows0", [P, RING, TROW])
        S = sb("S0", [P, 2, GRP, 4, WIN])
        picked = sb("picked", [P, GRP, 3, WIN])
        dst_term = sb("dst_term", [P, GRP, 3])
        z = sb("z0", [P, 2, GRP, 3])
        zr = sb("zr0", [P, 2, GRP, 3])
        a = sb("a0", [P, 2, GRP, 3])
        out = ps("out0", [P, 2, GRP, 256])
        index_ready, granted = sem("index_ready"), sem("granted")
        link, z_ready, relu_ok, a_ready = sem("link"), sem("z_ready"), sem("relu_ok"), sem("a_ready")
        s_ready, summed, added, drained = sem("s_ready"), sem("summed"), sem("added"), sem("drained")
        block = ctx.enter_context(nc.Block())

        @block.gpsimd
        def _(pool):
            with pool.Fori(0, GROUPS // 4) as i:
                for q in range(4):
                    gather_rows(pool, sh.table, rows, index_ready, granted, sh, i * 4 + q, q)

        @block.scalar
        def _(act):
            def step(i, q):
                n = i * 4 + q
                stage_indices(act, sh, index_ready, summed, n + 2, (q + 2) % 4)
                act.wait_ge(z_ready, n + 1)
                at_least(act, a_ready, n)
                act.activation(zr[:, q % 2], z[:, q % 2], ACT.Relu).then_inc(relu_ok, 1)
                act.wait_ge(relu_ok, n + 1)
                at_least(act, s_ready, n - 1)
                act.activation(a[:, q % 2], zr[:, q % 2], ACT.Exp).then_inc(a_ready, 1)

            for q in range(2):
                stage_indices(act, sh, index_ready, summed, q, q)
            for q in range(4):
                step(0, q)
            with act.Fori(1, GROUPS // 4) as i:
                for q in range(4):
                    step(i, q)

        @block.tensor
        def _(pe):
            def step(i, q):
                n = i * 4 + q
                pe.wait_ge(s_ready, n + 1)
                at_least(pe, drained, n - 1)
                for u in range(GRP):
                    mm = pe.matmul(out[:, q % 2, u, 0:AROW],
                                   S[:, q % 2, u].rearrange("p k d -> p (k d)"),
                                   rows[:, GRP * q + u, 0:AROW], start=True, stop=True)
                mm.then_inc(summed, 1)

            for q in range(4):
                step(0, q)
            with pe.Fori(1, GROUPS // 4) as i:
                for q in range(4):
                    step(i, q)

        @block.vector
        def _(v):
            LINKS = 3

            windows = TileWindows(v, sh, "l0")

            def add_up(n, q):
                b = q % 2
                into = windows.of(q)
                v.wait_ge(summed, n + 1)
                for u, window in enumerate(into):
                    to = window_slice(sh.acc, window, AROW)
                    v.wait_ge(added, n * GRP + u + 1)
                    ins = v.tensor_tensor(to, to, out[:, b, u, 0:AROW], ALU.add)
                    ins.then_inc(added, 1)
                v.wait_ge(added, n * GRP + GRP + 1)
                v.sem_inc(drained, 1)

            def step(i, q, first=False):
                n = i * 4 + q
                b = q % 2
                one_hot = S[:, b, :, 3, :]
                at_least(v, summed, n - 1)
                v.tensor_tensor(one_hot, bcast_last(sh.rel_all[:, bass.ds(n * GRP, GRP)], WIN),
                                bcast_mid(sh.iota[:], GRP), ALU.is_equal).then_inc(link, 1)
                windows.load(i, q)
                picks = windows.of(q)
                v.wait_ge(link, n * LINKS + 1)
                for u, window in enumerate(picks):
                    terms = window_slice(sh.dst_terms, window, 3 * WIN)
                    ins = v.tensor_tensor(picked[:, u], terms.rearrange("p (k d) -> p k d", k=3),
                                          bcast_mid(one_hot[:, u, :], 3), ALU.mult)
                ins.then_inc(link, 1)
                v.wait_ge(link, n * LINKS + 2)
                v.tensor_reduce(dst_term[:], picked[:], axis=AX.X, op=ALU.add).then_inc(link, 1)
                v.wait_ge(link, n * LINKS + 3)
                wait_gathered(v, sh, 0, i, q)
                v.tensor_tensor(z[:, b], dst_term[:], rows[:, GRP * q:GRP * q + GRP, D + 1:D + 4],
                                ALU.add).then_inc(z_ready, 1)
                if not first:
                    add_up(n - 1, (q - 1) % 4)
                v.wait_ge(a_ready, n + 1)
                v.tensor_tensor(S[:, b, :, 0:3, :],
                                S[:, b, :, 3:4, :].to_broadcast([P, GRP, 3, WIN]),
                                a[:, b].unsqueeze(3).to_broadcast([P, GRP, 3, WIN]),
                                ALU.mult).then_inc(s_ready, 1)

            v.memset(sh.acc[:], 0.0).then_inc(added, 1)
            for q in range(4):
                step(0, q, first=q == 0)
            with v.Fori(1, GROUPS // 4) as i:
                for q in range(4):
                    step(i, q)
            add_up(GROUPS - 1, 3)


class Chain:

    def __init__(self, eng, sem, turn=0, per_turn=0, base=0):
        self.eng, self.sem, self.start, self.per_turn = eng, sem, turn * per_turn + base, per_turn
        self.count = 0

    def then(self, ins):
        self.count += 1
        ins.then_inc(self.sem, 1)
        self.eng.wait_ge(self.sem, self.start + self.count)

    def close(self):
        assert self.count == self.per_turn, self.count


NORM_LINKS = 4


class Norm:

    def __init__(self, sb, sem, name):
        self.stats = sb(f"{name}_stats", [P, BT, 6])
        self.mean_var = sb(f"{name}_mean_var", [P, BT, 2])
        self.std = sb(f"{name}_std", [P, BT])
        self.rstd = sb(f"{name}_rstd", [P, BT])
        self.go = sem(f"{name}_go")
        self.var_ok, self.std_ok = sem(f"{name}_var_ok"), sem(f"{name}_std_ok")

    def vector(self, v, chain, y, turn):
        v.sem_inc(self.go, 1)
        for j in range(BT):
            ins = v.bn_stats(self.stats[:, j, :], y[:, j, :])
        chain.then(ins)
        v.sem_inc(self.go, 1)
        for j in range(BT):
            ins = v.bn_aggr(self.mean_var[:, j, :], self.stats[:, j, :])
        chain.then(ins)
        v.sem_inc(self.var_ok, 1)
        v.wait_ge(self.std_ok, turn + 1)
        chain.then(v.reciprocal(self.rstd[:], self.std[:]))
        for j in range(BT):
            ins = v.tensor_scalar(y[:, j, :], y[:, j, :], self.mean_var[:, j, 0:1],
                                  self.rstd[:, j:j + 1], op0=ALU.subtract, op1=ALU.mult)
        chain.then(ins)

    def scalar(self, act, sh, turn):
        act.wait_ge(self.var_ok, turn + 1)
        act.activation(self.std[:], self.mean_var[:, :, 1], ACT.Sqrt,
                       bias=sh.eps[:, 0:1]).then_inc(self.std_ok, 1)


def tiles_of(buf):
    return buf.rearrange("p (j f) -> p j f", f=D)


def transpose_tiles(pe, out, rows, ident):
    for j in range(BT):
        mm = pe.transpose(out[:, P * j:P * j + P], rows[:, j, :], ident[:])
    return mm


def finish_attention(nc, sh, w):
    with ExitStack() as ctx:
        sb, ps, sem = scope(nc, ctx)
        inv = sb("inv", [P, WINDOWS])
        inv_deg = sb("inv_deg", [P, WINDOWS])
        x_rows, y = tiles_of(sb("x_rows1", [P, BN])[:]), tiles_of(sb("y1", [P, BN])[:])
        xT, hnT, c1, x1T = sb("xT1", [P, BN]), sb("hnT1", [P, BN]), sb("c1", [P, BN]), sb("x1T", [P, BN])
        normed = sb("normed", [3 * WIN, BW, D])
        table = sb("table1", [P, BT, TROW])
        w_c1, w_c2, b_c1, b_c2 = sb("w_c1", [P, 2, D]), sb("w_c2", [P, D]), sb("b_c1", [P, 1]), sb("b_c2", [P, D])
        w_proj, w_projT = sb("w_proj", [P, D]), sb("w_projT", [P, D])
        w_edge = sb("w_edge", [P, 2])
        edge_vec = sb("edge_vec", [P, 2])
        dst_rep = sb("dst_rep1", [P, P])
        norm = Norm(sb, sem, "norm1")
        psA, psB, psC, psD = (ps(f"ps1{c}", [P, 1024]) for c in "ABCD")
        params, setup, wT, wT_sb, rep_ok = sem("params"), sem("setup"), sem("wT"), sem("wT_sb"), sem("rep_ok")
        x_in, x_T, xT_sb, norm_ok, hn, hn_sb = (
            sem(n) for n in ("x_in", "x_T", "xT_sb", "norm_ok", "hn", "hn_sb"))
        c1_mm, c1_sb, c2_mm, x1_ok, x1_T, x1T_sb = (
            sem(n) for n in ("c1_mm", "c1_sb", "c2_mm", "x1_ok", "x1_T", "x1T_sb"))
        h_mm, feat_ok, terms_ok, dst_ok, stored, x1_out, link = (
            sem(n) for n in ("h_mm", "feat_ok", "terms_ok", "dst_ok", "stored", "x1_out", "link"))
        block = ctx.enter_context(nc.Block())
        PARAMS = 7 * 16

        @block.sync
        def _(sp):
            for to, of in ((w_c1[:], w["L0_gnn_W_c1"].rearrange("(s p) f -> p s f", p=P)),
                           (w_c2[:], w["L0_gnn_W_c2"]),
                           (b_c1[:], w["L0_gnn_b_c1"].rearrange("(a b) -> a b", b=1)),
                           (b_c2[:], row_of(w["L0_gnn_b_c2"])),
                           (w_proj[:], w["L1_gnn_W_proj"]),
                           (w_edge[:, 0:1], w["L1_gnn_w_edge"][0:D].rearrange("(a b) -> a b", b=1)),
                           (w_edge[:, 1:2], w["L1_gnn_w_edge"][D:2 * D].rearrange("(a b) -> a b", b=1))):
                sp.dma_start(to, of).then_inc(params, 16)
            with sp.Fori(0, BATCHES) as i:
                sp.wait_ge(x1_ok, i)
                sp.dma_start(x_rows, batch_rows(sh.xpad, i)).then_inc(x_in, 16)
                sp.wait_ge(x1_ok, i + 1)
                sp.dma_start(batch_rows(sh.x1, i), y).then_inc(x1_out, 16)
                sp.wait_ge(feat_ok, i + 1)
                sp.wait_ge(terms_ok, i + 1)
                sp.dma_start(batch_rows(sh.table1, i), table[:]).then_inc(stored, 16)
            sp.wait_ge(stored, 16 * BATCHES)
            sp.wait_ge(x1_out, 16 * BATCHES)

        @block.tensor
        def _(pe):
            pe.wait_ge(params, PARAMS)
            pe.transpose(psA[:, 0:P], w_proj[:], sh.ident[:])
            for s in range(2):
                mm = pe.matmul(psA[:, P + s:P + s + 1], w_proj[:], w_edge[:, s:s + 1], start=True, stop=True)
            mm.then_inc(wT, 1)
            pe.wait_ge(rep_ok, 1)
            with pe.Fori(0, BATCHES) as i:
                pe.wait_ge(x_in, 16 * i + 16)
                pe.wait_ge(x1T_sb, i)
                transpose_tiles(pe, psA, x_rows, sh.ident).then_inc(x_T, 1)
                pe.wait_ge(norm_ok, i + 1)
                pe.wait_ge(feat_ok, i)
                for win in range(BW):
                    mm = pe.matmul(psB[:, WIN * win:WIN * win + WIN], normed[:, win, :],
                                   sh.place[0:3 * WIN, 0, 0:WIN], start=True, stop=True)
                mm.then_inc(hn, 1)
                pe.wait_ge(xT_sb, i + 1)
                pe.wait_ge(hn_sb, i + 1)
                pe.wait_ge(terms_ok, i)
                pe.wait_ge(dst_ok, i)
                for a, b in HALVES:
                    pe.matmul(psC[:, a:b], w_c1[:, 0, :], xT[:, a:b], start=True, stop=False)
                    mm = pe.matmul(psC[:, a:b], w_c1[:, 1, :], hnT[:, a:b], start=False, stop=True)
                mm.then_inc(c1_mm, 1)
                pe.wait_ge(c1_sb, i + 1)
                for j in range(BT):
                    mm = pe.matmul(psD[:, P * j:P * j + P], c1[:, P * j:P * j + P], w_c2[:],
                                   start=True, stop=True)
                mm.then_inc(c2_mm, 1)
                pe.wait_ge(x1_ok, i + 1)
                transpose_tiles(pe, psA, y, sh.ident).then_inc(x1_T, 1)
                pe.wait_ge(x1T_sb, i + 1)
                for a, b in HALVES:
                    pe.matmul(psC[:, a:b], dst_rep[:], x1T[:, a:b], start=True, stop=True)
                for j in range(BT):
                    pe.matmul(psD[:, BN + j:BN + j + 1], x1T[:, P * j:P * j + P], edge_vec[:, 0:1],
                              start=True, stop=True)
                for j in range(BT):
                    mm = pe.matmul(psB[:, P * j:P * j + P], x1T[:, P * j:P * j + P], w_projT[:],
                                   start=True, stop=True)
                mm.then_inc(h_mm, 1)

        @block.scalar
        def _(act):
            act.wait_ge(params, PARAMS)
            with act.Fori(0, BATCHES) as i:
                act.wait_ge(hn, i + 1)
                act.copy(hnT[:], psB[:, 0:BN]).then_inc(hn_sb, 1)
                act.wait_ge(c1_mm, i + 1)
                act.activation(c1[:], psC[:, 0:BN], ACT.Relu, bias=b_c1[:, 0:1]).then_inc(c1_sb, 1)
                norm.scalar(act, sh, i)
                act.wait_ge(h_mm, i + 1)
                act.copy(sh.dst_terms1[:, bass.ds(i * BN, BN)], psC[:, 0:BN]).then_inc(dst_ok, 1)
                act.wait_ge(stored, 16 * i)
                act.copy(table[:, :, 0:D], tiles_of(psB[:, 0:BN])).then_inc(feat_ok, 1)

        @block.vector
        def _(v):
            acc3 = sh.acc[:].rearrange("p (w c) -> p w c", c=AROW)
            v.wait_ge(params, PARAMS)
            v.memset(table[:, :, D:TROW], 1.0)
            once = Chain(v, setup)
            once.then(v.tensor_scalar(inv[:], acc3[:, :, D], 1.0, None, op0=ALU.max))
            once.then(v.reciprocal(inv[:], inv[:]))
            for k in range(3):
                ins = v.tensor_copy(inv_deg[WIN * k:WIN * k + WIN, :], inv[3 * WIN:4 * WIN, :])
            once.then(ins)
            once.then(v.scalar_tensor_tensor(out=inv[0:3 * WIN, :], in0=inv[0:3 * WIN, :],
                                             scalar=1.0 / 3.0, in1=inv_deg[0:3 * WIN, :],
                                             op0=ALU.mult, op1=ALU.mult))
            v.wait_ge(wT, 1)
            v.tensor_copy(w_projT[:], psA[:, 0:P])
            once.then(v.tensor_copy(edge_vec[:], psA[:, P:P + 2]))
            v.tensor_copy(dst_rep[:], edge_vec[:, 1:2].to_broadcast([P, P])).then_inc(rep_ok, 1)
            with v.Fori(0, BATCHES) as i:
                chain = Chain(v, link, i, 2 + NORM_LINKS)
                v.wait_ge(hn, i)
                v.tensor_tensor(normed[:], window_slice(sh.acc, i * BW, AROW, BW)[0:3 * WIN, :, 0:D],
                                bcast_last(inv[0:3 * WIN, bass.ds(i * BW, BW)], D),
                                ALU.mult).then_inc(norm_ok, 1)
                v.wait_ge(x_T, i + 1)
                v.wait_ge(c1_mm, i)
                v.tensor_copy(xT[:], psA[:, 0:BN]).then_inc(xT_sb, 1)
                v.wait_ge(c2_mm, i + 1)
                v.wait_ge(x1_out, 16 * i)
                v.wait_ge(x1_T, i)
                chain.then(v.tensor_tensor(y, tiles_of(psD[:, 0:BN]), bcast_mid(b_c2[:], BT), ALU.add))
                v.wait_ge(x_in, 16 * i + 16)
                chain.then(v.tensor_tensor(y, y, x_rows, ALU.add))
                norm.vector(v, chain, y, i)
                v.sem_inc(x1_ok, 1)
                v.wait_ge(x1_T, i + 1)
                v.wait_ge(h_mm, i)
                v.tensor_copy(x1T[:], psA[:, 0:BN]).then_inc(x1T_sb, 1)
                v.wait_ge(h_mm, i + 1)
                v.wait_ge(stored, 16 * i)
                v.tensor_copy(sh.src_terms1[:, bass.ds(i * BT, BT)], psD[:, BN:BN + BT])
                v.tensor_copy(table[:, :, D + 1], psD[:, BN:BN + BT]).then_inc(terms_ok, 1)
                chain.close()


SHIFT_MARGIN = 45.0
SLOPE = 0.2
NO_EDGE = -1.0e30


def softmax_edges(nc, sh):
    with ExitStack() as ctx:
        sb, ps, sem = scope(nc, ctx)
        rows = sb("rows1", [P, RING, TROW])
        one_hots = sb("one_hot1", [P, 2, GRP, WIN])
        S = sb("S1", [P, 2, GRP, 2, WIN])
        picked = sb("picked1", [P, GRP, WIN])
        dst_term = sb("dst_term1", [P, GRP])
        z = sb("z1", [P, GRP])
        far = sb("far1", [P, GRP])
        leaky = sb("leaky1", [P, 2, GRP])
        a = sb("a1", [P, 2, GRP])
        w_all = sb("w_all1", [P, TCOLS])
        top = sb("top1", [P, 2])
        top_src = sb("top_src", [P, 1])
        best = sb("best", [P, GRP])
        out = ps("out1", [P, 2, GRP, 256])
        index_ready, granted = sem("index_ready"), sem("granted")
        w_in, top_ok, top_all, shift_link = sem("w_in"), sem("top_ok"), sem("top_all"), sem("shift_link")
        link, z_ready, a_ready, s_ready = sem("link"), sem("z_ready"), sem("a_ready"), sem("s_ready")
        summed, added, drained = sem("summed"), sem("added"), sem("drained")
        block = ctx.enter_context(nc.Block())
        LINKS = 8

        @block.sync
        def _(sp):
            sp.dma_start(w_all[:], sh.w_dram).then_inc(w_in, 16)
            sp.wait_ge(w_in, 16)

        @block.gpsimd
        def _(pool):
            pool.wait_ge(top_ok, 1)
            pool.partition_all_reduce(top_src[:], top[:, 0:1], P, bass.bass_isa.ReduceOp.max
                                      ).then_inc(top_all, 1)
            with pool.Fori(0, GROUPS // 4) as i:
                for q in range(4):
                    gather_rows(pool, sh.table1, rows, index_ready, granted, sh, i * 4 + q, q)

        @block.scalar
        def _(act):
            def step(i, q):
                n = i * 4 + q
                stage_indices(act, sh, index_ready, summed, n + 2, (q + 2) % 4)
                act.wait_ge(z_ready, n + 1)
                at_least(act, s_ready, n - 1)
                act.activation(a[:, q % 2], leaky[:, q % 2], ACT.Exp,
                               bias=sh.minus_shift[:, 0:1]).then_inc(a_ready, 1)

            for q in range(2):
                stage_indices(act, sh, index_ready, summed, q, q)
            for q in range(4):
                step(0, q)
            with act.Fori(1, GROUPS // 4) as i:
                for q in range(4):
                    step(i, q)

        @block.tensor
        def _(pe):
            def step(i, q):
                n = i * 4 + q
                pe.wait_ge(s_ready, n + 1)
                at_least(pe, drained, n - 1)
                for u in range(GRP):
                    mm = pe.matmul(out[0:2 * WIN, q % 2, u, 0:AROW],
                                   S[:, q % 2, u].rearrange("p k d -> p (k d)"),
                                   rows[:, GRP * q + u, 0:AROW], start=True, stop=True)
                mm.then_inc(summed, 1)

            for q in range(4):
                step(0, q)
            with pe.Fori(1, GROUPS // 4) as i:
                for q in range(4):
                    step(i, q)

        @block.vector
        def _(v):
            windows = TileWindows(v, sh, "l1")

            def add_up(n, q):
                into = windows.of(q)
                v.wait_ge(summed, n + 1)
                for u, window in enumerate(into):
                    to = window_slice(sh.acc, window, AROW)[0:2 * WIN]
                    v.wait_ge(added, n * GRP + u + 1)
                    v.tensor_tensor(to, to, out[0:2 * WIN, q % 2, u, 0:AROW], ALU.add).then_inc(added, 1)
                v.wait_ge(added, n * GRP + GRP + 1)
                v.sem_inc(drained, 1)

            def step(i, q, first=False):
                n = i * 4 + q
                b = q % 2
                chain = Chain(v, link, n, LINKS)
                one_hot = one_hots[:, b]
                at_least(v, summed, n - 1)
                rel = sh.rel_all[:, bass.ds(n * GRP, GRP)]
                chain.then(v.tensor_tensor(one_hot, bcast_last(rel, WIN), bcast_mid(sh.iota[:], GRP),
                                           ALU.is_equal))
                windows.load(i, q)
                for u, window in enumerate(windows.of(q)):
                    ins = v.tensor_tensor(picked[:, u], window_slice(sh.dst_terms1, window, WIN),
                                          one_hot[:, u, :], ALU.mult)
                chain.then(ins)
                chain.then(v.tensor_reduce(dst_term[:], picked[:], axis=AX.X, op=ALU.add))
                wait_gathered(v, sh, 1, i, q)
                chain.then(v.tensor_tensor(z[:], dst_term[:], rows[:, GRP * q:GRP * q + GRP, D + 1],
                                           ALU.add))
                v.scalar_tensor_tensor(out=leaky[:, b], in0=z[:], scalar=SLOPE, in1=z[:],
                                       op0=ALU.mult, op1=ALU.max).then_inc(z_ready, 1)
                chain.then(v.tensor_scalar(far[:], rel, float(WIN), NO_EDGE, op0=ALU.is_ge, op1=ALU.mult))
                chain.then(v.tensor_tensor(far[:], far[:], z[:], ALU.add))
                chain.then(v.tensor_tensor(best[:], best[:], far[:], ALU.max))
                chain.then(v.tensor_tensor(S[:, b, :, 1, :], one_hot[:],
                                           bcast_last(w_all[:, bass.ds(n * GRP, GRP)], WIN), ALU.mult))
                chain.close()
                if not first:
                    add_up(n - 1, (q - 1) % 4)
                v.wait_ge(a_ready, n + 1)
                v.tensor_tensor(S[:, b, :, 0, :], one_hot, bcast_last(a[:, b], WIN),
                                ALU.mult).then_inc(s_ready, 1)

            v.tensor_reduce(top[:, 0:1], sh.src_terms1[:], axis=AX.X, op=ALU.max).then_inc(top_ok, 1)
            v.tensor_reduce(top[:, 1:2], sh.dst_terms1[:], axis=AX.X, op=ALU.max)
            v.memset(best[:], NO_EDGE)
            v.memset(sh.acc[:], 0.0).then_inc(added, 1)
            v.wait_ge(added, 1)
            v.wait_ge(top_all, 1)
            once = Chain(v, shift_link)
            once.then(v.tensor_tensor(top[:, 0:1], top_src[:], top[:, 1:2], ALU.add))
            once.then(v.scalar_tensor_tensor(out=top[:, 1:2], in0=top[:, 0:1], scalar=SLOPE,
                                             in1=top[:, 0:1], op0=ALU.mult, op1=ALU.max))
            once.then(v.tensor_scalar(sh.minus_shift[:], top[:, 1:2], -1.0, SHIFT_MARGIN,
                                      op0=ALU.mult, op1=ALU.add))
            v.wait_ge(w_in, 16)
            for q in range(4):
                step(0, q, first=q == 0)
            with v.Fori(1, GROUPS // 4) as i:
                for q in range(4):
                    step(i, q)
            add_up(GROUPS - 1, 3)
            v.tensor_reduce(sh.best[:], best[:], axis=AX.X, op=ALU.max)


def place_rows(pe, sh, out, i, width):
    for j in range(BT):
        for q in range(4):
            row = window_slice(sh.acc, i * BW + 4 * j + q, AROW)[0:WIN, 0:width]
            mm = pe.matmul(out[:, j, 0:width], sh.place[0:WIN, q, :], row, start=q == 0, stop=q == 3)
    return mm


def finish_softmax(nc, sh, w):
    with ExitStack() as ctx:
        sb, ps, sem = scope(nc, ctx)
        x_rows, y = tiles_of(sb("x_rows2", [P, BN])[:]), tiles_of(sb("y2", [P, BN])[:])
        act_out = tiles_of(sb("gelu2", [P, BN])[:])
        gamma, beta = sb("gamma2", [P, D]), sb("beta2", [P, D])
        best_all, score, small = sb("best_all", [P, 1]), sb("score2", [P, 1]), sb("small2", [P, 1])
        den, inv = sb("den2", [P, BT]), sb("inv2", [P, BT])
        norm_a, norm_b = Norm(sb, sem, "norm2a"), Norm(sb, sem, "norm2b")
        out = ps("placed2", [P, BT + 1, 256])
        deg = ps("deg2", [P, NODE_TILES])
        params, best_ok, score_ok, small_ok, small_link = (
            sem(n) for n in ("params", "best_ok", "score_ok", "small_ok", "small_link"))
        deg_mm, placed, read, x_in, link, in_gelu, gelu_ok, x2_ok, stored = (
            sem(n) for n in ("deg_mm", "placed", "read", "x_in", "link", "in_gelu", "gelu_ok", "x2_ok", "stored"))
        block = ctx.enter_context(nc.Block())

        @block.sync
        def _(sp):
            sp.dma_start(gamma[:], row_of(w["L1_gnn_ln_gamma"])).then_inc(params, 16)
            sp.dma_start(beta[:], row_of(w["L1_gnn_ln_beta"])).then_inc(params, 16)
            with sp.Fori(0, BATCHES) as i:
                sp.wait_ge(x2_ok, i)
                sp.dma_start(x_rows, batch_rows(sh.x1, i)).then_inc(x_in, 16)
                sp.wait_ge(x2_ok, i + 1)
                sp.dma_start(batch_rows(sh.x2, i), y).then_inc(stored, 16)
            sp.wait_ge(stored, 16 * BATCHES)

        @block.gpsimd
        def _(pool):
            pool.partition_all_reduce(best_all[:], sh.best[:], P, bass.bass_isa.ReduceOp.max
                                      ).then_inc(best_ok, 1)

        @block.tensor
        def _(pe):
            for q in range(4):
                col = sh.acc[WIN:2 * WIN, :].rearrange("p (c q f) -> p c q f", q=4, f=AROW)[:, :, q, D]
                mm = pe.matmul(deg[:], sh.place[WIN:2 * WIN, q, :], col, start=q == 0, stop=q == 3)
            mm.then_inc(deg_mm, 1)
            with pe.Fori(0, BATCHES) as i:
                pe.wait_ge(read, i)
                place_rows(pe, sh, out, i, AROW).then_inc(placed, 1)

        @block.scalar
        def _(act):
            act.wait_ge(score_ok, 1)
            act.activation(small[:], score[:], ACT.Exp, bias=sh.minus_shift[:, 0:1]).then_inc(small_ok, 1)
            with act.Fori(0, BATCHES) as i:
                norm_a.scalar(act, sh, i)
                act.wait_ge(in_gelu, i + 1)
                act.activation(act_out, y, ACT.Gelu).then_inc(gelu_ok, 1)
                norm_b.scalar(act, sh, i)

        @block.vector
        def _(v):
            once = Chain(v, small_link)
            v.wait_ge(best_ok, 1)
            v.scalar_tensor_tensor(out=score[:], in0=best_all[:], scalar=SLOPE, in1=best_all[:],
                                   op0=ALU.mult, op1=ALU.max).then_inc(score_ok, 1)
            v.wait_ge(small_ok, 1)
            once.then(v.tensor_scalar(small[:], small[:], 1e-6, None, op0=ALU.mult))
            v.wait_ge(deg_mm, 1)
            once.then(v.tensor_copy(sh.weight_sum[:], deg[:]))
            v.wait_ge(params, 32)
            with v.Fori(0, BATCHES) as i:
                chain = Chain(v, link, i, 6 + 2 * NORM_LINKS)
                v.wait_ge(placed, i + 1)
                chain.then(v.tensor_scalar(den[:], out[:, 0:BT, D], small[:, 0:1], None, op0=ALU.add))
                chain.then(v.reciprocal(inv[:], den[:]))
                v.wait_ge(x_in, 16 * i + 16)
                v.wait_ge(stored, 16 * i)
                for j in range(BT):
                    ins = v.scalar_tensor_tensor(out=y[:, j, :], in0=out[:, j, 0:D],
                                                 scalar=inv[:, j:j + 1], in1=x_rows[:, j, :],
                                                 op0=ALU.mult, op1=ALU.add)
                chain.then(ins)
                v.sem_inc(read, 1)
                norm_a.vector(v, chain, y, i)
                chain.then(v.tensor_tensor(y, y, bcast_mid(gamma[:], BT), ALU.mult))
                chain.then(v.tensor_tensor(y, y, bcast_mid(beta[:], BT), ALU.add))
                v.sem_inc(in_gelu, 1)
                v.wait_ge(gelu_ok, i + 1)
                chain.then(v.tensor_tensor(y, act_out, x_rows, ALU.add))
                norm_b.vector(v, chain, y, i)
                v.sem_inc(x2_ok, 1)
                chain.close()


def relation_edges(nc, sh, w):
    with ExitStack() as ctx:
        sb, ps, sem = scope(nc, ctx)
        rows = sb("rows2", [P, RING, D])
        one_hot = sb("one_hot2", [P, GRP, WIN])
        S = sb("S2", [P, 2, GRP, BASES, WIN])
        types = sb("types2", [RELS, 4, GRP * P])
        type_hot = sb("type_hot", [RELS, 2, GRP * P])
        rel_id = sb("rel_id", [RELS, 1])
        compT = sb("compT", [RELS, BASES])
        coef = sb("coef", [P, GRP, BASES])
        T = sb("T2", [P, 2, BASES, GRP, WIN])
        w_base = sb("w_base", [P, BASES, D])
        n_all = sb("n_all2", [P, TCOLS])
        per_base = ps("per_base", [P, 2, GRP, BASES * WIN])
        coef_ps = ps("coef_ps", [P, GRP * BASES])
        summed_ps = ps("summed_ps", [P, 2, 512])
        params, rel_ok, setup = sem("params"), sem("rel_ok"), sem("setup")
        index_ready, granted = sem("index_ready"), sem("granted")
        types_in = [sem(f"types_in{s}") for s in range(4)]
        type_ok, coef_mm, link, s_ready = sem("type_ok"), sem("coef_mm"), sem("link"), sem("s_ready")
        coef_read = sem("coef_read")
        based, T_ok, summed, added, drained = (
            sem(n) for n in ("based", "T_ok", "summed", "added", "drained"))
        block = ctx.enter_context(nc.Block())
        PARAMS = 3 * 16
        LINKS = 2

        def load_types(sp, n, q):
            at_least(sp, type_ok, n - 3)
            types_row = sh.type_rows[bass.ds(n * GRP, GRP), :].rearrange("a b -> (a b)")
            sp.dma_start(types[:, q, :], row_of(types_row, RELS)).then_inc(types_in[q], 16)

        @block.sync
        def _(sp):
            sp.dma_start(w_base[:], w["L2_gnn_weight"].rearrange("b d f -> d b f")).then_inc(params, 16)
            sp.dma_start(compT[:], w["L2_gnn_w_comp"]).then_inc(params, 16)
            sp.dma_start(n_all[:], sh.n_dram).then_inc(params, 16)
            for q in range(4):
                load_types(sp, q, q)
            with sp.Fori(1, GROUPS // 4) as i:
                for q in range(4):
                    load_types(sp, i * 4 + q, q)
            load_types(sp, GROUPS, 0)
            sp.wait_ge(params, PARAMS)
            for q in range(4):
                sp.wait_ge(types_in[q], 16 * (GROUPS // 4 + (q == 0)))

        @block.gpsimd
        def _(pool):
            pool.iota(rel_id[:], pattern=[[1, 1]], base=0, channel_multiplier=1,
                      allow_small_or_imprecise_dtypes=True).then_inc(rel_ok, 1)
            with pool.Fori(0, GROUPS // 4) as i:
                for q in range(4):
                    gather_rows(pool, sh.x2, rows, index_ready, granted, sh, i * 4 + q, q)

        @block.scalar
        def _(act):
            def step(i, q):
                n = i * 4 + q
                stage_indices(act, sh, index_ready, based, n + 2, (q + 2) % 4)
                act.wait_ge(based, n + 1)
                at_least(act, summed, n - 1)
                for u in range(GRP):
                    ins = act.copy(T[:, q % 2, :, u, :],
                                   per_base[:, q % 2, u, :].rearrange("p (b d) -> p b d", d=WIN))
                ins.then_inc(T_ok, 1)

            for q in range(2):
                stage_indices(act, sh, index_ready, based, q, q)
            for q in range(4):
                step(0, q)
            with act.Fori(1, GROUPS // 4) as i:
                for q in range(4):
                    step(i, q)

        @block.tensor
        def _(pe):
            def coefficients(n, b):
                pe.wait_ge(type_ok, n + 1)
                at_least(pe, coef_read, n)
                for u in range(GRP):
                    mm = pe.matmul(coef_ps[:, BASES * u:BASES * u + BASES],
                                   type_hot[:, b, P * u:P * u + P], compT[:], start=True, stop=True)
                mm.then_inc(coef_mm, 1)

            def over_bases(n, b):
                pe.wait_ge(T_ok, n + 1)
                at_least(pe, drained, n - 1)
                for k in range(BASES):
                    mm = pe.matmul(summed_ps[:, b, 0:GRP * WIN], w_base[:, k, :],
                                   T[:, b, k].rearrange("p u d -> p (u d)"),
                                   start=k == 0, stop=k == BASES - 1)
                mm.then_inc(summed, 1)

            def step(i, q, first=False):
                n = i * 4 + q
                b = q % 2
                pe.wait_ge(s_ready, n + 1)
                wait_gathered(pe, sh, 2, i, q)
                at_least(pe, T_ok, n - 1)
                for u in range(GRP):
                    mm = pe.matmul(per_base[:, b, u, :], rows[:, GRP * q + u, :],
                                   S[:, b, u].rearrange("p k d -> p (k d)"), start=True, stop=True)
                mm.then_inc(based, 1)
                coefficients(n + 1, 1 - b)
                if not first:
                    over_bases(n - 1, 1 - b)

            pe.wait_ge(params, PARAMS)
            coefficients(0, 0)
            for q in range(4):
                step(0, q, first=q == 0)
            with pe.Fori(1, GROUPS // 4) as i:
                for q in range(4):
                    step(i, q)
            over_bases(GROUPS - 1, 1)

        @block.vector
        def _(v):
            windows = TileWindows(v, sh, "l2")

            def type_one_hot(turn, q, n):
                v.wait_ge(types_in[q], turn * 16 + 16)
                at_least(v, coef_mm, n - 1)
                v.tensor_scalar(type_hot[:, q % 2], types[:, q, :], rel_id[:, 0:1], None,
                                op0=ALU.is_equal).then_inc(type_ok, 1)

            def add_up(n, q):
                into = windows.of(q)
                v.wait_ge(summed, n + 1)
                for u, window in enumerate(into):
                    to = window_slice(sh.acc, window, WIN)
                    v.wait_ge(added, n * GRP + u + 1)
                    v.tensor_tensor(to, to, summed_ps[:, q % 2, WIN * u:WIN * u + WIN],
                                    ALU.add).then_inc(added, 1)
                v.wait_ge(added, n * GRP + GRP + 1)
                v.sem_inc(drained, 1)

            def step(i, q, lag_ok=True):
                n = i * 4 + q
                b = q % 2
                chain = Chain(v, link, n, LINKS)
                type_one_hot(i + (q + 1) // 4, (q + 1) % 4, n + 1)
                v.tensor_tensor(one_hot[:], bcast_last(sh.rel_all[:, bass.ds(n * GRP, GRP)], WIN),
                                bcast_mid(sh.iota[:], GRP), ALU.is_equal)
                v.wait_ge(coef_mm, n + 1)
                chain.then(v.tensor_tensor(coef[:], coef_ps[:].rearrange("p (u k) -> p u k", k=BASES),
                                           bcast_last(n_all[:, bass.ds(n * GRP, GRP)], BASES), ALU.mult))
                v.sem_inc(coef_read, 1)
                at_least(v, based, n - 1)
                for u in range(GRP):
                    ins = v.tensor_tensor(S[:, b, u], bcast_mid(one_hot[:, u, :], BASES),
                                          bcast_last(coef[:, u, :], WIN), ALU.mult)
                chain.then(ins)
                v.sem_inc(s_ready, 1)
                chain.close()
                if lag_ok:
                    add_up(n - 2, (q - 2) % 4)
                if q == 1:
                    windows.load_all(i)

            v.memset(sh.acc[:, 0:NPAD], 0.0).then_inc(added, 1)
            v.wait_ge(rel_ok, 1)
            v.wait_ge(params, PARAMS)
            type_one_hot(0, 0, 0)
            for q in range(4):
                step(0, q, lag_ok=q >= 2)
            with v.Fori(1, GROUPS // 4) as i:
                for q in range(4):
                    step(i, q)
            add_up(GROUPS - 2, 2)
            add_up(GROUPS - 1, 3)


def finish_relations(nc, sh, w):
    with ExitStack() as ctx:
        sb, ps, sem = scope(nc, ctx)
        x_rows, y = tiles_of(sb("x_rows3", [P, BN])[:]), tiles_of(sb("y3", [P, BN])[:])
        xT, sums, x3T = sb("xT3", [P, BN]), sb("sums3", [P, BN]), sb("x3T", [P, BN])
        table = tiles_of(sb("table3", [P, BN])[:])
        w_loop, w3, bias = sb("w_loop", [P, D]), sb("w3", [P, D]), sb("bias3", [P, D])
        deg, above, root = sb("deg3", [P, NODE_TILES]), sb("above3", [P, NODE_TILES]), sb("root3", [P, NODE_TILES])
        norm = Norm(sb, sem, "norm3")
        psA, psB, psC, psD = (ps(f"ps3{c}", [P, 1024]) for c in "ABCD")
        params, setup, deg_ok, root_ok, dinv_ok = (
            sem(n) for n in ("params", "setup", "deg_ok", "root_ok", "dinv_ok"))
        x_in, x_T, xT_sb, sums_ok, mixed, x3_ok, x3_T, x3T_sb, xw, table_ok, stored, x3_out, link = (
            sem(n) for n in ("x_in", "x_T", "xT_sb", "sums_ok", "mixed", "x3_ok", "x3_T", "x3T_sb",
                             "xw", "table_ok", "stored", "x3_out", "link"))
        block = ctx.enter_context(nc.Block())

        @block.sync
        def _(sp):
            sp.dma_start(w_loop[:], w["L2_gnn_loop_weight"]).then_inc(params, 16)
            sp.dma_start(w3[:], w["L3_gnn_W"]).then_inc(params, 16)
            sp.dma_start(bias[:], row_of(w["L2_gnn_h_bias"])).then_inc(params, 16)
            with sp.Fori(0, BATCHES) as i:
                sp.wait_ge(x3_ok, i)
                sp.dma_start(x_rows, batch_rows(sh.x2, i)).then_inc(x_in, 16)
                sp.wait_ge(x3_ok, i + 1)
                sp.dma_start(batch_rows(sh.x3, i), y).then_inc(x3_out, 16)
                sp.wait_ge(table_ok, i + 1)
                sp.dma_start(batch_rows(sh.table3, i), table).then_inc(stored, 16)
            sp.wait_ge(x3_out, 16 * BATCHES)
            sp.wait_ge(stored, 16 * BATCHES)

        @block.tensor
        def _(pe):
            pe.wait_ge(params, 48)
            with pe.Fori(0, BATCHES) as i:
                pe.wait_ge(x_in, 16 * i + 16)
                pe.wait_ge(xT_sb, i)
                transpose_tiles(pe, psA, x_rows, sh.ident).then_inc(x_T, 1)
                pe.wait_ge(xT_sb, i + 1)
                pe.wait_ge(sums_ok, i + 1)
                for j in range(BT):
                    cols = slice(P * j, P * j + P)
                    pe.matmul(psB[:, cols], sums[:, cols], sh.ident[:], start=True, stop=False)
                    mm = pe.matmul(psB[:, cols], xT[:, cols], w_loop[:], start=False, stop=True)
                mm.then_inc(mixed, 1)
                pe.wait_ge(x3_ok, i + 1)
                transpose_tiles(pe, psC, y, sh.ident).then_inc(x3_T, 1)
                pe.wait_ge(x3T_sb, i + 1)
                pe.wait_ge(table_ok, i)
                for j in range(BT):
                    cols = slice(P * j, P * j + P)
                    mm = pe.matmul(psD[:, cols], x3T[:, cols], w3[:], start=True, stop=True)
                mm.then_inc(xw, 1)

        @block.scalar
        def _(act):
            act.wait_ge(deg_ok, 1)
            act.activation(root[:], deg[:], ACT.Sqrt).then_inc(root_ok, 1)
            with act.Fori(0, BATCHES) as i:
                act.wait_ge(mixed, i)
                act.copy(sums[:], sh.acc[:, bass.ds(i * BN, BN)]).then_inc(sums_ok, 1)
                norm.scalar(act, sh, i)
                act.wait_ge(x3_T, i + 1)
                act.wait_ge(xw, i)
                act.copy(x3T[:], psC[:, 0:BN]).then_inc(x3T_sb, 1)

        @block.vector
        def _(v):
            once = Chain(v, setup)
            once.then(v.tensor_scalar(deg[:], sh.weight_sum[:], 1.0, None, op0=ALU.add))
            once.then(v.tensor_scalar(above[:], deg[:], 0.0, None, op0=ALU.is_gt))
            v.tensor_scalar(deg[:], deg[:], 1e-35, None, op0=ALU.max).then_inc(deg_ok, 1)
            v.wait_ge(root_ok, 1)
            once.then(v.reciprocal(root[:], root[:]))
            once.then(v.tensor_tensor(sh.dinv[:], root[:], above[:], ALU.mult))
            v.wait_ge(params, 48)
            with v.Fori(0, BATCHES) as i:
                chain = Chain(v, link, i, 3 + NORM_LINKS)
                v.wait_ge(x_T, i + 1)
                v.wait_ge(mixed, i)
                v.tensor_copy(xT[:], psA[:, 0:BN]).then_inc(xT_sb, 1)
                v.wait_ge(mixed, i + 1)
                v.wait_ge(x3_out, 16 * i)
                v.wait_ge(x3_T, i)
                chain.then(v.tensor_tensor(y, tiles_of(psB[:, 0:BN]), bcast_mid(bias[:], BT), ALU.add))
                chain.then(v.tensor_scalar(y, y, 0.0, None, op0=ALU.max))
                chain.then(v.tensor_tensor(y, y, x_rows, ALU.add))
                norm.vector(v, chain, y, i)
                v.sem_inc(x3_ok, 1)
                v.wait_ge(xw, i + 1)
                v.wait_ge(stored, 16 * i)
                v.tensor_tensor(table, tiles_of(psD[:, 0:BN]),
                                bcast_last(sh.dinv[:, bass.ds(i * BT, BT)], D),
                                ALU.mult).then_inc(table_ok, 1)
                chain.close()


def convolution_edges(nc, sh):
    with ExitStack() as ctx:
        sb, ps, sem = scope(nc, ctx)
        rows = sb("rows3", [P, RING, D])
        one_hot = sb("one_hot3", [P, 2, GRP, WIN])
        S = sb("S3", [P, 2, GRP, WIN])
        w_all = sb("w_all3", [P, TCOLS])
        out = ps("out3", [P, 2, GRP, 256])
        index_ready, granted, w_in = sem("index_ready"), sem("granted"), sem("w_in")
        link, s_ready = sem("link"), sem("s_ready")
        summed, added, drained = sem("summed"), sem("added"), sem("drained")
        block = ctx.enter_context(nc.Block())

        @block.sync
        def _(sp):
            sp.dma_start(w_all[:], sh.w_dram).then_inc(w_in, 16)
            sp.wait_ge(w_in, 16)

        @block.gpsimd
        def _(pool):
            with pool.Fori(0, GROUPS // 4) as i:
                for q in range(4):
                    gather_rows(pool, sh.table3, rows, index_ready, granted, sh, i * 4 + q, q)

        @block.scalar
        def _(act):
            for q in range(4):
                stage_indices(act, sh, index_ready, summed, q, q)
            with act.Fori(1, GROUPS // 4) as i:
                for q in range(4):
                    stage_indices(act, sh, index_ready, summed, i * 4 + q, q)

        @block.tensor
        def _(pe):
            def step(i, q):
                n = i * 4 + q
                pe.wait_ge(s_ready, n + 1)
                at_least(pe, drained, n - 1)
                wait_gathered(pe, sh, 3, i, q)
                for u in range(GRP):
                    mm = pe.matmul(out[0:WIN, q % 2, u, 0:D], S[:, q % 2, u, :],
                                   rows[:, GRP * q + u, :], start=True, stop=True)
                mm.then_inc(summed, 1)

            for q in range(4):
                step(0, q)
            with pe.Fori(1, GROUPS // 4) as i:
                for q in range(4):
                    step(i, q)

        @block.vector
        def _(v):
            windows = TileWindows(v, sh, "l3")

            def add_up(n, q):
                into = windows.of(q)
                v.wait_ge(summed, n + 1)
                for u, window in enumerate(into):
                    to = window_slice(sh.acc, window, AROW)[0:WIN, 0:D]
                    v.wait_ge(added, n * GRP + u + 1)
                    v.tensor_tensor(to, to, out[0:WIN, q % 2, u, 0:D], ALU.add).then_inc(added, 1)
                v.wait_ge(added, n * GRP + GRP + 1)
                v.sem_inc(drained, 1)

            def step(i, q, first=False):
                n = i * 4 + q
                at_least(v, summed, n - 1)
                v.tensor_tensor(one_hot[:, q % 2], bcast_last(sh.rel_all[:, bass.ds(n * GRP, GRP)], WIN),
                                bcast_mid(sh.iota[:], GRP), ALU.is_equal).then_inc(link, 1)
                v.wait_ge(link, n + 1)
                v.tensor_tensor(S[:, q % 2], one_hot[:, q % 2], bcast_last(w_all[:, bass.ds(n * GRP, GRP)], WIN),
                                ALU.mult).then_inc(s_ready, 1)
                if not first:
                    add_up(n - 1, (q - 1) % 4)
                windows.load(i, q)

            v.memset(sh.acc[0:WIN, :], 0.0).then_inc(added, 1)
            v.wait_ge(w_in, 16)
            for q in range(4):
                step(0, q, first=q == 0)
            with v.Fori(1, GROUPS // 4) as i:
                for q in range(4):
                    step(i, q)
            add_up(GROUPS - 1, 3)


def finish_convolution(nc, sh, w, result):
    with ExitStack() as ctx:
        sb, ps, sem = scope(nc, ctx)
        own = sb("own4", [P, NODE_TILES, D])
        y = sb("y4", [P, NODE_TILES, D])
        x3 = tiles_of(sb("x34", [P, BN])[:])
        bias, gamma, beta = sb("bias4", [P, D]), sb("gamma4", [P, D]), sb("beta4", [P, D])
        real = sb("real4", [P, 1])
        part, mean, scale = sb("part4", [P, D]), sb("mean4", [P, D]), sb("scale4", [P, D])
        norm = Norm(sb, sem, "norm4")
        out = ps("placed4", [P, BT + 1, 256])
        total = ps("total4", [P, 2, 512])
        params, real_ok, own_in, placed, read, link1, link2, link3 = (
            sem(n) for n in ("params", "real_ok", "own_in", "placed", "read", "link1", "link2", "link3"))
        part_ok, total_ok, root_ok, x_in, done, stored = (
            sem(n) for n in ("part_ok", "total_ok", "root_ok", "x_in", "done", "stored"))
        block = ctx.enter_context(nc.Block())
        FULL = NODE_TILES - 1

        @block.sync
        def _(sp):
            sp.dma_start(own[:], sh.table3.rearrange("(c p) f -> p c f", p=P)).then_inc(own_in, 16)
            sp.dma_start(bias[:], row_of(w["L3_gnn_b"])).then_inc(params, 16)
            sp.dma_start(gamma[:], row_of(w["L3_gnn_gamma"])).then_inc(params, 16)
            sp.dma_start(beta[:], row_of(w["L3_gnn_beta"])).then_inc(params, 16)
            with sp.Fori(0, BATCHES) as i:
                sp.wait_ge(done, i)
                sp.dma_start(x3, batch_rows(sh.x3, i)).then_inc(x_in, 16)
            sp.wait_ge(done, BATCHES)
            sp.dma_start(result[0:FULL * P, :].rearrange("(c p) f -> p c f", p=P),
                         y[:, 0:FULL, :]).then_inc(stored, 16)
            sp.dma_start(result[FULL * P:N, :], y[0:N - FULL * P, FULL, :]).then_inc(stored, 16)
            sp.wait_ge(stored, 32)

        @block.gpsimd
        def _(pool):
            pool.affine_select(out=real[:], in_=sh.ones[:, 0:1], compare_op=ALU.is_gt, fill=0.0,
                               base=N - FULL * P, pattern=[[0, 1]], channel_multiplier=-1
                               ).then_inc(real_ok, 1)

        @block.tensor
        def _(pe):
            with pe.Fori(0, BATCHES) as i:
                pe.wait_ge(read, i)
                place_rows(pe, sh, out, i, D).then_inc(placed, 1)
            for k in range(2):
                pe.wait_ge(part_ok, k + 1)
                pe.matmul(total[:, k, 0:D], sh.ones[:], part[:], start=True, stop=True
                          ).then_inc(total_ok, 1)

        @block.scalar
        def _(act):
            act.wait_ge(part_ok, 3)
            act.activation(scale[:], scale[:], ACT.Sqrt, bias=sh.eps[:, 0:1]).then_inc(root_ok, 1)
            with act.Fori(0, BATCHES) as i:
                norm.scalar(act, sh, i)

        @block.vector
        def _(v):
            by_feature = lambda t: t[:].rearrange("p c f -> p f c")
            v.wait_ge(own_in, 16)
            v.wait_ge(params, 48)
            with v.Fori(0, BATCHES) as i:
                chain = Chain(v, link1, i, 3)
                rows = bass.ds(i * BT, BT)
                v.wait_ge(placed, i + 1)
                chain.then(v.tensor_tensor(y[:, rows, :], out[:, 0:BT, 0:D], own[:, rows, :], ALU.add))
                v.sem_inc(read, 1)
                chain.then(v.tensor_tensor(y[:, rows, :], y[:, rows, :],
                                           bcast_last(sh.dinv[:, rows], D), ALU.mult))
                chain.then(v.tensor_tensor(y[:, rows, :], y[:, rows, :], bcast_mid(bias[:], BT), ALU.add))
                chain.close()
            once = Chain(v, link2)
            v.wait_ge(real_ok, 1)
            once.then(v.tensor_scalar(y[:, FULL, :], y[:, FULL, :], real[:, 0:1], None, op0=ALU.mult))
            v.tensor_reduce(part[:], by_feature(y), axis=AX.X, op=ALU.add).then_inc(part_ok, 1)
            v.wait_ge(total_ok, 1)
            once.then(v.tensor_scalar(mean[:], total[:, 0, 0:D], 1.0 / N, None, op0=ALU.mult))
            once.then(v.tensor_tensor(y[:], y[:], bcast_mid(mean[:], NODE_TILES), ALU.subtract))
            once.then(v.tensor_scalar(y[:, FULL, :], y[:, FULL, :], real[:, 0:1], None, op0=ALU.mult))
            once.then(v.tensor_tensor(own[:], y[:], y[:], ALU.mult))
            v.tensor_reduce(part[:], by_feature(own), axis=AX.X, op=ALU.add).then_inc(part_ok, 1)
            v.wait_ge(total_ok, 2)
            v.tensor_scalar(scale[:], total[:, 1, 0:D], 1.0 / N, None, op0=ALU.mult).then_inc(part_ok, 1)
            v.wait_ge(root_ok, 1)
            once.then(v.reciprocal(scale[:], scale[:]))
            once.then(v.tensor_tensor(scale[:], scale[:], gamma[:], ALU.mult))
            once.then(v.tensor_tensor(y[:], y[:], bcast_mid(scale[:], NODE_TILES), ALU.mult))
            once.then(v.tensor_tensor(y[:], y[:], bcast_mid(beta[:], NODE_TILES), ALU.add))
            once.then(v.tensor_scalar(y[:], y[:], 0.0, None, op0=ALU.max))
            with v.Fori(0, BATCHES) as i:
                chain = Chain(v, link3, i, 1 + NORM_LINKS)
                rows = y[:, bass.ds(i * BT, BT), :]
                v.wait_ge(x_in, 16 * i + 16)
                chain.then(v.tensor_tensor(rows, rows, x3, ALU.add))
                norm.vector(v, chain, rows, i)
                v.sem_inc(done, 1)
                chain.close()





def build(nc, w, result):
    def dram(name, shape, dt=F32):
        return nc.dram_tensor(name, shape, dt, kind="Internal").ap()

    with ExitStack() as ctx:
        sb, _, _ = scope(nc, ctx)
        sh = Shared()
        _, _, sem = scope(nc, ctx)
        sh.rows_in, sh.fetched = sem("rows_in"), [sem(f"fetched{k}") for k in range(5)]
        sh.gathered = [sem(f"gathered{s}") for s in range(RING)]
        sh.first_sem = sh.gathered[-1].num + 1
        sh.ident, sh.iota, sh.ones = sb("ident", [P, P]), sb("iota", [P, WIN]), sb("ones", [P, P])
        sh.eps, sh.place = sb("eps", [P, 1]), sb("place", [P, 4, P])
        sh.src_all, sh.rel_all = sb("src_all", [P, TCOLS], U16), sb("rel_all", [P, TCOLS], BF16)
        sh.win_all, sh.index = sb("win_all", [1, TCOLS], U8), sb("index", [P, RING], I32)
        sh.minus_shift, sh.best = sb("minus_shift", [P, 1]), sb("best_edge", [P, 1])
        sh.weight_sum, sh.dinv = sb("weight_sum", [P, NODE_TILES]), sb("dinv", [P, NODE_TILES])
        sh.acc = sb("acc", [P, WINDOWS * AROW])
        sh.xpad, sh.x1, sh.x2, sh.x3 = (dram(n, (NPAD, D)) for n in ("xpad", "x1", "x2", "x3"))
        sh.table, sh.table1 = dram("table0", (NPAD, TROW)), dram("table1_rows", (NPAD, TROW))
        sh.table3 = dram("table3_rows", (NPAD, D))
        fields = [dram(f"edge_{n}", (EPAD,), dt) for n, dt in
                  (("src", I32), ("dst", I32), ("type", I32), ("weight", F32), ("norm", F32))]
        win_dram = dram("win_dram", (TCOLS,), U8)
        sh.type_rows = dram("types_tiled", (TCOLS, P))
        sh.w_dram, sh.n_dram = dram("weights_tiled", (P, TCOLS)), dram("norms_tiled", (P, TCOLS))

        build_constants(nc, sh, w["x"], sh.xpad)
        zero_semaphores(nc, sh)
        build_edge_tiles(nc, sh, [w[n] for n in ("src", "dst", "edge_type_32", "edge_weight", "edge_weight1")],
                         fields, sh.type_rows, sh.w_dram, sh.n_dram, win_dram,
                         sh.src_all, sh.rel_all, sh.win_all)
        zero_semaphores(nc, sh)
        with nc.sbuf_tensor("dst_terms", [P, WINDOWS * 3 * WIN], F32) as sh.dst_terms:
            attention_tables(nc, sh, w)
            zero_semaphores(nc, sh)
            attention_edges(nc, sh)
            zero_semaphores(nc, sh)
        with (nc.sbuf_tensor("dst_terms1", [P, NPAD], F32) as sh.dst_terms1,
              nc.sbuf_tensor("src_terms1", [P, NODE_TILES], F32) as sh.src_terms1):
            finish_attention(nc, sh, w)
            zero_semaphores(nc, sh)
            softmax_edges(nc, sh)
            zero_semaphores(nc, sh)
        finish_softmax(nc, sh, w)
        zero_semaphores(nc, sh)
        relation_edges(nc, sh, w)
        zero_semaphores(nc, sh)
        finish_relations(nc, sh, w)
        zero_semaphores(nc, sh)
        convolution_edges(nc, sh)
        zero_semaphores(nc, sh)
        finish_convolution(nc, sh, w, result)


def kernel(**inputs):
    import concourse.bacc as bacc
    from concourse.bass_utils import run_bass_kernel_spmd

    nc = bacc.Bacc("TRN2", target_bir_lowering=False, num_devices=1)
    arrays = {name: np.ascontiguousarray(a) for name, a in inputs.items()}
    arrays["edge_weight1"] = arrays["edge_weight1"].reshape(-1)
    w = {name: nc.dram_tensor(f"in_{name}", a.shape, mybir.dt.from_np(a.dtype), kind="ExternalInput").ap()
         for name, a in arrays.items()}
    result = nc.dram_tensor("out_0", (N, D), F32, kind="ExternalOutput").ap()
    build(nc, w, result)
    r = run_bass_kernel_spmd(nc, [{f"in_{name}": a for name, a in arrays.items()}], core_ids=[0])
    return r.results[0]["out_0"]
```

```python
from contextlib import ExitStack

import numpy as np

import concourse.bass as bass
from concourse import mybir

F32 = mybir.dt.float32
BF16 = mybir.dt.bfloat16
I32 = mybir.dt.int32
U16 = mybir.dt.uint16
U8 = mybir.dt.uint8
ALU = mybir.AluOpType
ACT = mybir.ActivationFunctionType
AX = mybir.AxisListType

P = 128
N = 6250
E = 206250
D = 128
WIN = 32
NODE_TILES = -(-N // P)
NPAD = NODE_TILES * P
WINDOWS = NPAD // WIN
GRP = 4
RING = 4 * GRP
TILES = -(-((E + (P - 1) * WINDOWS) // P) // RING) * RING
GROUPS = TILES // GRP
CHUNKS = -(-TILES // P)
TCOLS = CHUNKS * P
ROW = 1650
ROWS = E // ROW
EPAD = (ROWS + 1) * ROW
PAD_DST = 8192
FAR = 64.0
RELS, BASES = 32, 8
TROW = 132


def bcast_mid(ap, n):
    return ap.unsqueeze(1).to_broadcast([ap.shape[0], n, ap.shape[1]])


def bcast_last(ap, n):
    return ap.unsqueeze(2).to_broadcast([ap.shape[0], ap.shape[1], n])


def build_identity(nc, pool, ident, zeroed, ready):
    pool.memset(ident[:], 0.0).then_inc(zeroed, 1)
    pool.wait_ge(zeroed, 1)
    pool.affine_select(out=ident[:], in_=ident[:], compare_op=ALU.not_equal, fill=1.0, base=0,
                       pattern=[[-1, P]], channel_multiplier=1).then_inc(ready, 1)


def build_edge_tiles(nc, sh, fields_in, fields, types_tiled, weights_dram, norms_dram, win_dram,
                     src_all, rel_all, win_all):
    with ExitStack() as ctx:
        def sb(name, shape, dt=F32):
            return ctx.enter_context(nc.sbuf_tensor(name, shape, dt))

        def sem(name):
            return ctx.enter_context(nc.semaphore(name))

        pad_i = sb("pad_i", [1, ROW], I32)
        pad_z = sb("pad_z", [1, ROW], I32)
        ident = sb("ident_e", [P, P])
        last_i = sb("last_i", [ROWS, 1], I32)
        last_f = sb("last_f", [ROWS, 1])
        thr_row = sb("thr_row", [ROWS, 2 * P + 1])
        below = sb("below", [ROWS, 2 * P + 1])
        ones_col = sb("ones_col", [P, 1])
        ones_sq = sb("ones_sq", [P, P])
        tri = sb("tri", [P, P])
        thr_col = sb("thr_col", [P, 4])
        row_i = sb("row_i", [P, 4], I32)
        row_f = sb("row_f", [P, 4])
        edge_rows = sb("edge_rows", [P, 4, ROW], I32)
        less = sb("less", [P, ROW])
        partial = sb("partial", [P, 4])
        bound = sb("bound", [P, 4])
        count_i = sb("count_i", [P, 2], I32)
        ntile_i = sb("ntile_i", [P, 2], I32)
        ntile = sb("ntile", [P, 2])
        first = sb("first", [P, 2])
        end = sb("end", [P, 2])
        tile_row = sb("tile_row", [P, TCOLS])
        member = sb("member", [P, 2, TCOLS])
        per_win = sb("per_win", [P, 2, 3])
        tile_col = sb("tile_col", [P, CHUNKS])
        got = sb("got", [P, CHUNKS, 3])
        used_off = sb("used_off", [P, CHUNKS])
        off_f = sb("off_f", [P, CHUNKS])
        off_i = sb("off_i", [P, CHUNKS], I32)
        win32 = sb("win32", [P, CHUNKS])
        win_t = sb("win_t", [CHUNKS, P], U8)
        off_c = sb("off_c", [P, 1], I32)
        raw_i = sb("raw_i", [P, 3, P], I32)
        raw_f = sb("raw_f", [P, 2, P])
        src_f = sb("src_f", [P, P])
        rel_f = sb("rel_f", [P, P])
        type_f = sb("type_f", [P, P])
        w_all = sb("w_all", [P, TCOLS])
        n_all = sb("n_all", [P, TCOLS])
        ps_rows = ctx.enter_context(nc.psum_tensor("ps_rows", [P, 4], F32))
        ps_first = ctx.enter_context(nc.psum_tensor("ps_first", [P, 2], F32))
        ps_got = ctx.enter_context(nc.psum_tensor("ps_got", [P, CHUNKS * 3], F32))
        ps_win = ctx.enter_context(nc.psum_tensor("ps_win", [CHUNKS, P], F32))
        ps_t = ctx.enter_context(nc.psum_tensor("ps_t", [P, 4 * P], F32))

        pads_set, padded, last_in = sem("pads_set"), sem("padded"), sem("last_in")
        const, zeroed, ident_ok = sem("const"), sem("zeroed_e"), sem("ident_e_ok")
        dve_step, rows_mm, rows_in = sem("dve_step"), sem("rows_mm"), sh.rows_in
        below_ok, row_ok, ntile_ok, first_mm = sem("below_ok"), sem("row_ok"), sem("ntile_ok"), sem("first_mm")
        member_ok, got_mm, winf_ok = sem("member_ok"), sem("got_mm"), sem("winf_ok")
        win_tr, win_u8, win_out, win_in = sem("win_tr"), sem("win_u8"), sem("win_out"), sem("win_in")
        off_ok, off_go, fetched = sem("off_ok"), sem("off_go"), sh.fetched
        conv_ok, turned, laid = sem("conv_ok"), sem("turned"), sem("laid")
        types_out, laid_out = sem("types_out"), sem("laid_out")
        block = ctx.enter_context(nc.Block())

        @block.sync
        def _(sp):
            for k, (src, dst) in enumerate(zip(fields_in, fields)):
                sp.dma_start(dst[0:E].rearrange("(a b) -> a b", a=330),
                             src.rearrange("(a b) -> a b", a=330)).then_inc(padded, 16)
            sp.wait_ge(pads_set, 2)
            for k, dst in enumerate(fields):
                fill = pad_i if k == 1 else pad_z
                fill = fill[:] if dst.dtype == I32 else fill[:].bitcast(F32)
                sp.dma_start(dst[E:EPAD].rearrange("(a b) -> a b", a=1), fill).then_inc(padded, 16)
            sp.dma_start(last_i[:], fields_in[1].rearrange("(a b) -> a b", b=ROW)[:, ROW - 1:ROW],
                         allow_slow_non_contiguous=True).then_inc(last_in, 16)
            sp.wait_ge(win_u8, 1)
            sp.dma_start(win_dram.rearrange("(a b) -> a b", b=P), win_t[:]).then_inc(win_out, 16)
            sp.wait_ge(win_out, 16)
            sp.dma_start(win_all[:], win_dram.rearrange("(a b) -> a b", a=1)).then_inc(win_in, 16)
            with sp.Fori(0, CHUNKS) as c:
                sp.wait_ge(conv_ok, c + 1)
                sp.dma_start(types_tiled[bass.ds(c * P, P), :], type_f[:]).then_inc(types_out, 16)
            sp.wait_ge(laid, CHUNKS)
            sp.dma_start(weights_dram, w_all[:]).then_inc(laid_out, 16)
            sp.dma_start(norms_dram, n_all[:]).then_inc(laid_out, 16)
            sp.wait_ge(laid_out, 32)
            sp.wait_ge(types_out, 16 * CHUNKS)
            sp.wait_ge(win_in, 16)

        @block.gpsimd
        def _(pool):
            build_identity(nc, pool, ident, zeroed, ident_ok)
            pool.memset(pad_i[:], PAD_DST).then_inc(pads_set, 1)
            pool.memset(pad_z[:], 0).then_inc(pads_set, 1)
            pool.memset(ones_col[:], 1.0)
            pool.memset(ones_sq[:], 1.0).then_inc(zeroed, 1)
            pool.iota(thr_row[:], pattern=[[WIN, 2 * P + 1]], base=0, channel_multiplier=0,
                      allow_small_or_imprecise_dtypes=True)
            for c in range(2):
                for s in range(2):
                    pool.iota(thr_col[:, 2 * c + s:2 * c + s + 1], pattern=[[1, 1]],
                              base=WIN * (P * c + s), channel_multiplier=WIN,
                              allow_small_or_imprecise_dtypes=True)
            pool.iota(tile_row[:], pattern=[[1, TCOLS]], base=0, channel_multiplier=0,
                      allow_small_or_imprecise_dtypes=True)
            pool.iota(tile_col[:], pattern=[[P, CHUNKS]], base=0, channel_multiplier=1,
                      allow_small_or_imprecise_dtypes=True)
            for c in range(2):
                pool.iota(per_win[:, c, 1:2], pattern=[[1, 1]], base=P * c, channel_multiplier=1,
                          allow_small_or_imprecise_dtypes=True)
                pool.memset(per_win[:, c, 2:3], 1.0)
            pool.wait_ge(zeroed, 2)
            pool.affine_select(out=tri[:], in_=ones_sq[:], compare_op=ALU.is_gt, fill=0.0, base=0,
                               pattern=[[1, P]], channel_multiplier=-1).then_inc(const, 1)
            pool.wait_ge(padded, 160)
            pool.wait_ge(row_ok, 1)
            for k in range(4):
                pool.indirect_dma_start(
                    out=edge_rows[:, k, :], out_offset=None,
                    in_=fields[1].rearrange("(a b) -> a b", b=ROW),
                    in_offset=bass.IndirectOffsetOnAxis(ap=row_i[:, k:k + 1], axis=0),
                ).then_inc(rows_in, 16)
            pool.wait_ge(rows_in, 64)
            with pool.Fori(0, CHUNKS) as c:
                pool.wait_ge(off_ok, c + 1)
                pool.sem_inc(off_go, 1)
                for k, field in enumerate(fields):
                    to = raw_i[:, k, :] if k < 3 else raw_f[:, k - 3, :]
                    pool.indirect_dma_start(
                        out=to, out_offset=None, in_=field.rearrange("(a b) -> a b", b=1),
                        in_offset=bass.IndirectOffsetOnAxis(ap=off_c[:, 0:1], axis=0),
                    ).then_inc(fetched[k], 16)

        @block.tensor
        def _(pe):
            pe.wait_ge(ident_ok, 1)
            pe.wait_ge(const, 1)
            pe.wait_ge(below_ok, 1)
            for c in range(2):
                for s in range(2):
                    mm = pe.matmul(ps_rows[:, 2 * c + s:2 * c + s + 1],
                                   below[:, P * c + s:P * c + s + P], ones_col[0:ROWS, :],
                                   start=True, stop=True)
            mm.then_inc(rows_mm, 1)
            pe.wait_ge(ntile_ok, 1)
            pe.matmul(ps_first[:, 0:1], tri[:], ntile[:, 0:1], start=True, stop=True)
            pe.matmul(ps_first[:, 1:2], tri[:], ntile[:, 1:2], start=True, stop=False)
            pe.matmul(ps_first[:, 1:2], ones_sq[:], ntile[:, 0:1], start=False,
                      stop=True).then_inc(first_mm, 1)
            pe.wait_ge(member_ok, 1)
            for k in range(CHUNKS):
                for c in range(2):
                    mm = pe.matmul(ps_got[:, 3 * k:3 * k + 3], member[:, c, P * k:P * k + P],
                                   per_win[:, c, :], start=c == 0, stop=c == 1)
            mm.then_inc(got_mm, 1)
            pe.wait_ge(winf_ok, 1)
            pe.transpose(ps_win[:], used_off[:], ident[:]).then_inc(win_tr, 1)
            with pe.Fori(0, CHUNKS) as c:
                pe.wait_ge(fetched[3], 16 * c + 16)
                pe.wait_ge(fetched[4], 16 * c + 16)
                pe.wait_ge(conv_ok, c + 1)
                pe.wait_ge(laid, c)
                pe.transpose(ps_t[:, 0:P], src_f[:], ident[:])
                pe.transpose(ps_t[:, P:2 * P], rel_f[:], ident[:])
                pe.transpose(ps_t[:, 2 * P:3 * P], raw_f[:, 0, :], ident[:])
                pe.transpose(ps_t[:, 3 * P:4 * P], raw_f[:, 1, :], ident[:]).then_inc(turned, 1)

        @block.vector
        def _(v):
            step = [0]

            def then(ins):
                step[0] += 1
                ins.then_inc(dve_step, 1)
                v.wait_ge(dve_step, step[0])

            v.wait_ge(last_in, 16)
            v.wait_ge(const, 1)
            then(v.tensor_copy(last_f[:], last_i[:]))
            v.tensor_scalar(below[:], thr_row[:], last_f[:, 0:1], None,
                            op0=ALU.is_gt).then_inc(below_ok, 1)
            v.wait_ge(rows_mm, 1)
            v.tensor_copy(row_i[:], ps_rows[:]).then_inc(row_ok, 1)
            then(v.tensor_copy(row_f[:], ps_rows[:]))
            v.wait_ge(rows_in, 64)
            for k in range(4):
                then(v.tensor_scalar(less[:], edge_rows[:, k, :], thr_col[:, k:k + 1], 0.0,
                                     op0=ALU.is_lt, op1=ALU.add, accum_out=partial[:, k:k + 1]))
            then(v.scalar_tensor_tensor(out=bound[:], in0=row_f[:], scalar=float(ROW),
                                        in1=partial[:], op0=ALU.mult, op1=ALU.add))
            b = bound[:].rearrange("p (c s) -> p c s", s=2)
            then(v.scalar_tensor_tensor(out=count_i[:], in0=b[:, :, 1], scalar=float(P - 1),
                                        in1=b[:, :, 0], op0=ALU.add, op1=ALU.subtract))
            then(v.tensor_scalar(ntile_i[:], count_i[:], 7, None, op0=ALU.arith_shift_right))
            then(v.tensor_copy(ntile[:], ntile_i[:]))
            v.sem_inc(ntile_ok, 1)
            v.wait_ge(first_mm, 1)
            then(v.tensor_copy(first[:], ps_first[:]))
            then(v.tensor_tensor(end[:], first[:], ntile[:], ALU.add))
            v.scalar_tensor_tensor(out=per_win[:, :, 0], in0=first[:], scalar=-float(P),
                                   in1=b[:, :, 0], op0=ALU.mult, op1=ALU.add)
            for c in range(2):
                then(v.tensor_scalar(member[:, c, :], tile_row[:], first[:, c:c + 1], None,
                                     op0=ALU.is_ge))
                then(v.scalar_tensor_tensor(out=member[:, c, :], in0=tile_row[:],
                                            scalar=end[:, c:c + 1], in1=member[:, c, :],
                                            op0=ALU.is_lt, op1=ALU.mult))
            v.sem_inc(member_ok, 1)
            v.wait_ge(got_mm, 1)
            then(v.tensor_copy(got[:].rearrange("p a b -> p (a b)"), ps_got[:]))
            then(v.tensor_scalar(used_off[:], tile_col[:], float(P), -float(E), op0=ALU.mult,
                                 op1=ALU.add))
            then(v.tensor_tensor(used_off[:], used_off[:], got[:, :, 2], ALU.mult))
            then(v.scalar_tensor_tensor(out=off_f[:], in0=used_off[:], scalar=float(E),
                                        in1=got[:, :, 0], op0=ALU.add, op1=ALU.add))
            then(v.tensor_copy(off_i[:], off_f[:]))
            then(v.tensor_scalar(win32[:], got[:, :, 1], float(WIN), None, op0=ALU.mult))
            then(v.tensor_copy(used_off[:], got[:, :, 1]))
            v.sem_inc(winf_ok, 1)
            v.wait_ge(win_tr, 1)
            v.tensor_copy(win_t[:], ps_win[:]).then_inc(win_u8, 1)
            base = step[0]
            with v.Fori(0, CHUNKS) as c:
                for k in range(5):
                    v.wait_ge(fetched[k], 16 * c)
                v.wait_ge(types_out, 16 * c)
                v.tensor_copy(off_c[:], off_i[:, bass.ds(c, 1)]).then_inc(off_ok, 1)
                for k in range(3):
                    v.wait_ge(fetched[k], 16 * c + 16)
                v.tensor_copy(src_f[:], raw_i[:, 0, :])
                v.tensor_copy(type_f[:], raw_i[:, 2, :])
                v.tensor_scalar(rel_f[:], raw_i[:, 1, :], win32[:, bass.ds(c, 1)], None,
                                op0=ALU.subtract).then_inc(dve_step, 1)
                v.wait_ge(dve_step, base + c + 1)
                v.tensor_scalar(rel_f[:], rel_f[:], FAR, None, op0=ALU.min).then_inc(conv_ok, 1)
                v.wait_ge(turned, c + 1)
                v.tensor_copy(src_all[:, bass.ds(c * P, P)], ps_t[:, 0:P])
                v.tensor_copy(rel_all[:, bass.ds(c * P, P)], ps_t[:, P:2 * P])
                v.tensor_copy(w_all[:, bass.ds(c * P, P)], ps_t[:, 2 * P:3 * P])
                v.tensor_copy(n_all[:, bass.ds(c * P, P)], ps_t[:, 3 * P:4 * P]).then_inc(laid, 1)


BT = 7
BATCHES = NODE_TILES // BT
BN = BT * P
BW = BN // WIN
HALVES = ((0, 512), (512, BN))
AROW = D + 1
LN_EPS = 1e-5
SEM_END = 256


def at_least(eng, sem, value):
    if not isinstance(value, int) or value > 0:
        eng.wait_ge(sem, value)


def upto(eng, i, c):
    return c if isinstance(i, int) else eng.to_reg(i * 4 + c)


def on(ins, sem, value):
    if not isinstance(value, int) or value > 0:
        ins.wait_op(sem, value, "sem-ge")
    return ins


def row_of(vec, parts=P):
    return vec.rearrange("(a b) -> a b", a=1).to_broadcast([parts, vec.shape[0]])


class Shared:
    pass


def scope(nc, ctx):
    def sb(name, shape, dt=F32):
        return ctx.enter_context(nc.sbuf_tensor(name, shape, dt))

    def ps(name, shape, dt=F32):
        return ctx.enter_context(nc.psum_tensor(name, shape, dt))

    def sem(name):
        return ctx.enter_context(nc.semaphore(name))

    return sb, ps, sem


def zero_semaphores(nc, sh):
    with nc.Block() as block:
        @block.gpsimd
        def _(pool):
            pool.sem_clear(range(sh.first_sem, SEM_END))


def build_constants(nc, sh, x, xpad):
    with ExitStack() as ctx:
        sb, ps, sem = scope(nc, ctx)
        zero_rows = sb("zero_rows", [NPAD - N, D])
        zeroed, ident_ok, iota_ok = sem("zeroed"), sem("ident_ok"), sem("iota_ok")
        placed, copied = sem("placed"), sem("copied")
        block = ctx.enter_context(nc.Block())

        @block.gpsimd
        def _(pool):
            build_identity(nc, pool, sh.ident, zeroed, ident_ok)
            pool.iota(sh.iota[:], pattern=[[1, WIN]], base=0, channel_multiplier=0,
                      allow_small_or_imprecise_dtypes=True)
            pool.memset(sh.ones[:], 1.0)
            pool.memset(sh.eps[:], LN_EPS)
            pool.memset(zero_rows[:], 0.0).then_inc(zeroed, 1)

        @block.vector
        def _(v):
            v.memset(sh.place[:], 0.0).then_inc(placed, 1)
            v.wait_ge(placed, 1)
            v.wait_ge(ident_ok, 1)
            for k in range(4):
                for q in range(4):
                    rows = slice(WIN * k, WIN * k + WIN)
                    v.tensor_copy(sh.place[rows, q, WIN * q:WIN * q + WIN], sh.ident[rows, rows])

        @block.sync
        def _(sp):
            sp.dma_start(xpad[0:N, :], x).then_inc(copied, 16)
            sp.wait_ge(zeroed, 2)
            sp.dma_start(xpad[N:NPAD, :], zero_rows[:]).then_inc(copied, 16)
            sp.wait_ge(copied, 32)


def batch_rows(dram, i):
    return dram[bass.ds(i * BN, BN), :].rearrange("(j p) f -> p j f", p=P)


def attention_tables(nc, sh, w):
    with ExitStack() as ctx:
        sb, ps, sem = scope(nc, ctx)
        at = [0]

        def carve(width, parts=P):
            view = sh.acc[0:parts, at[0]:at[0] + width]
            at[0] += width
            return view

        x_rows = carve(BN).rearrange("p (j f) -> p j f", f=D)
        xT, m1, m2 = carve(BN), carve(BN), carve(BN)
        biased = carve(BN).rearrange("p (j f) -> p j f", f=D)
        table = carve(BT * TROW).rearrange("p (j f) -> p j f", f=TROW)
        wm = carve(3 * D).rearrange("p (k f) -> p k f", f=D)
        b_col = carve(2)
        b3_row = carve(D)
        w_att = carve(6).rearrange("p (s k) -> p s k", s=2)
        b_att = carve(3)
        w_dst = carve(3 * P).rearrange("p (k f) -> p k f", f=P)
        psA, psB, psC, psD = (ps(f"ps{c}", [P, 1024]) for c in "ABCD")
        params, dst_rep, ones_in, x_in = sem("params"), sem("dst_rep"), sem("ones_in"), sem("x_in")
        x_T, x_Tsb, h1, h1sb, h2, h2sb = (sem(n) for n in ("x_T", "x_Tsb", "h1", "h1sb", "h2", "h2sb"))
        h3, dst, dst_sb, biased_ok, feat_ok, src_ok, stored = (
            sem(n) for n in ("h3", "dst", "dst_sb", "biased_ok", "feat_ok", "src_ok", "stored"))
        block = ctx.enter_context(nc.Block())

        @block.sync
        def _(sp):
            for k in range(3):
                sp.dma_start(wm[:, k, :], w[f"L0_gnn_W_msg_{k + 1}"]).then_inc(params, 16)
                for s in range(2):
                    sp.dma_start(w_att[:, s, k:k + 1],
                                 w[f"L0_gnn_W_att_{k + 1}"][s * D:(s + 1) * D, :]).then_inc(params, 16)
                sp.dma_start(b_att[:, k:k + 1], row_of(w[f"L0_gnn_b_att_{k + 1}"])).then_inc(params, 16)
            for k in range(2):
                sp.dma_start(b_col[:, k:k + 1], w[f"L0_gnn_b_msg_{k + 1}"].rearrange("(a b) -> a b", b=1)
                             ).then_inc(params, 16)
            sp.dma_start(b3_row, row_of(w["L0_gnn_b_msg_3"])).then_inc(params, 16)
            with sp.Fori(0, BATCHES) as i:
                sp.wait_ge(x_T, i)
                sp.dma_start(x_rows, batch_rows(sh.xpad, i)).then_inc(x_in, 16)
                sp.wait_ge(feat_ok, i + 1)
                sp.wait_ge(src_ok, i + 1)
                sp.dma_start(batch_rows(sh.table, i), table).then_inc(stored, 16)
            sp.wait_ge(stored, 16 * BATCHES)

        @block.tensor
        def _(pe):
            pe.wait_ge(params, 15 * 16)
            pe.wait_ge(dst_rep, 1)
            with pe.Fori(0, BATCHES) as i:
                pe.wait_ge(x_in, 16 * i + 16)
                pe.wait_ge(dst_sb, 3 * i)
                for j in range(BT):
                    mm = pe.transpose(psA[:, P * j:P * j + P], x_rows[:, j, :], sh.ident[:])
                mm.then_inc(x_T, 1)
                for src_ok_, lhs, rhs, out, done in ((x_Tsb, wm[:, 0, :], xT, psB, h1),
                                                     (h1sb, wm[:, 1, :], m1, psC, h2)):
                    pe.wait_ge(src_ok_, i + 1)
                    for a, b in HALVES:
                        mm = pe.matmul(out[:, a:b], lhs, rhs[:, a:b], start=True, stop=True)
                    mm.then_inc(done, 1)
                for k, (out, free) in enumerate(((psA, x_Tsb), (psB, h1sb), (psC, h2sb))):
                    pe.wait_ge(free, i + 1)
                    for a, b in HALVES:
                        mm = pe.matmul(out[:, a:b], w_dst[:, k, :], xT[:, a:b], start=True, stop=True)
                    mm.then_inc(dst, 1)
                pe.wait_ge(biased_ok, i)
                pe.wait_ge(src_ok, i)
                for j in range(BT):
                    pe.matmul(psD[:, P * j:P * j + P], m2[:, P * j:P * j + P], wm[:, 2, :],
                              start=True, stop=True)
                for j in range(BT):
                    mm = pe.matmul(psD[:, BN + 3 * j:BN + 3 * j + 3], xT[:, P * j:P * j + P],
                                   w_att[:, 0, :], start=True, stop=True)
                mm.then_inc(h3, 1)

        @block.scalar
        def _(act):
            act.wait_ge(params, 15 * 16)
            with act.Fori(0, BATCHES) as i:
                act.wait_ge(h1, i + 1)
                act.activation(m1, psB[:, 0:BN], ACT.Relu, bias=b_col[:, 0:1]).then_inc(h1sb, 1)
                act.wait_ge(h2, i + 1)
                act.activation(m2, psC[:, 0:BN], ACT.Relu, bias=b_col[:, 1:2]).then_inc(h2sb, 1)
                for k, out in enumerate((psA, psB, psC)):
                    act.wait_ge(dst, 3 * i + k + 1)
                    to = sh.dst_terms[:, bass.ds(i * BW * 3 * WIN, BW * 3 * WIN)].rearrange(
                        "p (w k d) -> p w k d", k=3, d=WIN)[:, :, k, :]
                    act.copy(to, out[:, 0:BN].rearrange("p (w d) -> p w d", d=WIN)).then_inc(dst_sb, 1)
                act.wait_ge(biased_ok, i + 1)
                act.wait_ge(stored, 16 * i)
                act.activation(table[:, :, 0:D], biased, ACT.Relu).then_inc(feat_ok, 1)

        @block.vector
        def _(v):
            v.wait_ge(params, 15 * 16)
            v.tensor_copy(w_dst, bcast_last(w_att[:, 1, :], P)).then_inc(dst_rep, 1)
            v.memset(table[:, :, D:D + 1], 1.0)
            with v.Fori(0, BATCHES) as i:
                v.wait_ge(x_T, i + 1)
                v.wait_ge(h3, i)
                v.tensor_copy(xT, psA[:, 0:BN]).then_inc(x_Tsb, 1)
                v.wait_ge(h3, i + 1)
                v.wait_ge(feat_ok, i)
                v.tensor_tensor(biased, psD[:, 0:BN].rearrange("p (j f) -> p j f", f=D),
                                bcast_mid(b3_row, BT), ALU.add).then_inc(biased_ok, 1)
                v.wait_ge(stored, 16 * i)
                v.tensor_tensor(table[:, :, D + 1:D + 4],
                                psD[:, BN:BN + 3 * BT].rearrange("p (j k) -> p j k", k=3),
                                bcast_mid(b_att, BT), ALU.add).then_inc(src_ok, 1)


def window_slice(table, window, width, count=1):
    cols = table[:, bass.ds(window * width, width * count)]
    return cols if count == 1 else cols.rearrange("p (w c) -> p w c", c=width)


class TileWindows:

    def __init__(self, v, sh, name):
        self.v, self.sh = v, sh
        self.regs = [v.alloc_register(f"{name}_window{t}") for t in range(RING)]

    def load(self, i, q):
        first, last = {0: (0, RING - GRP), 3: (RING - GRP, RING)}.get(q, (0, 0))
        if last:
            self.v.load(self.regs[first:last],
                        self.sh.win_all[0:1, bass.ds(i * RING + first, last - first)])

    def load_all(self, i):
        self.v.load(self.regs, self.sh.win_all[0:1, bass.ds(i * RING, RING)])

    def of(self, q):
        return [self.v.snap(r, min_val=0, max_val=WINDOWS - 1)
                for r in self.regs[GRP * q:GRP * q + GRP]]


def gather_rows(pool, table, rows, index_ready, granted, sh, n, q):
    pool.wait_ge(index_ready, n + 1)
    pool.sem_inc(granted, 1)
    for u in range(GRP):
        slot = GRP * q + u
        pool.indirect_dma_start(
            out=rows[:, slot, :], out_offset=None, in_=table[:, :],
            in_offset=bass.IndirectOffsetOnAxis(ap=sh.index[:, slot:slot + 1], axis=0),
        ).then_inc(sh.gathered[q], 16)


def gathered_count(layer, i):
    return i * (16 * GRP) + (layer * (GROUPS // 4) + 1) * 16 * GRP


def add_up(v, sh, windows, out, summed, added, i, q, rows=P, width=AROW):
    into = windows.of((q - 1) % 4)
    done, before = upto(v, i, q), upto(v, i, q - 1)
    for u, window in enumerate(into):
        to = window_slice(sh.acc, window, AROW)[0:rows, 0:width]
        if u == 0:
            at_least(v, added[GRP - 1], before)
        ins = v.tensor_tensor(to, to, out[0:rows, (q - 1) % 2, u, 0:width], ALU.add)
        if u == 0:
            on(ins, summed, done)
        else:
            on(ins, added[u - 1], done)
        ins.then_inc(added[u], 1)
        yield


def stage_indices(act, sh, index_ready, summed, n, q):
    at_least(act, summed, n - 3)
    act.copy(sh.index[:, GRP * q:GRP * q + GRP],
             sh.src_all[:, bass.ds(n * GRP, GRP)]).then_inc(index_ready, 1)


def attention_edges(nc, sh):
    with ExitStack() as ctx:
        sb, ps, sem = scope(nc, ctx)
        rows = sb("rows0", [P, RING, TROW])
        S = sb("S0", [P, 2, GRP, 4, WIN])
        picked = sb("picked", [P, GRP, 3, WIN])
        dst_term = sb("dst_term", [P, GRP, 3])
        z = sb("z0", [P, 2, GRP, 3])
        zr = sb("zr0", [P, 2, GRP, 3])
        a = sb("a0", [P, 2, GRP, 3])
        out = ps("out0", [P, 2, GRP, 256])
        index_ready, granted = sem("index_ready"), sem("granted")
        hot_ok, picked_ok, term_ok = sem("hot_ok"), sem("picked_ok"), sem("term_ok")
        z_ready, relu_ok, a_ready = sem("z_ready"), sem("relu_ok"), sem("a_ready")
        s_ready, summed, zeroed = sem("s_ready"), sem("summed"), sem("zeroed")
        added = [sem(f"added{u}") for u in range(GRP)]
        block = ctx.enter_context(nc.Block())

        @block.gpsimd
        def _(pool):
            with pool.Fori(0, GROUPS // 4) as i:
                for q in range(4):
                    gather_rows(pool, sh.table, rows, index_ready, granted, sh, i * 4 + q, q)

        @block.scalar
        def _(act):
            def step(i, q):
                n = i * 4 + q
                stage_indices(act, sh, index_ready, summed, n + 2, (q + 2) % 4)
                act.wait_ge(z_ready, n + 1)
                at_least(act, a_ready, n)
                act.activation(zr[:, q % 2], z[:, q % 2], ACT.Relu).then_inc(relu_ok, 1)
                act.wait_ge(relu_ok, n + 1)
                at_least(act, s_ready, n - 1)
                act.activation(a[:, q % 2], zr[:, q % 2], ACT.Exp).then_inc(a_ready, 1)

            for q in range(2):
                stage_indices(act, sh, index_ready, summed, q, q)
            for q in range(4):
                step(0, q)
            with act.Fori(1, GROUPS // 4) as i:
                for q in range(4):
                    step(i, q)

        @block.tensor
        def _(pe):
            def step(i, q):
                n = i * 4 + q
                pe.wait_ge(s_ready, n + 1)
                at_least(pe, added[GRP - 1], n - 1)
                for u in range(GRP):
                    mm = pe.matmul(out[:, q % 2, u, 0:AROW],
                                   S[:, q % 2, u].rearrange("p k d -> p (k d)"),
                                   rows[:, GRP * q + u, 0:AROW], start=True, stop=True)
                mm.then_inc(summed, 1)

            for q in range(4):
                step(0, q)
            with pe.Fori(1, GROUPS // 4) as i:
                for q in range(4):
                    step(i, q)

        @block.vector
        def _(v):
            windows = TileWindows(v, sh, "l0")

            def step(i, q, first=False):
                b = q % 2
                one_hot = S[:, b, :, 3, :]
                adds = iter(()) if first else add_up(v, sh, windows, out, summed, added, i, q)
                now, two_ago = upto(v, i, q + 1), upto(v, i, q - 1)
                on(v.tensor_tensor(one_hot, bcast_last(sh.rel_all[:, bass.ds((i * 4 + q) * GRP, GRP)], WIN),
                                   bcast_mid(sh.iota[:], GRP), ALU.is_equal),
                   summed, two_ago).then_inc(hot_ok, 1)
                windows.load(i, q)
                for u, window in enumerate(windows.of(q)):
                    terms = window_slice(sh.dst_terms, window, 3 * WIN)
                    ins = v.tensor_tensor(picked[:, u], terms.rearrange("p (k d) -> p k d", k=3),
                                          bcast_mid(one_hot[:, u, :], 3), ALU.mult)
                    if u == 0:
                        on(ins, hot_ok, now)
                ins.then_inc(picked_ok, 1)
                next(adds, None)
                on(v.tensor_reduce(dst_term[:], picked[:], axis=AX.X, op=ALU.add),
                   picked_ok, now).then_inc(term_ok, 1)
                next(adds, None)
                v.wait_ge(sh.gathered[q], gathered_count(0, i))
                on(v.tensor_tensor(z[:, b], dst_term[:], rows[:, GRP * q:GRP * q + GRP, D + 1:D + 4],
                                   ALU.add), term_ok, now).then_inc(z_ready, 1)
                for _ in adds:
                    pass
                on(v.tensor_tensor(S[:, b, :, 0:3, :],
                                   S[:, b, :, 3:4, :].to_broadcast([P, GRP, 3, WIN]),
                                   a[:, b].unsqueeze(3).to_broadcast([P, GRP, 3, WIN]),
                                   ALU.mult), a_ready, now).then_inc(s_ready, 1)

            v.memset(sh.acc[:], 0.0).then_inc(zeroed, 1)
            v.wait_ge(zeroed, 1)
            for q in range(4):
                step(0, q, first=q == 0)
            with v.Fori(1, GROUPS // 4) as i:
                for q in range(4):
                    step(i, q)
            for _ in add_up(v, sh, windows, out, summed, added, 0, GROUPS):
                pass


class Chain:

    def __init__(self, eng, sem, turn=0, per_turn=0, base=0):
        self.eng, self.sem, self.start, self.per_turn = eng, sem, turn * per_turn + base, per_turn
        self.count = 0

    def then(self, ins):
        self.count += 1
        ins.then_inc(self.sem, 1)
        self.eng.wait_ge(self.sem, self.start + self.count)

    def close(self):
        assert self.count == self.per_turn, self.count


NORM_LINKS = 4


class Norm:

    def __init__(self, sb, sem, name):
        self.stats = sb(f"{name}_stats", [P, BT, 6])
        self.mean_var = sb(f"{name}_mean_var", [P, BT, 2])
        self.std = sb(f"{name}_std", [P, BT])
        self.rstd = sb(f"{name}_rstd", [P, BT])
        self.go = sem(f"{name}_go")
        self.var_ok, self.std_ok = sem(f"{name}_var_ok"), sem(f"{name}_std_ok")

    def vector(self, v, chain, y, turn):
        v.sem_inc(self.go, 1)
        for j in range(BT):
            ins = v.bn_stats(self.stats[:, j, :], y[:, j, :])
        chain.then(ins)
        v.sem_inc(self.go, 1)
        for j in range(BT):
            ins = v.bn_aggr(self.mean_var[:, j, :], self.stats[:, j, :])
        chain.then(ins)
        v.sem_inc(self.var_ok, 1)
        v.wait_ge(self.std_ok, turn + 1)
        chain.then(v.reciprocal(self.rstd[:], self.std[:]))
        for j in range(BT):
            ins = v.tensor_scalar(y[:, j, :], y[:, j, :], self.mean_var[:, j, 0:1],
                                  self.rstd[:, j:j + 1], op0=ALU.subtract, op1=ALU.mult)
        chain.then(ins)

    def scalar(self, act, sh, turn):
        act.wait_ge(self.var_ok, turn + 1)
        act.activation(self.std[:], self.mean_var[:, :, 1], ACT.Sqrt,
                       bias=sh.eps[:, 0:1]).then_inc(self.std_ok, 1)


def tiles_of(buf):
    return buf.rearrange("p (j f) -> p j f", f=D)


def transpose_tiles(pe, out, rows, ident):
    for j in range(BT):
        mm = pe.transpose(out[:, P * j:P * j + P], rows[:, j, :], ident[:])
    return mm


def finish_attention(nc, sh, w):
    with ExitStack() as ctx:
        sb, ps, sem = scope(nc, ctx)
        inv = sb("inv", [P, WINDOWS])
        inv_deg = sb("inv_deg", [P, WINDOWS])
        x_rows, y = tiles_of(sb("x_rows1", [P, BN])[:]), tiles_of(sb("y1", [P, BN])[:])
        xT, hnT, c1, x1T = sb("xT1", [P, BN]), sb("hnT1", [P, BN]), sb("c1", [P, BN]), sb("x1T", [P, BN])
        normed = sb("normed", [3 * WIN, BW, D])
        table = sb("table1", [P, BT, TROW])
        w_c1, w_c2, b_c1, b_c2 = sb("w_c1", [P, 2, D]), sb("w_c2", [P, D]), sb("b_c1", [P, 1]), sb("b_c2", [P, D])
        w_proj, w_projT = sb("w_proj", [P, D]), sb("w_projT", [P, D])
        w_edge = sb("w_edge", [P, 2])
        edge_vec = sb("edge_vec", [P, 2])
        dst_rep = sb("dst_rep1", [P, P])
        norm = Norm(sb, sem, "norm1")
        psA, psB, psC, psD = (ps(f"ps1{c}", [P, 1024]) for c in "ABCD")
        params, setup, wT, wT_sb, rep_ok = sem("params"), sem("setup"), sem("wT"), sem("wT_sb"), sem("rep_ok")
        x_in, x_T, xT_sb, norm_ok, hn, hn_sb = (
            sem(n) for n in ("x_in", "x_T", "xT_sb", "norm_ok", "hn", "hn_sb"))
        c1_mm, c1_sb, c2_mm, x1_ok, x1_T, x1T_sb = (
            sem(n) for n in ("c1_mm", "c1_sb", "c2_mm", "x1_ok", "x1_T", "x1T_sb"))
        h_mm, feat_ok, terms_ok, dst_ok, stored, x1_out, link = (
            sem(n) for n in ("h_mm", "feat_ok", "terms_ok", "dst_ok", "stored", "x1_out", "link"))
        block = ctx.enter_context(nc.Block())
        PARAMS = 7 * 16

        @block.sync
        def _(sp):
            for to, of in ((w_c1[:], w["L0_gnn_W_c1"].rearrange("(s p) f -> p s f", p=P)),
                           (w_c2[:], w["L0_gnn_W_c2"]),
                           (b_c1[:], w["L0_gnn_b_c1"].rearrange("(a b) -> a b", b=1)),
                           (b_c2[:], row_of(w["L0_gnn_b_c2"])),
                           (w_proj[:], w["L1_gnn_W_proj"]),
                           (w_edge[:, 0:1], w["L1_gnn_w_edge"][0:D].rearrange("(a b) -> a b", b=1)),
                           (w_edge[:, 1:2], w["L1_gnn_w_edge"][D:2 * D].rearrange("(a b) -> a b", b=1))):
                sp.dma_start(to, of).then_inc(params, 16)
            with sp.Fori(0, BATCHES) as i:
                sp.wait_ge(x1_ok, i)
                sp.dma_start(x_rows, batch_rows(sh.xpad, i)).then_inc(x_in, 16)
                sp.wait_ge(x1_ok, i + 1)
                sp.dma_start(batch_rows(sh.x1, i), y).then_inc(x1_out, 16)
                sp.wait_ge(feat_ok, i + 1)
                sp.wait_ge(terms_ok, i + 1)
                sp.dma_start(batch_rows(sh.table1, i), table[:]).then_inc(stored, 16)
            sp.wait_ge(stored, 16 * BATCHES)
            sp.wait_ge(x1_out, 16 * BATCHES)

        @block.tensor
        def _(pe):
            pe.wait_ge(params, PARAMS)
            pe.transpose(psA[:, 0:P], w_proj[:], sh.ident[:])
            for s in range(2):
                mm = pe.matmul(psA[:, P + s:P + s + 1], w_proj[:], w_edge[:, s:s + 1], start=True, stop=True)
            mm.then_inc(wT, 1)
            pe.wait_ge(rep_ok, 1)
            with pe.Fori(0, BATCHES) as i:
                pe.wait_ge(x_in, 16 * i + 16)
                pe.wait_ge(x1T_sb, i)
                transpose_tiles(pe, psA, x_rows, sh.ident).then_inc(x_T, 1)
                pe.wait_ge(norm_ok, i + 1)
                pe.wait_ge(feat_ok, i)
                for win in range(BW):
                    mm = pe.matmul(psB[:, WIN * win:WIN * win + WIN], normed[:, win, :],
                                   sh.place[0:3 * WIN, 0, 0:WIN], start=True, stop=True)
                mm.then_inc(hn, 1)
                pe.wait_ge(xT_sb, i + 1)
                pe.wait_ge(hn_sb, i + 1)
                pe.wait_ge(terms_ok, i)
                pe.wait_ge(dst_ok, i)
                for a, b in HALVES:
                    pe.matmul(psC[:, a:b], w_c1[:, 0, :], xT[:, a:b], start=True, stop=False)
                    mm = pe.matmul(psC[:, a:b], w_c1[:, 1, :], hnT[:, a:b], start=False, stop=True)
                mm.then_inc(c1_mm, 1)
                pe.wait_ge(c1_sb, i + 1)
                for j in range(BT):
                    mm = pe.matmul(psD[:, P * j:P * j + P], c1[:, P * j:P * j + P], w_c2[:],
                                   start=True, stop=True)
                mm.then_inc(c2_mm, 1)
                pe.wait_ge(x1_ok, i + 1)
                transpose_tiles(pe, psA, y, sh.ident).then_inc(x1_T, 1)
                pe.wait_ge(x1T_sb, i + 1)
                for a, b in HALVES:
                    pe.matmul(psC[:, a:b], dst_rep[:], x1T[:, a:b], start=True, stop=True)
                for j in range(BT):
                    pe.matmul(psD[:, BN + j:BN + j + 1], x1T[:, P * j:P * j + P], edge_vec[:, 0:1],
                              start=True, stop=True)
                for j in range(BT):
                    mm = pe.matmul(psB[:, P * j:P * j + P], x1T[:, P * j:P * j + P], w_projT[:],
                                   start=True, stop=True)
                mm.then_inc(h_mm, 1)

        @block.scalar
        def _(act):
            act.wait_ge(params, PARAMS)
            with act.Fori(0, BATCHES) as i:
                act.wait_ge(hn, i + 1)
                act.copy(hnT[:], psB[:, 0:BN]).then_inc(hn_sb, 1)
                act.wait_ge(c1_mm, i + 1)
                act.activation(c1[:], psC[:, 0:BN], ACT.Relu, bias=b_c1[:, 0:1]).then_inc(c1_sb, 1)
                norm.scalar(act, sh, i)
                act.wait_ge(h_mm, i + 1)
                act.copy(sh.dst_terms1[:, bass.ds(i * BN, BN)], psC[:, 0:BN]).then_inc(dst_ok, 1)
                act.wait_ge(stored, 16 * i)
                act.copy(table[:, :, 0:D], tiles_of(psB[:, 0:BN])).then_inc(feat_ok, 1)

        @block.vector
        def _(v):
            acc3 = sh.acc[:].rearrange("p (w c) -> p w c", c=AROW)
            v.wait_ge(params, PARAMS)
            v.memset(table[:, :, D:TROW], 1.0)
            once = Chain(v, setup)
            once.then(v.tensor_scalar(inv[:], acc3[:, :, D], 1.0, None, op0=ALU.max))
            once.then(v.reciprocal(inv[:], inv[:]))
            for k in range(3):
                ins = v.tensor_copy(inv_deg[WIN * k:WIN * k + WIN, :], inv[3 * WIN:4 * WIN, :])
            once.then(ins)
            once.then(v.scalar_tensor_tensor(out=inv[0:3 * WIN, :], in0=inv[0:3 * WIN, :],
                                             scalar=1.0 / 3.0, in1=inv_deg[0:3 * WIN, :],
                                             op0=ALU.mult, op1=ALU.mult))
            v.wait_ge(wT, 1)
            v.tensor_copy(w_projT[:], psA[:, 0:P])
            once.then(v.tensor_copy(edge_vec[:], psA[:, P:P + 2]))
            v.tensor_copy(dst_rep[:], edge_vec[:, 1:2].to_broadcast([P, P])).then_inc(rep_ok, 1)
            with v.Fori(0, BATCHES) as i:
                chain = Chain(v, link, i, 2 + NORM_LINKS)
                v.wait_ge(hn, i)
                v.tensor_tensor(normed[:], window_slice(sh.acc, i * BW, AROW, BW)[0:3 * WIN, :, 0:D],
                                bcast_last(inv[0:3 * WIN, bass.ds(i * BW, BW)], D),
                                ALU.mult).then_inc(norm_ok, 1)
                v.wait_ge(x_T, i + 1)
                v.wait_ge(c1_mm, i)
                v.tensor_copy(xT[:], psA[:, 0:BN]).then_inc(xT_sb, 1)
                v.wait_ge(c2_mm, i + 1)
                v.wait_ge(x1_out, 16 * i)
                v.wait_ge(x1_T, i)
                chain.then(v.tensor_tensor(y, tiles_of(psD[:, 0:BN]), bcast_mid(b_c2[:], BT), ALU.add))
                v.wait_ge(x_in, 16 * i + 16)
                chain.then(v.tensor_tensor(y, y, x_rows, ALU.add))
                norm.vector(v, chain, y, i)
                v.sem_inc(x1_ok, 1)
                v.wait_ge(x1_T, i + 1)
                v.wait_ge(h_mm, i)
                v.tensor_copy(x1T[:], psA[:, 0:BN]).then_inc(x1T_sb, 1)
                v.wait_ge(h_mm, i + 1)
                v.wait_ge(stored, 16 * i)
                v.tensor_copy(sh.src_terms1[:, bass.ds(i * BT, BT)], psD[:, BN:BN + BT])
                v.tensor_copy(table[:, :, D + 1], psD[:, BN:BN + BT]).then_inc(terms_ok, 1)
                chain.close()


SHIFT_MARGIN = 45.0
SLOPE = 0.2
NO_EDGE = -1.0e30


def softmax_edges(nc, sh):
    with ExitStack() as ctx:
        sb, ps, sem = scope(nc, ctx)
        rows = sb("rows1", [P, RING, TROW])
        one_hots = sb("one_hot1", [P, 2, GRP, WIN])
        S = sb("S1", [P, 2, GRP, 2, WIN])
        picked = sb("picked1", [P, GRP, WIN])
        dst_term = sb("dst_term1", [P, GRP])
        z_all = sb("z_all1", [P, TILES])
        far = sb("far1", [P, TILES])
        leaky = sb("leaky1", [P, 2, GRP])
        a = sb("a1", [P, 2, GRP])
        w_all = sb("w_all1", [P, TCOLS])
        top = sb("top1", [P, 2])
        top_src = sb("top_src", [P, 1])
        out = ps("out1", [P, 2, GRP, 256])
        index_ready, granted = sem("index_ready"), sem("granted")
        w_in, top_ok, top_all, shift_link = sem("w_in"), sem("top_ok"), sem("top_all"), sem("shift_link")
        hot_ok, picked_ok, term_ok, z_ok = sem("hot_ok"), sem("picked_ok"), sem("term_ok"), sem("z_ok")
        z_ready, a_ready, s_ready, ws_ok = sem("z_ready"), sem("a_ready"), sem("s_ready"), sem("ws_ok")
        summed, zeroed, far_link = sem("summed"), sem("zeroed"), sem("far_link")
        added = [sem(f"added{u}") for u in range(GRP)]
        block = ctx.enter_context(nc.Block())

        @block.sync
        def _(sp):
            sp.dma_start(w_all[:], sh.w_dram).then_inc(w_in, 16)
            sp.wait_ge(w_in, 16)

        @block.gpsimd
        def _(pool):
            pool.wait_ge(top_ok, 1)
            pool.partition_all_reduce(top_src[:], top[:, 0:1], P, bass.bass_isa.ReduceOp.max
                                      ).then_inc(top_all, 1)
            with pool.Fori(0, GROUPS // 4) as i:
                for q in range(4):
                    gather_rows(pool, sh.table1, rows, index_ready, granted, sh, i * 4 + q, q)

        @block.scalar
        def _(act):
            def step(i, q):
                n = i * 4 + q
                stage_indices(act, sh, index_ready, summed, n + 2, (q + 2) % 4)
                act.wait_ge(z_ready, n + 1)
                at_least(act, s_ready, n - 1)
                act.activation(a[:, q % 2], leaky[:, q % 2], ACT.Exp,
                               bias=sh.minus_shift[:, 0:1]).then_inc(a_ready, 1)

            for q in range(2):
                stage_indices(act, sh, index_ready, summed, q, q)
            for q in range(4):
                step(0, q)
            with act.Fori(1, GROUPS // 4) as i:
                for q in range(4):
                    step(i, q)

        @block.tensor
        def _(pe):
            def step(i, q):
                n = i * 4 + q
                pe.wait_ge(s_ready, n + 1)
                pe.wait_ge(ws_ok, n + 1)
                at_least(pe, added[GRP - 1], n - 1)
                for u in range(GRP):
                    mm = pe.matmul(out[0:2 * WIN, q % 2, u, 0:AROW],
                                   S[:, q % 2, u].rearrange("p k d -> p (k d)"),
                                   rows[:, GRP * q + u, 0:AROW], start=True, stop=True)
                mm.then_inc(summed, 1)

            for q in range(4):
                step(0, q)
            with pe.Fori(1, GROUPS // 4) as i:
                for q in range(4):
                    step(i, q)

        @block.vector
        def _(v):
            windows = TileWindows(v, sh, "l1")

            def step(i, q, first=False):
                b = q % 2
                tiles = bass.ds((i * 4 + q) * GRP, GRP)
                one_hot = one_hots[:, b]
                adds = iter(()) if first else add_up(v, sh, windows, out, summed, added, i, q, 2 * WIN)
                now, two_ago = upto(v, i, q + 1), upto(v, i, q - 1)
                on(v.tensor_tensor(one_hot, bcast_last(sh.rel_all[:, tiles], WIN),
                                   bcast_mid(sh.iota[:], GRP), ALU.is_equal),
                   summed, two_ago).then_inc(hot_ok, 1)
                windows.load(i, q)
                for u, window in enumerate(windows.of(q)):
                    ins = v.tensor_tensor(picked[:, u], window_slice(sh.dst_terms1, window, WIN),
                                          one_hot[:, u, :], ALU.mult)
                    if u == 0:
                        on(ins, hot_ok, now)
                ins.then_inc(picked_ok, 1)
                v.tensor_tensor(S[:, b, :, 1, :], one_hot, bcast_last(w_all[:, tiles], WIN),
                                ALU.mult).then_inc(ws_ok, 1)
                on(v.tensor_reduce(dst_term[:], picked[:], axis=AX.X, op=ALU.add),
                   picked_ok, now).then_inc(term_ok, 1)
                next(adds, None)
                v.wait_ge(sh.gathered[q], gathered_count(1, i))
                on(v.tensor_tensor(z_all[:, tiles], dst_term[:], rows[:, GRP * q:GRP * q + GRP, D + 1],
                                   ALU.add), term_ok, now).then_inc(z_ok, 1)
                next(adds, None)
                on(v.scalar_tensor_tensor(out=leaky[:, b], in0=z_all[:, tiles], scalar=SLOPE,
                                          in1=z_all[:, tiles], op0=ALU.mult, op1=ALU.max),
                   z_ok, now).then_inc(z_ready, 1)
                for _ in adds:
                    pass
                on(v.tensor_tensor(S[:, b, :, 0, :], one_hot, bcast_last(a[:, b], WIN), ALU.mult),
                   a_ready, now).then_inc(s_ready, 1)

            v.tensor_reduce(top[:, 0:1], sh.src_terms1[:], axis=AX.X, op=ALU.max).then_inc(top_ok, 1)
            v.tensor_reduce(top[:, 1:2], sh.dst_terms1[:], axis=AX.X, op=ALU.max)
            v.memset(sh.acc[0:2 * WIN, :], 0.0).then_inc(zeroed, 1)
            v.wait_ge(zeroed, 1)
            v.wait_ge(top_all, 1)
            once = Chain(v, shift_link)
            once.then(v.tensor_tensor(top[:, 0:1], top_src[:], top[:, 1:2], ALU.add))
            once.then(v.scalar_tensor_tensor(out=top[:, 1:2], in0=top[:, 0:1], scalar=SLOPE,
                                             in1=top[:, 0:1], op0=ALU.mult, op1=ALU.max))
            once.then(v.tensor_scalar(sh.minus_shift[:], top[:, 1:2], -1.0, SHIFT_MARGIN,
                                      op0=ALU.mult, op1=ALU.add))
            v.wait_ge(w_in, 16)
            for q in range(4):
                step(0, q, first=q == 0)
            with v.Fori(1, GROUPS // 4) as i:
                for q in range(4):
                    step(i, q)
            for _ in add_up(v, sh, windows, out, summed, added, 0, GROUPS, 2 * WIN):
                pass
            last = Chain(v, far_link)
            last.then(v.tensor_scalar(far[:], sh.rel_all[:, 0:TILES], float(WIN), NO_EDGE,
                                      op0=ALU.is_ge, op1=ALU.mult))
            last.then(v.tensor_tensor(far[:], far[:], z_all[:], ALU.add))
            v.tensor_reduce(sh.best[:], far[:], axis=AX.X, op=ALU.max)


def place_rows(pe, sh, out, i, width):
    for j in range(BT):
        for q in range(4):
            row = window_slice(sh.acc, i * BW + 4 * j + q, AROW)[0:WIN, 0:width]
            mm = pe.matmul(out[:, j, 0:width], sh.place[0:WIN, q, :], row, start=q == 0, stop=q == 3)
    return mm


def finish_softmax(nc, sh, w):
    with ExitStack() as ctx:
        sb, ps, sem = scope(nc, ctx)
        x_rows, y = tiles_of(sb("x_rows2", [P, BN])[:]), tiles_of(sb("y2", [P, BN])[:])
        act_out = tiles_of(sb("gelu2", [P, BN])[:])
        gamma, beta = sb("gamma2", [P, D]), sb("beta2", [P, D])
        best_all, score, small = sb("best_all", [P, 1]), sb("score2", [P, 1]), sb("small2", [P, 1])
        den, inv = sb("den2", [P, BT]), sb("inv2", [P, BT])
        norm_a, norm_b = Norm(sb, sem, "norm2a"), Norm(sb, sem, "norm2b")
        out = ps("placed2", [P, BT + 1, 256])
        deg = ps("deg2", [P, NODE_TILES])
        params, best_ok, score_ok, small_ok, small_link = (
            sem(n) for n in ("params", "best_ok", "score_ok", "small_ok", "small_link"))
        deg_mm, placed, read, x_in, link, in_gelu, gelu_ok, x2_ok, stored = (
            sem(n) for n in ("deg_mm", "placed", "read", "x_in", "link", "in_gelu", "gelu_ok", "x2_ok", "stored"))
        block = ctx.enter_context(nc.Block())

        @block.sync
        def _(sp):
            sp.dma_start(gamma[:], row_of(w["L1_gnn_ln_gamma"])).then_inc(params, 16)
            sp.dma_start(beta[:], row_of(w["L1_gnn_ln_beta"])).then_inc(params, 16)
            with sp.Fori(0, BATCHES) as i:
                sp.wait_ge(x2_ok, i)
                sp.dma_start(x_rows, batch_rows(sh.x1, i)).then_inc(x_in, 16)
                sp.wait_ge(x2_ok, i + 1)
                sp.dma_start(batch_rows(sh.x2, i), y).then_inc(stored, 16)
            sp.wait_ge(stored, 16 * BATCHES)

        @block.gpsimd
        def _(pool):
            pool.partition_all_reduce(best_all[:], sh.best[:], P, bass.bass_isa.ReduceOp.max
                                      ).then_inc(best_ok, 1)

        @block.tensor
        def _(pe):
            for q in range(4):
                col = sh.acc[WIN:2 * WIN, :].rearrange("p (c q f) -> p c q f", q=4, f=AROW)[:, :, q, D]
                mm = pe.matmul(deg[:], sh.place[WIN:2 * WIN, q, :], col, start=q == 0, stop=q == 3)
            mm.then_inc(deg_mm, 1)
            with pe.Fori(0, BATCHES) as i:
                pe.wait_ge(read, i)
                place_rows(pe, sh, out, i, AROW).then_inc(placed, 1)

        @block.scalar
        def _(act):
            act.wait_ge(score_ok, 1)
            act.activation(small[:], score[:], ACT.Exp, bias=sh.minus_shift[:, 0:1]).then_inc(small_ok, 1)
            with act.Fori(0, BATCHES) as i:
                norm_a.scalar(act, sh, i)
                act.wait_ge(in_gelu, i + 1)
                act.activation(act_out, y, ACT.Gelu).then_inc(gelu_ok, 1)
                norm_b.scalar(act, sh, i)

        @block.vector
        def _(v):
            once = Chain(v, small_link)
            v.wait_ge(best_ok, 1)
            v.scalar_tensor_tensor(out=score[:], in0=best_all[:], scalar=SLOPE, in1=best_all[:],
                                   op0=ALU.mult, op1=ALU.max).then_inc(score_ok, 1)
            v.wait_ge(small_ok, 1)
            once.then(v.tensor_scalar(small[:], small[:], 1e-6, None, op0=ALU.mult))
            v.wait_ge(deg_mm, 1)
            once.then(v.tensor_copy(sh.weight_sum[:], deg[:]))
            v.wait_ge(params, 32)
            with v.Fori(0, BATCHES) as i:
                chain = Chain(v, link, i, 6 + 2 * NORM_LINKS)
                v.wait_ge(placed, i + 1)
                chain.then(v.tensor_scalar(den[:], out[:, 0:BT, D], small[:, 0:1], None, op0=ALU.add))
                chain.then(v.reciprocal(inv[:], den[:]))
                v.wait_ge(x_in, 16 * i + 16)
                v.wait_ge(stored, 16 * i)
                for j in range(BT):
                    ins = v.scalar_tensor_tensor(out=y[:, j, :], in0=out[:, j, 0:D],
                                                 scalar=inv[:, j:j + 1], in1=x_rows[:, j, :],
                                                 op0=ALU.mult, op1=ALU.add)
                chain.then(ins)
                v.sem_inc(read, 1)
                norm_a.vector(v, chain, y, i)
                chain.then(v.tensor_tensor(y, y, bcast_mid(gamma[:], BT), ALU.mult))
                chain.then(v.tensor_tensor(y, y, bcast_mid(beta[:], BT), ALU.add))
                v.sem_inc(in_gelu, 1)
                v.wait_ge(gelu_ok, i + 1)
                chain.then(v.tensor_tensor(y, act_out, x_rows, ALU.add))
                norm_b.vector(v, chain, y, i)
                v.sem_inc(x2_ok, 1)
                chain.close()


def relation_edges(nc, sh, w):
    with ExitStack() as ctx:
        sb, ps, sem = scope(nc, ctx)
        rows = sb("rows2", [P, RING, D])
        one_hot = sb("one_hot2", [P, GRP, WIN])
        S = sb("S2", [P, 2, GRP, BASES, WIN])
        types = sb("types2", [RELS, 4, GRP * P])
        type_hot = sb("type_hot", [RELS, 2, GRP * P])
        rel_id = sb("rel_id", [RELS, 1])
        compT = sb("compT", [RELS, BASES])
        coef = sb("coef", [P, GRP, BASES])
        T = sb("T2", [P, 2, BASES, GRP, WIN])
        w_base = sb("w_base", [P, BASES, D])
        n_all = sb("n_all2", [P, TCOLS])
        per_base = ps("per_base", [P, 2, GRP, BASES * WIN])
        coef_ps = ps("coef_ps", [P, GRP * BASES])
        summed_ps = ps("summed_ps", [P, 2, 512])
        params, rel_ok, setup = sem("params"), sem("rel_ok"), sem("setup")
        index_ready, granted = sem("index_ready"), sem("granted")
        types_in = [sem(f"types_in{s}") for s in range(4)]
        type_ok, coef_mm, coef_ok, s_ready = sem("type_ok"), sem("coef_mm"), sem("coef_ok"), sem("s_ready")
        based, T_ok, summed, zeroed = (sem(n) for n in ("based", "T_ok", "summed", "zeroed"))
        added = [sem(f"added{u}") for u in range(GRP)]
        block = ctx.enter_context(nc.Block())
        PARAMS = 3 * 16

        def load_types(sp, n, q):
            at_least(sp, type_ok, n - 3)
            types_row = sh.type_rows[bass.ds(n * GRP, GRP), :].rearrange("a b -> (a b)")
            sp.dma_start(types[:, q, :], row_of(types_row, RELS)).then_inc(types_in[q], 16)

        @block.sync
        def _(sp):
            sp.dma_start(w_base[:], w["L2_gnn_weight"].rearrange("b d f -> d b f")).then_inc(params, 16)
            sp.dma_start(compT[:], w["L2_gnn_w_comp"]).then_inc(params, 16)
            sp.dma_start(n_all[:], sh.n_dram).then_inc(params, 16)
            for q in range(4):
                load_types(sp, q, q)
            with sp.Fori(1, GROUPS // 4) as i:
                for q in range(4):
                    load_types(sp, i * 4 + q, q)
            load_types(sp, GROUPS, 0)
            sp.wait_ge(params, PARAMS)
            for q in range(4):
                sp.wait_ge(types_in[q], 16 * (GROUPS // 4 + (q == 0)))

        @block.gpsimd
        def _(pool):
            pool.iota(rel_id[:], pattern=[[1, 1]], base=0, channel_multiplier=1,
                      allow_small_or_imprecise_dtypes=True).then_inc(rel_ok, 1)
            with pool.Fori(0, GROUPS // 4) as i:
                for q in range(4):
                    gather_rows(pool, sh.x2, rows, index_ready, granted, sh, i * 4 + q, q)

        @block.scalar
        def _(act):
            def step(i, q):
                n = i * 4 + q
                stage_indices(act, sh, index_ready, based, n + 2, (q + 2) % 4)
                act.wait_ge(based, n + 1)
                at_least(act, summed, n - 1)
                for u in range(GRP):
                    ins = act.copy(T[:, q % 2, :, u, :],
                                   per_base[:, q % 2, u, :].rearrange("p (b d) -> p b d", d=WIN))
                ins.then_inc(T_ok, 1)

            for q in range(2):
                stage_indices(act, sh, index_ready, based, q, q)
            for q in range(4):
                step(0, q)
            with act.Fori(1, GROUPS // 4) as i:
                for q in range(4):
                    step(i, q)

        @block.tensor
        def _(pe):
            def coefficients(n, b):
                pe.wait_ge(type_ok, n + 1)
                at_least(pe, coef_ok, n)
                for u in range(GRP):
                    mm = pe.matmul(coef_ps[:, BASES * u:BASES * u + BASES],
                                   type_hot[:, b, P * u:P * u + P], compT[:], start=True, stop=True)
                mm.then_inc(coef_mm, 1)

            def over_bases(n, b):
                pe.wait_ge(T_ok, n + 1)
                at_least(pe, added[GRP - 1], n - 1)
                for k in range(BASES):
                    mm = pe.matmul(summed_ps[:, b, 0:GRP * WIN], w_base[:, k, :],
                                   T[:, b, k].rearrange("p u d -> p (u d)"),
                                   start=k == 0, stop=k == BASES - 1)
                mm.then_inc(summed, 1)

            def step(i, q, first=False):
                n = i * 4 + q
                b = q % 2
                pe.wait_ge(s_ready, n + 1)
                pe.wait_ge(sh.gathered[q], gathered_count(2, i))
                at_least(pe, T_ok, n - 1)
                for u in range(GRP):
                    mm = pe.matmul(per_base[:, b, u, :], rows[:, GRP * q + u, :],
                                   S[:, b, u].rearrange("p k d -> p (k d)"), start=True, stop=True)
                mm.then_inc(based, 1)
                coefficients(n + 1, 1 - b)
                if not first:
                    over_bases(n - 1, 1 - b)

            pe.wait_ge(params, PARAMS)
            coefficients(0, 0)
            for q in range(4):
                step(0, q, first=q == 0)
            with pe.Fori(1, GROUPS // 4) as i:
                for q in range(4):
                    step(i, q)
            over_bases(GROUPS - 1, 1)

        @block.vector
        def _(v):
            windows = TileWindows(v, sh, "l2")

            def type_one_hot(i, q):
                turn = i + q // 4
                v.wait_ge(types_in[q % 4], turn * 16 + 16)
                on(v.tensor_scalar(type_hot[:, q % 2], types[:, q % 4, :], rel_id[:, 0:1], None,
                                   op0=ALU.is_equal),
                   coef_mm, upto(v, i, q - 1)).then_inc(type_ok, 1)

            def add_up_two_ago(i, q):
                into = windows.of((q - 2) % 4)
                done, before = upto(v, i, q - 1), upto(v, i, q - 2)
                for u, window in enumerate(into):
                    to = window_slice(sh.acc, window, WIN)
                    if u == 0:
                        at_least(v, added[GRP - 1], before)
                    ins = v.tensor_tensor(to, to, summed_ps[:, q % 2, WIN * u:WIN * u + WIN], ALU.add)
                    if u == 0:
                        on(ins, summed, done)
                    else:
                        on(ins, added[u - 1], done)
                    ins.then_inc(added[u], 1)
                    yield

            def step(i, q, lag_ok=True):
                b = q % 2
                tiles = bass.ds((i * 4 + q) * GRP, GRP)
                adds = add_up_two_ago(i, q) if lag_ok else iter(())
                now, before, two_ago = (upto(v, i, q + k) for k in (1, 0, -1))
                on(v.tensor_tensor(one_hot[:], bcast_last(sh.rel_all[:, tiles], WIN),
                                   bcast_mid(sh.iota[:], GRP), ALU.is_equal), s_ready, before)
                on(v.tensor_tensor(coef[:], coef_ps[:].rearrange("p (u k) -> p u k", k=BASES),
                                   bcast_last(n_all[:, tiles], BASES), ALU.mult),
                   coef_mm, now).then_inc(coef_ok, 1)
                at_least(v, based, two_ago)
                on(v.tensor_tensor(S[:, b], one_hot[:].unsqueeze(2).to_broadcast([P, GRP, BASES, WIN]),
                                   coef[:].unsqueeze(3).to_broadcast([P, GRP, BASES, WIN]), ALU.mult),
                   coef_ok, now).then_inc(s_ready, 1)
                type_one_hot(i, q + 1)
                for _ in adds:
                    pass
                if q == 1:
                    windows.load_all(i)

            v.memset(sh.acc[:, 0:NPAD], 0.0).then_inc(zeroed, 1)
            v.wait_ge(zeroed, 1)
            v.wait_ge(rel_ok, 1)
            v.wait_ge(params, PARAMS)
            type_one_hot(0, 0)
            for q in range(4):
                step(0, q, lag_ok=q >= 2)
            with v.Fori(1, GROUPS // 4) as i:
                for q in range(4):
                    step(i, q)
            for q in (GROUPS, GROUPS + 1):
                for _ in add_up_two_ago(0, q):
                    pass


def finish_relations(nc, sh, w):
    with ExitStack() as ctx:
        sb, ps, sem = scope(nc, ctx)
        x_rows, y = tiles_of(sb("x_rows3", [P, BN])[:]), tiles_of(sb("y3", [P, BN])[:])
        xT, sums, x3T = sb("xT3", [P, BN]), sb("sums3", [P, BN]), sb("x3T", [P, BN])
        table = tiles_of(sb("table3", [P, BN])[:])
        w_loop, w3, bias = sb("w_loop", [P, D]), sb("w3", [P, D]), sb("bias3", [P, D])
        deg, above, root = sb("deg3", [P, NODE_TILES]), sb("above3", [P, NODE_TILES]), sb("root3", [P, NODE_TILES])
        norm = Norm(sb, sem, "norm3")
        psA, psB, psC, psD = (ps(f"ps3{c}", [P, 1024]) for c in "ABCD")
        params, setup, deg_ok, root_ok, dinv_ok = (
            sem(n) for n in ("params", "setup", "deg_ok", "root_ok", "dinv_ok"))
        x_in, x_T, xT_sb, sums_ok, mixed, x3_ok, x3_T, x3T_sb, xw, table_ok, stored, x3_out, link = (
            sem(n) for n in ("x_in", "x_T", "xT_sb", "sums_ok", "mixed", "x3_ok", "x3_T", "x3T_sb",
                             "xw", "table_ok", "stored", "x3_out", "link"))
        block = ctx.enter_context(nc.Block())

        @block.sync
        def _(sp):
            sp.dma_start(w_loop[:], w["L2_gnn_loop_weight"]).then_inc(params, 16)
            sp.dma_start(w3[:], w["L3_gnn_W"]).then_inc(params, 16)
            sp.dma_start(bias[:], row_of(w["L2_gnn_h_bias"])).then_inc(params, 16)
            with sp.Fori(0, BATCHES) as i:
                sp.wait_ge(x3_ok, i)
                sp.dma_start(x_rows, batch_rows(sh.x2, i)).then_inc(x_in, 16)
                sp.wait_ge(x3_ok, i + 1)
                sp.dma_start(batch_rows(sh.x3, i), y).then_inc(x3_out, 16)
                sp.wait_ge(table_ok, i + 1)
                sp.dma_start(batch_rows(sh.table3, i), table).then_inc(stored, 16)
            sp.wait_ge(x3_out, 16 * BATCHES)
            sp.wait_ge(stored, 16 * BATCHES)

        @block.tensor
        def _(pe):
            pe.wait_ge(params, 48)
            with pe.Fori(0, BATCHES) as i:
                pe.wait_ge(x_in, 16 * i + 16)
                pe.wait_ge(xT_sb, i)
                transpose_tiles(pe, psA, x_rows, sh.ident).then_inc(x_T, 1)
                pe.wait_ge(xT_sb, i + 1)
                pe.wait_ge(sums_ok, i + 1)
                for j in range(BT):
                    cols = slice(P * j, P * j + P)
                    pe.matmul(psB[:, cols], sums[:, cols], sh.ident[:], start=True, stop=False)
                    mm = pe.matmul(psB[:, cols], xT[:, cols], w_loop[:], start=False, stop=True)
                mm.then_inc(mixed, 1)
                pe.wait_ge(x3_ok, i + 1)
                transpose_tiles(pe, psC, y, sh.ident).then_inc(x3_T, 1)
                pe.wait_ge(x3T_sb, i + 1)
                pe.wait_ge(table_ok, i)
                for j in range(BT):
                    cols = slice(P * j, P * j + P)
                    mm = pe.matmul(psD[:, cols], x3T[:, cols], w3[:], start=True, stop=True)
                mm.then_inc(xw, 1)

        @block.scalar
        def _(act):
            act.wait_ge(deg_ok, 1)
            act.activation(root[:], deg[:], ACT.Sqrt).then_inc(root_ok, 1)
            with act.Fori(0, BATCHES) as i:
                act.wait_ge(mixed, i)
                act.copy(sums[:], sh.acc[:, bass.ds(i * BN, BN)]).then_inc(sums_ok, 1)
                norm.scalar(act, sh, i)
                act.wait_ge(x3_T, i + 1)
                act.wait_ge(xw, i)
                act.copy(x3T[:], psC[:, 0:BN]).then_inc(x3T_sb, 1)

        @block.vector
        def _(v):
            once = Chain(v, setup)
            once.then(v.tensor_scalar(deg[:], sh.weight_sum[:], 1.0, None, op0=ALU.add))
            once.then(v.tensor_scalar(above[:], deg[:], 0.0, None, op0=ALU.is_gt))
            v.tensor_scalar(deg[:], deg[:], 1e-35, None, op0=ALU.max).then_inc(deg_ok, 1)
            v.wait_ge(root_ok, 1)
            once.then(v.reciprocal(root[:], root[:]))
            once.then(v.tensor_tensor(sh.dinv[:], root[:], above[:], ALU.mult))
            v.wait_ge(params, 48)
            with v.Fori(0, BATCHES) as i:
                chain = Chain(v, link, i, 3 + NORM_LINKS)
                v.wait_ge(x_T, i + 1)
                v.wait_ge(mixed, i)
                v.tensor_copy(xT[:], psA[:, 0:BN]).then_inc(xT_sb, 1)
                v.wait_ge(mixed, i + 1)
                v.wait_ge(x3_out, 16 * i)
                v.wait_ge(x3_T, i)
                chain.then(v.tensor_tensor(y, tiles_of(psB[:, 0:BN]), bcast_mid(bias[:], BT), ALU.add))
                chain.then(v.tensor_scalar(y, y, 0.0, None, op0=ALU.max))
                chain.then(v.tensor_tensor(y, y, x_rows, ALU.add))
                norm.vector(v, chain, y, i)
                v.sem_inc(x3_ok, 1)
                v.wait_ge(xw, i + 1)
                v.wait_ge(stored, 16 * i)
                v.tensor_tensor(table, tiles_of(psD[:, 0:BN]),
                                bcast_last(sh.dinv[:, bass.ds(i * BT, BT)], D),
                                ALU.mult).then_inc(table_ok, 1)
                chain.close()


def convolution_edges(nc, sh):
    with ExitStack() as ctx:
        sb, ps, sem = scope(nc, ctx)
        rows = sb("rows3", [P, RING, D])
        one_hot = sb("one_hot3", [P, 2, GRP, WIN])
        S = sb("S3", [P, 2, GRP, WIN])
        w_all = sb("w_all3", [P, TCOLS])
        out = ps("out3", [P, 2, GRP, 256])
        index_ready, granted, w_in = sem("index_ready"), sem("granted"), sem("w_in")
        link, s_ready = sem("link"), sem("s_ready")
        summed, zeroed = sem("summed"), sem("zeroed")
        added = [sem(f"added{u}") for u in range(GRP)]
        block = ctx.enter_context(nc.Block())

        @block.sync
        def _(sp):
            sp.dma_start(w_all[:], sh.w_dram).then_inc(w_in, 16)
            sp.wait_ge(w_in, 16)

        @block.gpsimd
        def _(pool):
            with pool.Fori(0, GROUPS // 4) as i:
                for q in range(4):
                    gather_rows(pool, sh.table3, rows, index_ready, granted, sh, i * 4 + q, q)

        @block.scalar
        def _(act):
            for q in range(4):
                stage_indices(act, sh, index_ready, summed, q, q)
            with act.Fori(1, GROUPS // 4) as i:
                for q in range(4):
                    stage_indices(act, sh, index_ready, summed, i * 4 + q, q)

        @block.tensor
        def _(pe):
            def step(i, q):
                n = i * 4 + q
                pe.wait_ge(s_ready, n + 1)
                at_least(pe, added[GRP - 1], n - 1)
                pe.wait_ge(sh.gathered[q], gathered_count(3, i))
                for u in range(GRP):
                    mm = pe.matmul(out[0:WIN, q % 2, u, 0:D], S[:, q % 2, u, :],
                                   rows[:, GRP * q + u, :], start=True, stop=True)
                mm.then_inc(summed, 1)

            for q in range(4):
                step(0, q)
            with pe.Fori(1, GROUPS // 4) as i:
                for q in range(4):
                    step(i, q)

        @block.vector
        def _(v):
            windows = TileWindows(v, sh, "l3")

            def step(i, q, first=False):
                b = q % 2
                tiles = bass.ds((i * 4 + q) * GRP, GRP)
                now, two_ago = upto(v, i, q + 1), upto(v, i, q - 1)
                on(v.tensor_tensor(one_hot[:, b], bcast_last(sh.rel_all[:, tiles], WIN),
                                   bcast_mid(sh.iota[:], GRP), ALU.is_equal),
                   summed, two_ago).then_inc(link, 1)
                on(v.tensor_tensor(S[:, b], one_hot[:, b], bcast_last(w_all[:, tiles], WIN), ALU.mult),
                   link, now).then_inc(s_ready, 1)
                if not first:
                    for _ in add_up(v, sh, windows, out, summed, added, i, q, WIN, D):
                        pass
                windows.load(i, q)

            v.memset(sh.acc[0:WIN, :], 0.0).then_inc(zeroed, 1)
            v.wait_ge(zeroed, 1)
            v.wait_ge(w_in, 16)
            for q in range(4):
                step(0, q, first=q == 0)
            with v.Fori(1, GROUPS // 4) as i:
                for q in range(4):
                    step(i, q)
            for _ in add_up(v, sh, windows, out, summed, added, 0, GROUPS, WIN, D):
                pass


def finish_convolution(nc, sh, w, result):
    with ExitStack() as ctx:
        sb, ps, sem = scope(nc, ctx)
        own = sb("own4", [P, NODE_TILES, D])
        y = sb("y4", [P, NODE_TILES, D])
        x3 = tiles_of(sb("x34", [P, BN])[:])
        bias, gamma, beta = sb("bias4", [P, D]), sb("gamma4", [P, D]), sb("beta4", [P, D])
        real = sb("real4", [P, 1])
        part, mean, scale = sb("part4", [P, D]), sb("mean4", [P, D]), sb("scale4", [P, D])
        norm = Norm(sb, sem, "norm4")
        out = ps("placed4", [P, BT + 1, 256])
        total = ps("total4", [P, 2, 512])
        params, real_ok, own_in, placed, read, link1, link2, link3 = (
            sem(n) for n in ("params", "real_ok", "own_in", "placed", "read", "link1", "link2", "link3"))
        part_ok, total_ok, root_ok, x_in, done, stored = (
            sem(n) for n in ("part_ok", "total_ok", "root_ok", "x_in", "done", "stored"))
        block = ctx.enter_context(nc.Block())
        FULL = NODE_TILES - 1

        @block.sync
        def _(sp):
            sp.dma_start(own[:], sh.table3.rearrange("(c p) f -> p c f", p=P)).then_inc(own_in, 16)
            sp.dma_start(bias[:], row_of(w["L3_gnn_b"])).then_inc(params, 16)
            sp.dma_start(gamma[:], row_of(w["L3_gnn_gamma"])).then_inc(params, 16)
            sp.dma_start(beta[:], row_of(w["L3_gnn_beta"])).then_inc(params, 16)
            with sp.Fori(0, BATCHES) as i:
                sp.wait_ge(done, i)
                sp.dma_start(x3, batch_rows(sh.x3, i)).then_inc(x_in, 16)
            sp.wait_ge(done, BATCHES)
            sp.dma_start(result[0:FULL * P, :].rearrange("(c p) f -> p c f", p=P),
                         y[:, 0:FULL, :]).then_inc(stored, 16)
            sp.dma_start(result[FULL * P:N, :], y[0:N - FULL * P, FULL, :]).then_inc(stored, 16)
            sp.wait_ge(stored, 32)

        @block.gpsimd
        def _(pool):
            pool.affine_select(out=real[:], in_=sh.ones[:, 0:1], compare_op=ALU.is_gt, fill=0.0,
                               base=N - FULL * P, pattern=[[0, 1]], channel_multiplier=-1
                               ).then_inc(real_ok, 1)

        @block.tensor
        def _(pe):
            with pe.Fori(0, BATCHES) as i:
                pe.wait_ge(read, i)
                place_rows(pe, sh, out, i, D).then_inc(placed, 1)
            for k in range(2):
                pe.wait_ge(part_ok, k + 1)
                pe.matmul(total[:, k, 0:D], sh.ones[:], part[:], start=True, stop=True
                          ).then_inc(total_ok, 1)

        @block.scalar
        def _(act):
            act.wait_ge(part_ok, 3)
            act.activation(scale[:], scale[:], ACT.Sqrt, bias=sh.eps[:, 0:1]).then_inc(root_ok, 1)
            with act.Fori(0, BATCHES) as i:
                norm.scalar(act, sh, i)

        @block.vector
        def _(v):
            by_feature = lambda t: t[:].rearrange("p c f -> p f c")
            v.wait_ge(own_in, 16)
            v.wait_ge(params, 48)
            with v.Fori(0, BATCHES) as i:
                chain = Chain(v, link1, i, 3)
                rows = bass.ds(i * BT, BT)
                v.wait_ge(placed, i + 1)
                chain.then(v.tensor_tensor(y[:, rows, :], out[:, 0:BT, 0:D], own[:, rows, :], ALU.add))
                v.sem_inc(read, 1)
                chain.then(v.tensor_tensor(y[:, rows, :], y[:, rows, :],
                                           bcast_last(sh.dinv[:, rows], D), ALU.mult))
                chain.then(v.tensor_tensor(y[:, rows, :], y[:, rows, :], bcast_mid(bias[:], BT), ALU.add))
                chain.close()
            once = Chain(v, link2)
            v.wait_ge(real_ok, 1)
            once.then(v.tensor_scalar(y[:, FULL, :], y[:, FULL, :], real[:, 0:1], None, op0=ALU.mult))
            v.tensor_reduce(part[:], by_feature(y), axis=AX.X, op=ALU.add).then_inc(part_ok, 1)
            v.wait_ge(total_ok, 1)
            once.then(v.tensor_scalar(mean[:], total[:, 0, 0:D], 1.0 / N, None, op0=ALU.mult))
            once.then(v.tensor_tensor(y[:], y[:], bcast_mid(mean[:], NODE_TILES), ALU.subtract))
            once.then(v.tensor_scalar(y[:, FULL, :], y[:, FULL, :], real[:, 0:1], None, op0=ALU.mult))
            once.then(v.tensor_tensor(own[:], y[:], y[:], ALU.mult))
            v.tensor_reduce(part[:], by_feature(own), axis=AX.X, op=ALU.add).then_inc(part_ok, 1)
            v.wait_ge(total_ok, 2)
            v.tensor_scalar(scale[:], total[:, 1, 0:D], 1.0 / N, None, op0=ALU.mult).then_inc(part_ok, 1)
            v.wait_ge(root_ok, 1)
            once.then(v.reciprocal(scale[:], scale[:]))
            once.then(v.tensor_tensor(scale[:], scale[:], gamma[:], ALU.mult))
            once.then(v.tensor_tensor(y[:], y[:], bcast_mid(scale[:], NODE_TILES), ALU.mult))
            once.then(v.tensor_tensor(y[:], y[:], bcast_mid(beta[:], NODE_TILES), ALU.add))
            once.then(v.tensor_scalar(y[:], y[:], 0.0, None, op0=ALU.max))
            with v.Fori(0, BATCHES) as i:
                chain = Chain(v, link3, i, 1 + NORM_LINKS)
                rows = y[:, bass.ds(i * BT, BT), :]
                v.wait_ge(x_in, 16 * i + 16)
                chain.then(v.tensor_tensor(rows, rows, x3, ALU.add))
                norm.vector(v, chain, rows, i)
                v.sem_inc(done, 1)
                chain.close()





def build(nc, w, result):
    def dram(name, shape, dt=F32):
        return nc.dram_tensor(name, shape, dt, kind="Internal").ap()

    with ExitStack() as ctx:
        sb, _, _ = scope(nc, ctx)
        sh = Shared()
        _, _, sem = scope(nc, ctx)
        sh.rows_in, sh.fetched = sem("rows_in"), [sem(f"fetched{k}") for k in range(5)]
        sh.gathered = [sem(f"gathered{q}") for q in range(4)]
        sh.first_sem = sh.gathered[-1].num + 1
        sh.ident, sh.iota, sh.ones = sb("ident", [P, P]), sb("iota", [P, WIN]), sb("ones", [P, P])
        sh.eps, sh.place = sb("eps", [P, 1]), sb("place", [P, 4, P])
        sh.src_all, sh.rel_all = sb("src_all", [P, TCOLS], U16), sb("rel_all", [P, TCOLS], BF16)
        sh.win_all, sh.index = sb("win_all", [1, TCOLS], U8), sb("index", [P, RING], I32)
        sh.minus_shift, sh.best = sb("minus_shift", [P, 1]), sb("best_edge", [P, 1])
        sh.weight_sum, sh.dinv = sb("weight_sum", [P, NODE_TILES]), sb("dinv", [P, NODE_TILES])
        sh.acc = sb("acc", [P, WINDOWS * AROW])
        sh.xpad, sh.x1, sh.x2, sh.x3 = (dram(n, (NPAD, D)) for n in ("xpad", "x1", "x2", "x3"))
        sh.table, sh.table1 = dram("table0", (NPAD, TROW)), dram("table1_rows", (NPAD, TROW))
        sh.table3 = dram("table3_rows", (NPAD, D))
        fields = [dram(f"edge_{n}", (EPAD,), dt) for n, dt in
                  (("src", I32), ("dst", I32), ("type", I32), ("weight", F32), ("norm", F32))]
        win_dram = dram("win_dram", (TCOLS,), U8)
        sh.type_rows = dram("types_tiled", (TCOLS, P))
        sh.w_dram, sh.n_dram = dram("weights_tiled", (P, TCOLS)), dram("norms_tiled", (P, TCOLS))

        build_constants(nc, sh, w["x"], sh.xpad)
        zero_semaphores(nc, sh)
        build_edge_tiles(nc, sh, [w[n] for n in ("src", "dst", "edge_type_32", "edge_weight", "edge_weight1")],
                         fields, sh.type_rows, sh.w_dram, sh.n_dram, win_dram,
                         sh.src_all, sh.rel_all, sh.win_all)
        zero_semaphores(nc, sh)
        with nc.sbuf_tensor("dst_terms", [P, WINDOWS * 3 * WIN], F32) as sh.dst_terms:
            attention_tables(nc, sh, w)
            zero_semaphores(nc, sh)
            attention_edges(nc, sh)
            zero_semaphores(nc, sh)
        with (nc.sbuf_tensor("dst_terms1", [P, NPAD], F32) as sh.dst_terms1,
              nc.sbuf_tensor("src_terms1", [P, NODE_TILES], F32) as sh.src_terms1):
            finish_attention(nc, sh, w)
            zero_semaphores(nc, sh)
            softmax_edges(nc, sh)
            zero_semaphores(nc, sh)
        finish_softmax(nc, sh, w)
        zero_semaphores(nc, sh)
        relation_edges(nc, sh, w)
        zero_semaphores(nc, sh)
        finish_relations(nc, sh, w)
        zero_semaphores(nc, sh)
        convolution_edges(nc, sh)
        zero_semaphores(nc, sh)
        finish_convolution(nc, sh, w, result)


def kernel(**inputs):
    import concourse.bacc as bacc
    from concourse.bass_utils import run_bass_kernel_spmd

    nc = bacc.Bacc("TRN2", target_bir_lowering=False, num_devices=1)
    arrays = {name: np.ascontiguousarray(a) for name, a in inputs.items()}
    arrays["edge_weight1"] = arrays["edge_weight1"].reshape(-1)
    w = {name: nc.dram_tensor(f"in_{name}", a.shape, mybir.dt.from_np(a.dtype), kind="ExternalInput").ap()
         for name, a in arrays.items()}
    result = nc.dram_tensor("out_0", (N, D), F32, kind="ExternalOutput").ap()
    build(nc, w, result)
    r = run_bass_kernel_spmd(nc, [{f"in_{name}": a for name, a in arrays.items()}], core_ids=[0])
    return r.results[0]["out_0"]
```

```python
from contextlib import ExitStack

import numpy as np

import concourse.bass as bass
from concourse import mybir

F32 = mybir.dt.float32
BF16 = mybir.dt.bfloat16
I32 = mybir.dt.int32
U16 = mybir.dt.uint16
U8 = mybir.dt.uint8
ALU = mybir.AluOpType
ACT = mybir.ActivationFunctionType
AX = mybir.AxisListType

P = 128
N = 6250
E = 206250
D = 128
WIN = 32
NODE_TILES = -(-N // P)
NPAD = NODE_TILES * P
WINDOWS = NPAD // WIN
GRP = 4
RING = 4 * GRP
TILES = -(-((E + (P - 1) * WINDOWS) // P) // RING) * RING
GROUPS = TILES // GRP
CHUNKS = -(-TILES // P)
TCOLS = CHUNKS * P
ROW = 1650
ROWS = E // ROW
EPAD = (ROWS + 1) * ROW
PAD_DST = 8192
FAR = 64.0
RELS, BASES = 32, 8
TROW = 132


def bcast_mid(ap, n):
    return ap.unsqueeze(1).to_broadcast([ap.shape[0], n, ap.shape[1]])


def bcast_last(ap, n):
    return ap.unsqueeze(2).to_broadcast([ap.shape[0], ap.shape[1], n])


def build_identity(nc, pool, ident, zeroed, ready):
    pool.memset(ident[:], 0.0).then_inc(zeroed, 1)
    pool.wait_ge(zeroed, 1)
    pool.affine_select(out=ident[:], in_=ident[:], compare_op=ALU.not_equal, fill=1.0, base=0,
                       pattern=[[-1, P]], channel_multiplier=1).then_inc(ready, 1)


BT = 7
BATCHES = NODE_TILES // BT
BN = BT * P
BW = BN // WIN
HALVES = ((0, 512), (512, BN))
AROW = D + 1
LN_EPS = 1e-5
SEM_END = 256


def at_least(eng, sem, value):
    if not isinstance(value, int) or value > 0:
        eng.wait_ge(sem, value)


def upto(eng, i, c):
    return c if isinstance(i, int) else eng.to_reg(i * 4 + c)


def on(ins, sem, value):
    if not isinstance(value, int) or value > 0:
        ins.wait_op(sem, value, "sem-ge")
    return ins


def each_batch(eng):
    def run(steps):
        steps(0)
        with eng.Fori(1, BATCHES) as i:
            steps(i)
    return run


def staggered(eng, ahead=1):
    def run(steps):
        steps(0, ahead)
        with eng.Fori(1, BATCHES - ahead) as i:
            steps(i, ahead)
        for i in range(BATCHES - ahead, BATCHES):
            steps(i, BATCHES - 1 - i)
    return run


def row_of(vec, parts=P):
    return vec.rearrange("(a b) -> a b", a=1).to_broadcast([parts, vec.shape[0]])


class Shared:
    pass


def scope(nc, ctx):
    def sb(name, shape, dt=F32):
        return ctx.enter_context(nc.sbuf_tensor(name, shape, dt))

    def ps(name, shape, dt=F32):
        return ctx.enter_context(nc.psum_tensor(name, shape, dt))

    def sem(name):
        return ctx.enter_context(nc.semaphore(name))

    return sb, ps, sem


def zero_semaphores(nc, sh):
    with nc.Block() as block:
        @block.gpsimd
        def _(pool):
            pool.sem_clear(range(sh.first_sem, SEM_END))


def build_constants(nc, sh):
    with ExitStack() as ctx:
        sb, ps, sem = scope(nc, ctx)
        zeroed, ident_ok, iota_ok = sem("zeroed"), sem("ident_ok"), sem("iota_ok")
        placed = sem("placed")
        block = ctx.enter_context(nc.Block())

        @block.gpsimd
        def _(pool):
            build_identity(nc, pool, sh.ident, zeroed, ident_ok)
            pool.iota(sh.iota[:], pattern=[[1, WIN]], base=0, channel_multiplier=0,
                      allow_small_or_imprecise_dtypes=True)
            pool.memset(sh.ones[:], 1.0)
            pool.memset(sh.eps[:], LN_EPS)
            pool.memset(sh.zero[:], 0.0)

        @block.vector
        def _(v):
            v.memset(sh.place[:], 0.0).then_inc(placed, 1)
            v.wait_ge(placed, 1)
            v.wait_ge(ident_ok, 1)
            for k in range(4):
                for q in range(4):
                    rows = slice(WIN * k, WIN * k + WIN)
                    v.tensor_copy(sh.place[rows, q, WIN * q:WIN * q + WIN], sh.ident[rows, rows])


def batch_rows(dram, i):
    return dram[bass.ds(i * BN, BN), :].rearrange("(j p) f -> p j f", p=P)


def build_tiles_and_tables(nc, sh, w, fields_in, fields, types_tiled, win_dram):
    assert CHUNKS == 2 * BATCHES + 1
    with ExitStack() as ctx:
        _, ps, sem = scope(nc, ctx)
        at = [0]

        def carve(shape, dt=F32):
            width = int(np.prod(shape[1:]))
            view = sh.acc[0:shape[0], at[0]:at[0] + width]
            at[0] += width
            if dt != F32:
                view = view.bitcast(dt)[:, 0:width]
            if len(shape) == 3:
                view = view.rearrange("p (a b) -> p a b", b=shape[2])
            return view

        edge_rows = carve([P, 4, ROW], I32)
        less = carve([P, ROW])
        searched = at[0]
        at[0] = 0
        w_all, n_all = carve([P, TCOLS]), carve([P, TCOLS])
        xT, m1, m2 = carve([P, BN]), carve([P, BN]), carve([P, BN])
        x_rows = carve([P, BT, D])
        assert at[0] <= searched
        at[0] = searched

        pad_i, pad_z = carve([1, ROW], I32), carve([1, ROW], I32)
        zero_rows = carve([NPAD - N, D])
        last_i, last_f = carve([ROWS, 1], I32), carve([ROWS, 1])
        thr_row = carve([ROWS, 2 * P + 1])
        below = carve([ROWS, 2 * P + 1])
        ones_col, ones_sq = carve([P, 1]), carve([P, P])
        tri = carve([P, P])
        thr_col = carve([P, 4])
        row_i, row_f = carve([P, 4], I32), carve([P, 4])
        partial = carve([P, 4])
        bound = carve([P, 4])
        count_i, ntile_i, ntile = carve([P, 2], I32), carve([P, 2], I32), carve([P, 2])
        first, end = carve([P, 2]), carve([P, 2])
        tile_row = carve([P, TCOLS])
        member = carve([P, 2, TCOLS])
        per_win = carve([P, 2, 3])
        tile_col = carve([P, CHUNKS])
        got = carve([P, CHUNKS, 3])
        used_off, off_f, off_i = carve([P, CHUNKS]), carve([P, CHUNKS]), carve([P, CHUNKS], I32)
        win32 = carve([P, CHUNKS])
        off_c = carve([P, 2], I32)
        raw_i = [carve([P, 3, P], I32) for _ in range(2)]
        raw_f = [carve([P, 2, P]) for _ in range(2)]
        src_f, rel_f, type_f = ([carve([P, P]) for _ in range(2)] for _ in range(3))
        biased = carve([P, BT, D])
        table = carve([P, BT, TROW])
        wm, b_col, b3_row = carve([P, 3, D]), carve([P, 2]), carve([P, D])
        w_att, b_att, w_dst = carve([P, 2, 3]), carve([P, 3]), carve([P, 3, P])
        assert at[0] <= WINDOWS * AROW
        win_t = ctx.enter_context(nc.sbuf_tensor("win_t", [CHUNKS, P], U8))

        small = ps("ps_small", [P, 512])
        ps_rows, ps_first = small[:, 0:4], small[:, 4:6]
        ps_got = small[:, 6:6 + 3 * CHUNKS]
        ps_win = small[0:CHUNKS, P:2 * P]
        ps_t = ps("ps_t", [P, 4 * P])
        psA, psB, psC = (ps(f"ps{c}", [P, 1024]) for c in "ABC")

        pads_set, padded, last_in, copied = sem("pads_set"), sem("padded"), sem("last_in"), sem("copied")
        const, zeroed = sem("const"), sem("ones_set")
        dve_step, rows_mm, rows_in = sem("dve_step"), sem("rows_mm"), sh.rows_in
        below_ok, row_ok, ntile_ok, first_mm = sem("below_ok"), sem("row_ok"), sem("ntile_ok"), sem("first_mm")
        member_ok, got_mm, winf_ok = sem("member_ok"), sem("got_mm"), sem("winf_ok")
        win_tr, win_u8, win_out, win_in = sem("win_tr"), sem("win_u8"), sem("win_out"), sem("win_in")
        off_ok, off_go, fetched = sem("off_ok"), sem("off_go"), sh.fetched
        rel_ok, conv_ok, turned, laid = sem("rel_ok"), sem("conv_ok"), sem("turned"), sem("laid")
        types_out, laid_out = [sem("types_out0"), sem("types_out1")], sem("laid_out")
        params, dst_rep, x_in = sem("params"), sem("dst_rep"), sem("x_in")
        x_T, x_Tsb, h1, h1sb, h2, h2sb = (sem(n) for n in ("x_T", "x_Tsb", "h1", "h1sb", "h2", "h2sb"))
        h3, dst_mm, dst_sb, biased_ok, feat_ok, src_ok, stored = (
            sem(n) for n in ("h3", "dst_mm", "dst_sb", "biased_ok", "feat_ok", "src_ok", "stored"))
        block = ctx.enter_context(nc.Block())
        PARAMS = 15 * 16

        @block.sync
        def _(sp):
            for src, to in zip(fields_in, fields):
                sp.dma_start(to[0:E].rearrange("(a b) -> a b", a=330),
                             src.rearrange("(a b) -> a b", a=330)).then_inc(padded, 16)
            sp.wait_ge(pads_set, 2)
            for k, to in enumerate(fields):
                fill = pad_i if k == 1 else pad_z
                fill = fill if to.dtype == I32 else fill.bitcast(F32)
                sp.dma_start(to[E:EPAD].rearrange("(a b) -> a b", a=1), fill).then_inc(padded, 16)
            sp.wait_ge(win_u8, 1)
            sp.dma_start(win_dram.rearrange("(a b) -> a b", b=P), win_t[:]).then_inc(win_out, 16)
            sp.wait_ge(win_out, 16)
            sp.dma_start(sh.win_all[:], win_dram.rearrange("(a b) -> a b", a=1)).then_inc(win_in, 16)
            sp.wait_ge(copied, 32)

            def store_types(i, b):
                n = 2 * i + b
                sp.wait_ge(conv_ok, n + 1)
                sp.dma_start(types_tiled[bass.ds(n * P, P), :], type_f[b]).then_inc(types_out[b], 16)

            @each_batch(sp)
            def _(i):
                at_least(sp, x_T, i)
                sp.dma_start(x_rows, batch_rows(sh.xpad, i)).then_inc(x_in, 16)
                store_types(i, 0)
                store_types(i, 1)
            store_types(BATCHES, 0)
            sp.wait_ge(laid, CHUNKS)
            sp.dma_start(sh.w_dram, w_all).then_inc(laid_out, 16)
            sp.dma_start(sh.n_dram, n_all).then_inc(laid_out, 16)
            sp.wait_ge(laid_out, 32)
            sp.wait_ge(types_out[0], 16 * (BATCHES + 1))
            sp.wait_ge(types_out[1], 16 * BATCHES)
            sp.wait_ge(win_in, 16)

        @block.gpsimd
        def _(pool):
            pool.memset(pad_i, PAD_DST).then_inc(pads_set, 1)
            pool.memset(pad_z, 0).then_inc(pads_set, 1)
            pool.memset(ones_col, 1.0)
            pool.memset(ones_sq, 1.0).then_inc(zeroed, 1)
            pool.iota(thr_row, pattern=[[WIN, 2 * P + 1]], base=0, channel_multiplier=0,
                      allow_small_or_imprecise_dtypes=True)
            for c in range(2):
                for s in range(2):
                    pool.iota(thr_col[:, 2 * c + s:2 * c + s + 1], pattern=[[1, 1]],
                              base=WIN * (P * c + s), channel_multiplier=WIN,
                              allow_small_or_imprecise_dtypes=True)
            pool.iota(tile_row, pattern=[[1, TCOLS]], base=0, channel_multiplier=0,
                      allow_small_or_imprecise_dtypes=True)
            pool.iota(tile_col, pattern=[[P, CHUNKS]], base=0, channel_multiplier=1,
                      allow_small_or_imprecise_dtypes=True)
            for c in range(2):
                pool.iota(per_win[:, c, 1:2], pattern=[[1, 1]], base=P * c, channel_multiplier=1,
                          allow_small_or_imprecise_dtypes=True)
                pool.memset(per_win[:, c, 2:3], 1.0)
            pool.wait_ge(zeroed, 1)
            pool.affine_select(out=tri, in_=ones_sq, compare_op=ALU.is_gt, fill=0.0, base=0,
                               pattern=[[1, P]], channel_multiplier=-1).then_inc(const, 1)
            pool.wait_ge(padded, 160)
            pool.wait_ge(row_ok, 1)
            for k in range(4):
                pool.indirect_dma_start(
                    out=edge_rows[:, k, :], out_offset=None,
                    in_=fields[1].rearrange("(a b) -> a b", b=ROW),
                    in_offset=bass.IndirectOffsetOnAxis(ap=row_i[:, k:k + 1], axis=0),
                ).then_inc(rows_in, 16)
            pool.wait_ge(rows_in, 64)

            def fetch(i, b):
                pool.wait_ge(off_ok, 2 * i + b + 1)
                pool.sem_inc(off_go, 1)
                for k, field in enumerate(fields):
                    to = raw_i[b][:, k, :] if k < 3 else raw_f[b][:, k - 3, :]
                    pool.indirect_dma_start(
                        out=to, out_offset=None, in_=field.rearrange("(a b) -> a b", b=1),
                        in_offset=bass.IndirectOffsetOnAxis(ap=off_c[:, b:b + 1], axis=0),
                    ).then_inc(fetched[b][k], 16)

            with pool.Fori(0, BATCHES) as i:
                fetch(i, 0)
                fetch(i, 1)
            fetch(BATCHES, 0)

        @block.tensor
        def _(pe):
            pe.wait_ge(const, 1)
            pe.wait_ge(below_ok, 1)
            for c in range(2):
                for s in range(2):
                    mm = pe.matmul(ps_rows[:, 2 * c + s:2 * c + s + 1],
                                   below[:, P * c + s:P * c + s + P], ones_col[0:ROWS, :],
                                   start=True, stop=True)
            mm.then_inc(rows_mm, 1)
            pe.wait_ge(ntile_ok, 1)
            pe.matmul(ps_first[:, 0:1], tri, ntile[:, 0:1], start=True, stop=True)
            pe.matmul(ps_first[:, 1:2], tri, ntile[:, 1:2], start=True, stop=False)
            pe.matmul(ps_first[:, 1:2], ones_sq, ntile[:, 0:1], start=False,
                      stop=True).then_inc(first_mm, 1)
            pe.wait_ge(member_ok, 1)
            for k in range(CHUNKS):
                for c in range(2):
                    mm = pe.matmul(ps_got[:, 3 * k:3 * k + 3], member[:, c, P * k:P * k + P],
                                   per_win[:, c, :], start=c == 0, stop=c == 1)
            mm.then_inc(got_mm, 1)
            pe.wait_ge(winf_ok, 1)
            pe.transpose(ps_win, used_off, sh.ident[:]).then_inc(win_tr, 1)
            pe.wait_ge(params, PARAMS)
            pe.wait_ge(dst_rep, 1)

            def turn_chunk(i, b):
                n = 2 * i + b
                pe.wait_ge(fetched[b][3], 16 * i + 16)
                pe.wait_ge(fetched[b][4], 16 * i + 16)
                pe.wait_ge(conv_ok, n + 1)
                at_least(pe, laid, n)
                pe.transpose(ps_t[:, 0:P], src_f[b], sh.ident[:])
                pe.transpose(ps_t[:, P:2 * P], rel_f[b], sh.ident[:])
                pe.transpose(ps_t[:, 2 * P:3 * P], raw_f[b][:, 0, :], sh.ident[:])
                pe.transpose(ps_t[:, 3 * P:4 * P], raw_f[b][:, 1, :], sh.ident[:]).then_inc(turned, 1)

            @each_batch(pe)
            def _(i):
                pe.wait_ge(x_in, 16 * i + 16)
                at_least(pe, biased_ok, i)
                at_least(pe, src_ok, i)
                for j in range(BT):
                    mm = pe.transpose(psA[:, P * j:P * j + P], x_rows[:, j, :], sh.ident[:])
                mm.then_inc(x_T, 1)
                pe.wait_ge(x_Tsb, i + 1)
                at_least(pe, dst_sb, 3 * i)
                for a, b in HALVES:
                    mm = pe.matmul(psB[:, a:b], wm[:, 0, :], xT[:, a:b], start=True, stop=True)
                mm.then_inc(h1, 1)
                for a, b in HALVES:
                    mm = pe.matmul(psA[:, a:b], w_dst[:, 0, :], xT[:, a:b], start=True, stop=True)
                mm.then_inc(dst_mm, 1)
                turn_chunk(i, 0)
                pe.wait_ge(h1sb, i + 1)
                for a, b in HALVES:
                    mm = pe.matmul(psC[:, a:b], wm[:, 1, :], m1[:, a:b], start=True, stop=True)
                mm.then_inc(h2, 1)
                for a, b in HALVES:
                    mm = pe.matmul(psB[:, a:b], w_dst[:, 1, :], xT[:, a:b], start=True, stop=True)
                mm.then_inc(dst_mm, 1)
                turn_chunk(i, 1)
                pe.wait_ge(h2sb, i + 1)
                for a, b in HALVES:
                    mm = pe.matmul(psC[:, a:b], w_dst[:, 2, :], xT[:, a:b], start=True, stop=True)
                mm.then_inc(dst_mm, 1)
                pe.wait_ge(dst_sb, 3 * i + 1)
                for j in range(BT):
                    pe.matmul(psA[:, P * j:P * j + P], m2[:, P * j:P * j + P], wm[:, 2, :],
                              start=True, stop=True)
                for j in range(BT):
                    mm = pe.matmul(psA[:, BN + 3 * j:BN + 3 * j + 3], xT[:, P * j:P * j + P],
                                   w_att[:, 0, :], start=True, stop=True)
                mm.then_inc(h3, 1)
            turn_chunk(BATCHES, 0)

        @block.scalar
        def _(act):
            act.dma_start(last_i, fields_in[1].rearrange("(a b) -> a b", b=ROW)[:, ROW - 1:ROW],
                          allow_slow_non_contiguous=True).then_inc(last_in, 16)
            for k in range(3):
                act.dma_start(wm[:, k, :], w[f"L0_gnn_W_msg_{k + 1}"]).then_inc(params, 16)
                for s in range(2):
                    act.dma_start(w_att[:, s, k:k + 1],
                                  w[f"L0_gnn_W_att_{k + 1}"][s * D:(s + 1) * D, :]).then_inc(params, 16)
                act.dma_start(b_att[:, k:k + 1], row_of(w[f"L0_gnn_b_att_{k + 1}"])).then_inc(params, 16)
            for k in range(2):
                act.dma_start(b_col[:, k:k + 1], w[f"L0_gnn_b_msg_{k + 1}"].rearrange("(a b) -> a b", b=1)
                              ).then_inc(params, 16)
            act.dma_start(b3_row, row_of(w["L0_gnn_b_msg_3"])).then_inc(params, 16)
            act.dma_start(sh.xpad[0:N, :], w["x"]).then_inc(copied, 16)
            act.wait_ge(dst_rep, 1)
            act.dma_start(sh.xpad[N:NPAD, :], zero_rows).then_inc(copied, 16)
            act.wait_ge(params, PARAMS)

            @each_batch(act)
            def _(i):
                def copy_terms(k, out):
                    act.wait_ge(dst_mm, 3 * i + k + 1)
                    to = sh.dst_terms[:, bass.ds(i * BW * 3 * WIN, BW * 3 * WIN)].rearrange(
                        "p (w k d) -> p w k d", k=3, d=WIN)[:, :, k, :]
                    act.copy(to, out[:, 0:BN].rearrange("p (w d) -> p w d", d=WIN)).then_inc(dst_sb, 1)

                act.wait_ge(h1, i + 1)
                act.activation(m1, psB[:, 0:BN], ACT.Relu, bias=b_col[:, 0:1]).then_inc(h1sb, 1)
                copy_terms(0, psA)
                act.wait_ge(h2, i + 1)
                act.activation(m2, psC[:, 0:BN], ACT.Relu, bias=b_col[:, 1:2]).then_inc(h2sb, 1)
                copy_terms(1, psB)
                copy_terms(2, psC)
                act.wait_ge(biased_ok, i + 1)
                at_least(act, stored, 16 * i)
                act.activation(table[:, :, 0:D], biased, ACT.Relu).then_inc(feat_ok, 1)
                act.wait_ge(feat_ok, i + 1)
                act.wait_ge(src_ok, i + 1)
                act.dma_start(batch_rows(sh.table, i), table).then_inc(stored, 16)
            act.wait_ge(stored, 16 * BATCHES)

        @block.vector
        def _(v):
            step = [0]

            def then(ins):
                step[0] += 1
                ins.then_inc(dve_step, 1)
                v.wait_ge(dve_step, step[0])

            v.wait_ge(last_in, 16)
            v.wait_ge(const, 1)
            then(v.tensor_copy(last_f, last_i))
            v.tensor_scalar(below, thr_row, last_f[:, 0:1], None,
                            op0=ALU.is_gt).then_inc(below_ok, 1)
            v.wait_ge(rows_mm, 1)
            v.tensor_copy(row_i, ps_rows).then_inc(row_ok, 1)
            then(v.tensor_copy(row_f, ps_rows))
            v.memset(zero_rows, 0.0)
            v.wait_ge(params, PARAMS)
            v.memset(table[:, :, D:D + 1], 1.0)
            v.tensor_copy(w_dst, bcast_last(w_att[:, 1, :], P)).then_inc(dst_rep, 1)
            v.wait_ge(rows_in, 64)
            for k in range(4):
                then(v.tensor_scalar(less, edge_rows[:, k, :], thr_col[:, k:k + 1], 0.0,
                                     op0=ALU.is_lt, op1=ALU.add, accum_out=partial[:, k:k + 1]))
            then(v.scalar_tensor_tensor(out=bound, in0=row_f, scalar=float(ROW),
                                        in1=partial, op0=ALU.mult, op1=ALU.add))
            b = bound.rearrange("p (c s) -> p c s", s=2)
            then(v.scalar_tensor_tensor(out=count_i, in0=b[:, :, 1], scalar=float(P - 1),
                                        in1=b[:, :, 0], op0=ALU.add, op1=ALU.subtract))
            then(v.tensor_scalar(ntile_i, count_i, 7, None, op0=ALU.arith_shift_right))
            then(v.tensor_copy(ntile, ntile_i))
            v.sem_inc(ntile_ok, 1)
            v.wait_ge(first_mm, 1)
            then(v.tensor_copy(first, ps_first))
            then(v.tensor_tensor(end, first, ntile, ALU.add))
            v.scalar_tensor_tensor(out=per_win[:, :, 0], in0=first, scalar=-float(P),
                                   in1=b[:, :, 0], op0=ALU.mult, op1=ALU.add)
            for c in range(2):
                then(v.tensor_scalar(member[:, c, :], tile_row, first[:, c:c + 1], None,
                                     op0=ALU.is_ge))
                then(v.scalar_tensor_tensor(out=member[:, c, :], in0=tile_row,
                                            scalar=end[:, c:c + 1], in1=member[:, c, :],
                                            op0=ALU.is_lt, op1=ALU.mult))
            v.sem_inc(member_ok, 1)
            v.wait_ge(got_mm, 1)
            then(v.tensor_copy(got.rearrange("p a b -> p (a b)"), ps_got))
            then(v.tensor_scalar(used_off, tile_col, float(P), -float(E), op0=ALU.mult,
                                 op1=ALU.add))
            then(v.tensor_tensor(used_off, used_off, got[:, :, 2], ALU.mult))
            then(v.scalar_tensor_tensor(out=off_f, in0=used_off, scalar=float(E),
                                        in1=got[:, :, 0], op0=ALU.add, op1=ALU.add))
            then(v.tensor_copy(off_i, off_f))
            v.tensor_copy(off_c[:, 0:1], off_i[:, 0:1]).then_inc(off_ok, 1)
            then(v.tensor_scalar(win32, got[:, :, 1], float(WIN), None, op0=ALU.mult))
            then(v.tensor_copy(used_off, got[:, :, 1]))
            v.sem_inc(winf_ok, 1)
            v.wait_ge(win_tr, 1)
            v.tensor_copy(win_t[:], ps_win).then_inc(win_u8, 1)

            def give_offsets(i, b):
                for k in range(5):
                    at_least(v, fetched[b][k], 16 * i)
                v.tensor_copy(off_c[:, b:b + 1], off_i[:, bass.ds(2 * i + b, 1)]).then_inc(off_ok, 1)

            def convert(i, b):
                n = 2 * i + b
                for k in range(3):
                    v.wait_ge(fetched[b][k], 16 * i + 16)
                at_least(v, types_out[b], 16 * i)
                v.tensor_copy(src_f[b], raw_i[b][:, 0, :])
                v.tensor_copy(type_f[b], raw_i[b][:, 2, :])
                v.tensor_scalar(rel_f[b], raw_i[b][:, 1, :], win32[:, bass.ds(n, 1)], None,
                                op0=ALU.subtract).then_inc(rel_ok, 1)
                v.wait_ge(rel_ok, n + 1)
                v.tensor_scalar(rel_f[b], rel_f[b], FAR, None, op0=ALU.min).then_inc(conv_ok, 1)

            def lay_out(n):
                v.wait_ge(turned, n + 1)
                v.tensor_copy(sh.src_all[:, bass.ds(n * P, P)], ps_t[:, 0:P])
                v.tensor_copy(sh.rel_all[:, bass.ds(n * P, P)], ps_t[:, P:2 * P])
                v.tensor_copy(w_all[:, bass.ds(n * P, P)], ps_t[:, 2 * P:3 * P])
                v.tensor_copy(n_all[:, bass.ds(n * P, P)], ps_t[:, 3 * P:4 * P]).then_inc(laid, 1)

            @each_batch(v)
            def _(i):
                give_offsets(i, 1)
                v.wait_ge(x_T, i + 1)
                at_least(v, h3, i)
                v.tensor_copy(xT, psA[:, 0:BN]).then_inc(x_Tsb, 1)
                convert(i, 0)
                lay_out(2 * i)
                give_offsets(i + 1, 0)
                convert(i, 1)
                lay_out(2 * i + 1)
                v.wait_ge(h3, i + 1)
                at_least(v, feat_ok, i)
                v.tensor_tensor(biased, psA[:, 0:BN].rearrange("p (j f) -> p j f", f=D),
                                bcast_mid(b3_row, BT), ALU.add).then_inc(biased_ok, 1)
                at_least(v, stored, 16 * i)
                v.tensor_tensor(table[:, :, D + 1:D + 4],
                                psA[:, BN:BN + 3 * BT].rearrange("p (j k) -> p j k", k=3),
                                bcast_mid(b_att, BT), ALU.add).then_inc(src_ok, 1)
            convert(BATCHES, 0)
            lay_out(CHUNKS - 1)


def window_slice(table, window, width, count=1):
    cols = table[:, bass.ds(window * width, width * count)]
    return cols if count == 1 else cols.rearrange("p (w c) -> p w c", c=width)


class TileWindows:

    def __init__(self, v, sh, name):
        self.v, self.sh = v, sh
        self.regs = [v.alloc_register(f"{name}_window{t}") for t in range(RING)]

    def load(self, i, q):
        first, last = {0: (0, RING - GRP), 3: (RING - GRP, RING)}.get(q, (0, 0))
        if last:
            self.v.load(self.regs[first:last],
                        self.sh.win_all[0:1, bass.ds(i * RING + first, last - first)])

    def load_all(self, i):
        self.v.load(self.regs, self.sh.win_all[0:1, bass.ds(i * RING, RING)])

    def of(self, q):
        return [self.v.snap(r, min_val=0, max_val=WINDOWS - 1)
                for r in self.regs[GRP * q:GRP * q + GRP]]


def gather_rows(pool, table, rows, index_ready, granted, sh, n, q):
    pool.wait_ge(index_ready, n + 1)
    pool.sem_inc(granted, 1)
    for u in range(GRP):
        slot = GRP * q + u
        pool.indirect_dma_start(
            out=rows[:, slot, :], out_offset=None, in_=table[:, :],
            in_offset=bass.IndirectOffsetOnAxis(ap=sh.index[:, slot:slot + 1], axis=0),
        ).then_inc(sh.gathered[q], 16)


def gathered_count(layer, i):
    return i * (16 * GRP) + (layer * (GROUPS // 4) + 1) * 16 * GRP


def add_up(v, sh, windows, out, summed, added, i, q, rows=P, width=AROW):
    into = windows.of((q - 1) % 4)
    done, before = upto(v, i, q), upto(v, i, q - 1)
    for u, window in enumerate(into):
        to = window_slice(sh.acc, window, AROW)[0:rows, 0:width]
        if u == 0:
            at_least(v, added[GRP - 1], before)
        ins = v.tensor_tensor(to, to, out[0:rows, (q - 1) % 2, u, 0:width], ALU.add)
        if u == 0:
            on(ins, summed, done)
        else:
            on(ins, added[u - 1], done)
        ins.then_inc(added[u], 1)
        yield


def stage_indices(act, sh, index_ready, summed, n, q):
    at_least(act, summed, n - 3)
    act.copy(sh.index[:, GRP * q:GRP * q + GRP],
             sh.src_all[:, bass.ds(n * GRP, GRP)]).then_inc(index_ready, 1)


def attention_edges(nc, sh):
    with ExitStack() as ctx:
        sb, ps, sem = scope(nc, ctx)
        rows = sb("rows0", [P, RING, TROW])
        S = sb("S0", [P, 2, GRP, 4, WIN])
        picked = sb("picked", [P, GRP, 3, WIN])
        dst_term = sb("dst_term", [P, GRP, 3])
        z = sb("z0", [P, 2, GRP, 3])
        zr = sb("zr0", [P, 2, GRP, 3])
        a = sb("a0", [P, 2, GRP, 3])
        out = ps("out0", [P, 2, GRP, 256])
        index_ready, granted = sem("index_ready"), sem("granted")
        hot_ok, picked_ok, term_ok = sem("hot_ok"), sem("picked_ok"), sem("term_ok")
        z_ready, relu_ok, a_ready = sem("z_ready"), sem("relu_ok"), sem("a_ready")
        s_ready, summed, zeroed = sem("s_ready"), sem("summed"), sem("zeroed")
        added = [sem(f"added{u}") for u in range(GRP)]
        block = ctx.enter_context(nc.Block())
        ACT_ZERO = WINDOWS // 3 * AROW

        @block.gpsimd
        def _(pool):
            with pool.Fori(0, GROUPS // 4) as i:
                for q in range(4):
                    gather_rows(pool, sh.table, rows, index_ready, granted, sh, i * 4 + q, q)

        @block.scalar
        def _(act):
            def step(i, q):
                n = i * 4 + q
                stage_indices(act, sh, index_ready, summed, n + 2, (q + 2) % 4)
                act.wait_ge(z_ready, n + 1)
                at_least(act, a_ready, n)
                act.activation(zr[:, q % 2], z[:, q % 2], ACT.Relu).then_inc(relu_ok, 1)
                act.wait_ge(relu_ok, n + 1)
                at_least(act, s_ready, n - 1)
                act.activation(a[:, q % 2], zr[:, q % 2], ACT.Exp).then_inc(a_ready, 1)

            for q in range(2):
                stage_indices(act, sh, index_ready, summed, q, q)
            act.copy(sh.acc[:, 0:ACT_ZERO],
                     sh.zero[:, 0:1].to_broadcast([P, ACT_ZERO])).then_inc(zeroed, 1)
            for q in range(4):
                step(0, q)
            with act.Fori(1, GROUPS // 4) as i:
                for q in range(4):
                    step(i, q)

        @block.tensor
        def _(pe):
            def step(i, q):
                n = i * 4 + q
                pe.wait_ge(s_ready, n + 1)
                at_least(pe, added[GRP - 1], n - 1)
                for u in range(GRP):
                    mm = pe.matmul(out[:, q % 2, u, 0:AROW],
                                   S[:, q % 2, u].rearrange("p k d -> p (k d)"),
                                   rows[:, GRP * q + u, 0:AROW], start=True, stop=True)
                mm.then_inc(summed, 1)

            for q in range(4):
                step(0, q)
            with pe.Fori(1, GROUPS // 4) as i:
                for q in range(4):
                    step(i, q)

        @block.vector
        def _(v):
            windows = TileWindows(v, sh, "l0")

            def step(i, q, first=False):
                b = q % 2
                one_hot = S[:, b, :, 3, :]
                adds = iter(()) if first else add_up(v, sh, windows, out, summed, added, i, q)
                now, two_ago = upto(v, i, q + 1), upto(v, i, q - 1)
                on(v.tensor_tensor(one_hot, bcast_last(sh.rel_all[:, bass.ds((i * 4 + q) * GRP, GRP)], WIN),
                                   bcast_mid(sh.iota[:], GRP), ALU.is_equal),
                   summed, two_ago).then_inc(hot_ok, 1)
                windows.load(i, q)
                for u, window in enumerate(windows.of(q)):
                    terms = window_slice(sh.dst_terms, window, 3 * WIN)
                    ins = v.tensor_tensor(picked[:, u], terms.rearrange("p (k d) -> p k d", k=3),
                                          bcast_mid(one_hot[:, u, :], 3), ALU.mult)
                    if u == 0:
                        on(ins, hot_ok, now)
                ins.then_inc(picked_ok, 1)
                on(v.tensor_reduce(dst_term[:], picked[:], axis=AX.X, op=ALU.add),
                   picked_ok, now).then_inc(term_ok, 1)
                v.wait_ge(sh.gathered[q], gathered_count(0, i))
                on(v.tensor_tensor(z[:, b], dst_term[:], rows[:, GRP * q:GRP * q + GRP, D + 1:D + 4],
                                   ALU.add), term_ok, now).then_inc(z_ready, 1)
                for _ in adds:
                    pass
                on(v.tensor_tensor(S[:, b, :, 0:3, :],
                                   S[:, b, :, 3:4, :].to_broadcast([P, GRP, 3, WIN]),
                                   a[:, b].unsqueeze(3).to_broadcast([P, GRP, 3, WIN]),
                                   ALU.mult), a_ready, now).then_inc(s_ready, 1)

            step(0, 0, first=True)
            v.memset(sh.acc[:, ACT_ZERO:], 0.0).then_inc(zeroed, 1)
            v.wait_ge(zeroed, 2)
            for q in range(1, 4):
                step(0, q)
            with v.Fori(1, GROUPS // 4) as i:
                for q in range(4):
                    step(i, q)
            for _ in add_up(v, sh, windows, out, summed, added, 0, GROUPS):
                pass


class Chain:

    def __init__(self, eng, sem, turn=0, per_turn=0, base=0):
        self.eng, self.sem, self.start, self.per_turn = eng, sem, turn * per_turn + base, per_turn
        self.count = 0

    def then(self, ins):
        self.count += 1
        ins.then_inc(self.sem, 1)
        self.eng.wait_ge(self.sem, self.start + self.count)

    def close(self):
        assert self.count == self.per_turn, self.count


NORM_LINKS = 4


class Norm:

    def __init__(self, sb, sem, name):
        self.stats = sb(f"{name}_stats", [P, BT, 6])
        self.mean_var = sb(f"{name}_mean_var", [P, BT, 2])
        self.std = sb(f"{name}_std", [P, BT])
        self.rstd = sb(f"{name}_rstd", [P, BT])
        self.go = sem(f"{name}_go")
        self.var_ok, self.std_ok = sem(f"{name}_var_ok"), sem(f"{name}_std_ok")

    def moments(self, v, chain, y):
        v.sem_inc(self.go, 1)
        for j in range(BT):
            ins = v.bn_stats(self.stats[:, j, :], y[:, j, :])
        chain.then(ins)
        v.sem_inc(self.go, 1)
        for j in range(BT):
            ins = v.bn_aggr(self.mean_var[:, j, :], self.stats[:, j, :])
        chain.then(ins)
        v.sem_inc(self.var_ok, 1)

    def apply(self, v, chain, y, turn):
        v.wait_ge(self.std_ok, turn + 1)
        chain.then(v.reciprocal(self.rstd[:], self.std[:]))
        for j in range(BT):
            ins = v.tensor_scalar(y[:, j, :], y[:, j, :], self.mean_var[:, j, 0:1],
                                  self.rstd[:, j:j + 1], op0=ALU.subtract, op1=ALU.mult)
        chain.then(ins)

    def vector(self, v, chain, y, turn):
        self.moments(v, chain, y)
        self.apply(v, chain, y, turn)

    def scalar(self, act, sh, turn):
        act.wait_ge(self.var_ok, turn + 1)
        act.activation(self.std[:], self.mean_var[:, :, 1], ACT.Sqrt,
                       bias=sh.eps[:, 0:1]).then_inc(self.std_ok, 1)


def tiles_of(buf):
    return buf.rearrange("p (j f) -> p j f", f=D)


def transpose_tiles(pe, out, rows, ident):
    for j in range(BT):
        mm = pe.transpose(out[:, P * j:P * j + P], rows[:, j, :], ident[:])
    return mm


def set_zero(pool, sh, cols):
    return pool.tensor_copy(cols, sh.zero[0:cols.shape[0], 0:1].to_broadcast(list(cols.shape)))


def finish_attention(nc, sh, w):
    with ExitStack() as ctx:
        sb, ps, sem = scope(nc, ctx)
        inv = sb("inv", [P, WINDOWS])
        inv_deg = sb("inv_deg", [P, WINDOWS])
        x_rows, y = tiles_of(sb("x_rows1", [P, BN])[:]), tiles_of(sb("y1", [P, BN])[:])
        xT, hnT, c1, x1T = sb("xT1", [P, BN]), sb("hnT1", [P, BN]), sb("c1", [P, BN]), sb("x1T", [P, BN])
        normed = sb("normed", [3 * WIN, BW, D])
        table = sb("table1", [P, BT, TROW])
        w_c1, w_c2, b_c1, b_c2 = sb("w_c1", [P, 2, D]), sb("w_c2", [P, D]), sb("b_c1", [P, 1]), sb("b_c2", [P, D])
        w_proj, w_projT = sb("w_proj", [P, D]), sb("w_projT", [P, D])
        w_edge = sb("w_edge", [P, 2])
        edge_vec = sb("edge_vec", [P, 2])
        dst_rep = sb("dst_rep1", [P, P])
        norm = Norm(sb, sem, "norm1")
        psA, psB, psC, psD = (ps(f"ps1{c}", [P, 1024]) for c in "ABCD")
        params, setup, wT, rep_ok = sem("params"), sem("setup"), sem("wT"), sem("rep_ok")
        inv_ok, cleared = sem("inv_ok"), sem("cleared")
        x_in, x_T, xT_sb, norm_ok, hn, hn_sb = (
            sem(n) for n in ("x_in", "x_T", "xT_sb", "norm_ok", "hn", "hn_sb"))
        c1_mm, c1_sb, c2_mm, x1_ok, x1_T, x1T_sb = (
            sem(n) for n in ("c1_mm", "c1_sb", "c2_mm", "x1_ok", "x1_T", "x1T_sb"))
        src_mm, h_mm, feat_ok, terms_ok, dst_ok, stored, x1_out, link = (
            sem(n) for n in ("src_mm", "h_mm", "feat_ok", "terms_ok", "dst_ok", "stored", "x1_out", "link"))
        block = ctx.enter_context(nc.Block())
        PARAMS = 7 * 16

        @block.sync
        def _(sp):
            sp.dma_start(x_rows, batch_rows(sh.xpad, 0)).then_inc(x_in, 16)
            for to, of in ((w_c1[:], w["L0_gnn_W_c1"].rearrange("(s p) f -> p s f", p=P)),
                           (w_c2[:], w["L0_gnn_W_c2"]),
                           (b_c1[:], w["L0_gnn_b_c1"].rearrange("(a b) -> a b", b=1)),
                           (b_c2[:], row_of(w["L0_gnn_b_c2"])),
                           (w_proj[:], w["L1_gnn_W_proj"]),
                           (w_edge[:, 0:1], w["L1_gnn_w_edge"][0:D].rearrange("(a b) -> a b", b=1)),
                           (w_edge[:, 1:2], w["L1_gnn_w_edge"][D:2 * D].rearrange("(a b) -> a b", b=1))):
                sp.dma_start(to, of).then_inc(params, 16)

            @staggered(sp)
            def _(i, more):
                if more:
                    sp.wait_ge(x_T, i + 1)
                    sp.dma_start(x_rows, batch_rows(sh.xpad, i + 1)).then_inc(x_in, 16)
                sp.wait_ge(x1_ok, i + 1)
                sp.dma_start(batch_rows(sh.x1, i), y).then_inc(x1_out, 16)
            sp.wait_ge(x1_out, 16 * BATCHES)

        @block.gpsimd
        def _(pool):
            pool.wait_ge(inv_ok, 1)

            @each_batch(pool)
            def _(i):
                pool.wait_ge(norm_ok, i + 1)
                set_zero(pool, sh, sh.acc[0:2 * WIN, bass.ds(i * BW * AROW, BW * AROW)]).then_inc(cleared, 1)
                pool.wait_ge(cleared, i + 1)

        @block.tensor
        def _(pe):
            pe.wait_ge(params, PARAMS)
            pe.transpose(psA[:, 0:P], w_proj[:], sh.ident[:])
            for s in range(2):
                mm = pe.matmul(psA[:, P + s:P + s + 1], w_proj[:], w_edge[:, s:s + 1], start=True, stop=True)
            mm.then_inc(wT, 1)
            pe.wait_ge(rep_ok, 1)
            def first_product(i):
                pe.wait_ge(x_in, 16 * i + 16)
                at_least(pe, terms_ok, i - 1)
                transpose_tiles(pe, psA, x_rows, sh.ident).then_inc(x_T, 1)
                pe.wait_ge(norm_ok, i + 1)
                at_least(pe, feat_ok, i - 1)
                for win in range(BW):
                    mm = pe.matmul(psB[:, WIN * win:WIN * win + WIN], normed[:, win, :],
                                   sh.place[0:3 * WIN, 0, 0:WIN], start=True, stop=True)
                mm.then_inc(hn, 1)
                pe.wait_ge(xT_sb, i + 1)
                pe.wait_ge(hn_sb, i + 1)
                at_least(pe, dst_ok, i - 1)
                for a, b in HALVES:
                    pe.matmul(psC[:, a:b], w_c1[:, 0, :], xT[:, a:b], start=True, stop=False)
                    mm = pe.matmul(psC[:, a:b], w_c1[:, 1, :], hnT[:, a:b], start=False, stop=True)
                mm.then_inc(c1_mm, 1)

            def second_product(i):
                pe.wait_ge(c1_sb, i + 1)
                for j in range(BT):
                    tile = slice(P * j, P * j + P)
                    pe.matmul(psD[:, tile], c1[:, tile], w_c2[:], start=True, stop=False)
                    mm = pe.matmul(psD[:, tile], xT[:, tile], sh.ident[:], start=False, stop=True)
                mm.then_inc(c2_mm, 1)

            first_product(0)
            second_product(0)

            @staggered(pe)
            def _(i, more):
                if more:
                    first_product(i + 1)
                pe.wait_ge(x1_ok, i + 1)
                transpose_tiles(pe, psA, y, sh.ident).then_inc(x1_T, 1)
                if more:
                    second_product(i + 1)
                pe.wait_ge(x1T_sb, i + 1)
                for a, b in HALVES:
                    pe.matmul(psC[:, a:b], dst_rep[:], x1T[:, a:b], start=True, stop=True)
                for j in range(BT):
                    mm = pe.matmul(psA[:, BN + j:BN + j + 1], x1T[:, P * j:P * j + P],
                                   edge_vec[:, 0:1], start=True, stop=True)
                mm.then_inc(src_mm, 1)
                for j in range(BT):
                    mm = pe.matmul(psB[:, P * j:P * j + P], x1T[:, P * j:P * j + P], w_projT[:],
                                   start=True, stop=True)
                mm.then_inc(h_mm, 1)

        @block.scalar
        def _(act):
            act.wait_ge(params, PARAMS)

            def first_part(i):
                act.wait_ge(hn, i + 1)
                act.copy(hnT[:], psB[:, 0:BN]).then_inc(hn_sb, 1)
                act.wait_ge(c1_mm, i + 1)
                act.activation(c1[:], psC[:, 0:BN], ACT.Relu, bias=b_c1[:, 0:1]).then_inc(c1_sb, 1)

            first_part(0)

            @staggered(act)
            def _(i, more):
                norm.scalar(act, sh, i)
                if more:
                    first_part(i + 1)
                act.wait_ge(src_mm, i + 1)
                act.copy(sh.dst_terms1[:, bass.ds(i * BN, BN)], psC[:, 0:BN]).then_inc(dst_ok, 1)
                act.wait_ge(h_mm, i + 1)
                at_least(act, stored, 16 * i)
                act.copy(table[:, :, 0:D], tiles_of(psB[:, 0:BN])).then_inc(feat_ok, 1)
                act.wait_ge(feat_ok, i + 1)
                act.wait_ge(terms_ok, i + 1)
                act.dma_start(batch_rows(sh.table1, i), table[:]).then_inc(stored, 16)
            act.wait_ge(stored, 16 * BATCHES)

        @block.vector
        def _(v):
            acc3 = sh.acc[:].rearrange("p (w c) -> p w c", c=AROW)
            v.wait_ge(params, PARAMS)
            v.memset(table[:, :, D:TROW], 1.0)
            once = Chain(v, setup)
            once.then(v.tensor_scalar(inv[:], acc3[:, :, D], 1.0, None, op0=ALU.max))
            once.then(v.reciprocal(inv[:], inv[:]))
            for k in range(3):
                ins = v.tensor_copy(inv_deg[WIN * k:WIN * k + WIN, :], inv[3 * WIN:4 * WIN, :])
            once.then(ins)
            once.then(v.scalar_tensor_tensor(out=inv[0:3 * WIN, :], in0=inv[0:3 * WIN, :],
                                             scalar=1.0 / 3.0, in1=inv_deg[0:3 * WIN, :],
                                             op0=ALU.mult, op1=ALU.mult))
            v.sem_inc(inv_ok, 1)
            v.wait_ge(wT, 1)
            v.tensor_copy(w_projT[:], psA[:, 0:P])
            once.then(v.tensor_copy(edge_vec[:], psA[:, P:P + 2]))
            v.tensor_copy(dst_rep[:], edge_vec[:, 1:2].to_broadcast([P, P])).then_inc(rep_ok, 1)
            def normalise_sums(i):
                at_least(v, hn, i)
                v.tensor_tensor(normed[:], window_slice(sh.acc, i * BW, AROW, BW)[0:3 * WIN, :, 0:D],
                                bcast_last(inv[0:3 * WIN, bass.ds(i * BW, BW)], D),
                                ALU.mult).then_inc(norm_ok, 1)

            def copy_xT(i):
                v.wait_ge(x_T, i + 1)
                at_least(v, c2_mm, i)
                v.tensor_copy(xT[:], psA[:, 0:BN]).then_inc(xT_sb, 1)

            normalise_sums(0)
            copy_xT(0)
            normalise_sums(1)

            @staggered(v, ahead=2)
            def _(i, more):
                chain = Chain(v, link, i, 1 + NORM_LINKS)
                v.wait_ge(c2_mm, i + 1)
                at_least(v, x1_out, 16 * i)
                at_least(v, x1_T, i)
                chain.then(v.tensor_tensor(y, tiles_of(psD[:, 0:BN]), bcast_mid(b_c2[:], BT), ALU.add))
                norm.moments(v, chain, y)
                if more:
                    copy_xT(i + 1)
                norm.apply(v, chain, y, i)
                v.sem_inc(x1_ok, 1)
                if more > 1:
                    normalise_sums(i + 2)
                v.wait_ge(x1_T, i + 1)
                at_least(v, h_mm, i)
                v.tensor_copy(x1T[:], psA[:, 0:BN]).then_inc(x1T_sb, 1)
                v.wait_ge(src_mm, i + 1)
                at_least(v, stored, 16 * i)
                v.tensor_copy(sh.src_terms1[:, bass.ds(i * BT, BT)], psA[:, BN:BN + BT])
                v.tensor_copy(table[:, :, D + 1], psA[:, BN:BN + BT]).then_inc(terms_ok, 1)
                chain.close()


SHIFT_MARGIN = 45.0
SLOPE = 0.2
NO_EDGE = -1.0e30


def softmax_edges(nc, sh):
    with ExitStack() as ctx:
        sb, ps, sem = scope(nc, ctx)
        rows = sb("rows1", [P, RING, TROW])
        one_hots = sb("one_hot1", [P, 2, GRP, WIN])
        S = sb("S1", [P, 2, GRP, 2, WIN])
        picked = sb("picked1", [P, GRP, WIN])
        dst_term = sb("dst_term1", [P, GRP])
        z_all = sb("z_all1", [P, TILES])
        far = sb("far1", [P, TILES])
        leaky = sb("leaky1", [P, 2, GRP])
        a = sb("a1", [P, 2, GRP])
        w_all = sb("w_all1", [P, TCOLS])
        top = sb("top1", [P, 2])
        top_src = sb("top_src", [P, 1])
        out = ps("out1", [P, 2, GRP, 256])
        index_ready, granted = sem("index_ready"), sem("granted")
        w_in, top_ok, top_all, shift_link = sem("w_in"), sem("top_ok"), sem("top_all"), sem("shift_link")
        hot_ok, picked_ok, term_ok, z_ok = sem("hot_ok"), sem("picked_ok"), sem("term_ok"), sem("z_ok")
        z_ready, a_ready, s_ready, ws_ok = sem("z_ready"), sem("a_ready"), sem("s_ready"), sem("ws_ok")
        summed, far_link = sem("summed"), sem("far_link")
        added = [sem(f"added{u}") for u in range(GRP)]
        block = ctx.enter_context(nc.Block())

        @block.sync
        def _(sp):
            sp.dma_start(w_all[:], sh.w_dram).then_inc(w_in, 16)
            sp.wait_ge(w_in, 16)

        @block.gpsimd
        def _(pool):
            pool.wait_ge(top_ok, 1)
            pool.partition_all_reduce(top_src[:], top[:, 0:1], P, bass.bass_isa.ReduceOp.max
                                      ).then_inc(top_all, 1)
            with pool.Fori(0, GROUPS // 4) as i:
                for q in range(4):
                    gather_rows(pool, sh.table1, rows, index_ready, granted, sh, i * 4 + q, q)

        @block.scalar
        def _(act):
            def step(i, q):
                n = i * 4 + q
                stage_indices(act, sh, index_ready, summed, n + 2, (q + 2) % 4)
                act.wait_ge(z_ready, n + 1)
                at_least(act, s_ready, n - 1)
                act.activation(a[:, q % 2], leaky[:, q % 2], ACT.Exp,
                               bias=sh.minus_shift[:, 0:1]).then_inc(a_ready, 1)

            for q in range(2):
                stage_indices(act, sh, index_ready, summed, q, q)
            for q in range(4):
                step(0, q)
            with act.Fori(1, GROUPS // 4) as i:
                for q in range(4):
                    step(i, q)

        @block.tensor
        def _(pe):
            def step(i, q):
                n = i * 4 + q
                pe.wait_ge(s_ready, n + 1)
                pe.wait_ge(ws_ok, n + 1)
                at_least(pe, added[GRP - 1], n - 1)
                for u in range(GRP):
                    mm = pe.matmul(out[0:2 * WIN, q % 2, u, 0:AROW],
                                   S[:, q % 2, u].rearrange("p k d -> p (k d)"),
                                   rows[:, GRP * q + u, 0:AROW], start=True, stop=True)
                mm.then_inc(summed, 1)

            for q in range(4):
                step(0, q)
            with pe.Fori(1, GROUPS // 4) as i:
                for q in range(4):
                    step(i, q)

        @block.vector
        def _(v):
            windows = TileWindows(v, sh, "l1")

            def step(i, q, first=False):
                b = q % 2
                tiles = bass.ds((i * 4 + q) * GRP, GRP)
                one_hot = one_hots[:, b]
                adds = iter(()) if first else add_up(v, sh, windows, out, summed, added, i, q, 2 * WIN)
                now, two_ago = upto(v, i, q + 1), upto(v, i, q - 1)
                on(v.tensor_tensor(one_hot, bcast_last(sh.rel_all[:, tiles], WIN),
                                   bcast_mid(sh.iota[:], GRP), ALU.is_equal),
                   summed, two_ago).then_inc(hot_ok, 1)
                windows.load(i, q)
                for u, window in enumerate(windows.of(q)):
                    ins = v.tensor_tensor(picked[:, u], window_slice(sh.dst_terms1, window, WIN),
                                          one_hot[:, u, :], ALU.mult)
                    if u == 0:
                        on(ins, hot_ok, now)
                ins.then_inc(picked_ok, 1)
                v.tensor_tensor(S[:, b, :, 1, :], one_hot, bcast_last(w_all[:, tiles], WIN),
                                ALU.mult).then_inc(ws_ok, 1)
                on(v.tensor_reduce(dst_term[:], picked[:], axis=AX.X, op=ALU.add),
                   picked_ok, now).then_inc(term_ok, 1)
                next(adds, None)
                v.wait_ge(sh.gathered[q], gathered_count(1, i))
                on(v.tensor_tensor(z_all[:, tiles], dst_term[:], rows[:, GRP * q:GRP * q + GRP, D + 1],
                                   ALU.add), term_ok, now).then_inc(z_ok, 1)
                next(adds, None)
                on(v.scalar_tensor_tensor(out=leaky[:, b], in0=z_all[:, tiles], scalar=SLOPE,
                                          in1=z_all[:, tiles], op0=ALU.mult, op1=ALU.max),
                   z_ok, now).then_inc(z_ready, 1)
                for _ in adds:
                    pass
                on(v.tensor_tensor(S[:, b, :, 0, :], one_hot, bcast_last(a[:, b], WIN), ALU.mult),
                   a_ready, now).then_inc(s_ready, 1)

            v.tensor_reduce(top[:, 0:1], sh.src_terms1[:], axis=AX.X, op=ALU.max).then_inc(top_ok, 1)
            once = Chain(v, shift_link)
            once.then(v.tensor_reduce(top[:, 1:2], sh.dst_terms1[:], axis=AX.X, op=ALU.max))
            v.wait_ge(top_all, 1)
            once.then(v.tensor_tensor(top[:, 0:1], top_src[:], top[:, 1:2], ALU.add))
            once.then(v.scalar_tensor_tensor(out=top[:, 1:2], in0=top[:, 0:1], scalar=SLOPE,
                                             in1=top[:, 0:1], op0=ALU.mult, op1=ALU.max))
            once.then(v.tensor_scalar(sh.minus_shift[:], top[:, 1:2], -1.0, SHIFT_MARGIN,
                                      op0=ALU.mult, op1=ALU.add))
            v.wait_ge(w_in, 16)
            for q in range(4):
                step(0, q, first=q == 0)
            with v.Fori(1, GROUPS // 4) as i:
                for q in range(4):
                    step(i, q)
            for _ in add_up(v, sh, windows, out, summed, added, 0, GROUPS, 2 * WIN):
                pass
            last = Chain(v, far_link)
            last.then(v.tensor_scalar(far[:], sh.rel_all[:, 0:TILES], float(WIN), NO_EDGE,
                                      op0=ALU.is_ge, op1=ALU.mult))
            last.then(v.tensor_tensor(far[:], far[:], z_all[:], ALU.add))
            v.tensor_reduce(sh.best[:], far[:], axis=AX.X, op=ALU.max)


GATHERED = 5 * 16


def gather_tiles(sp, sh, sums, width, rows, rows_dram, first_in, rest_in):
    by_tile = sh.acc[0:WIN, :].rearrange("p (c q f) -> p c q f", q=4, f=AROW)
    dram = rows_dram.rearrange("(c p) f -> p c f", p=P)
    for tiles, done in ((slice(0, BT), first_in), (slice(BT, NODE_TILES), rest_in)):
        for q in range(4):
            sp.dma_start(sums[WIN * q:WIN * q + WIN, tiles, 0:width],
                         by_tile[:, tiles, q, 0:width]).then_inc(done, 16)
        sp.dma_start(rows[:, tiles, :], dram[:, tiles, :]).then_inc(done, 16)


def finish_softmax(nc, sh, w):
    with ExitStack() as ctx:
        sb, ps, sem = scope(nc, ctx)
        x_all = sb("x_all2", [P, NODE_TILES, D])
        sums = sb("sums2", [P, NODE_TILES, AROW])
        y = tiles_of(sb("y2", [P, BN])[:])
        act_out = tiles_of(sb("gelu2", [P, BN])[:])
        gamma, beta = sb("gamma2", [P, D]), sb("beta2", [P, D])
        best_all, score, small = sb("best_all", [P, 1]), sb("score2", [P, 1]), sb("small2", [P, 1])
        den, inv = sb("den2", [P, BT]), sb("inv2", [P, BT])
        norm_a, norm_b = Norm(sb, sem, "norm2a"), Norm(sb, sem, "norm2b")
        deg = ps("deg2", [P, NODE_TILES])
        params, best_ok, score_ok, small_ok, small_link = (
            sem(n) for n in ("params", "best_ok", "score_ok", "small_ok", "small_link"))
        deg_mm, link, in_gelu, gelu_ok, x2_ok, stored = (
            sem(n) for n in ("deg_mm", "link", "in_gelu", "gelu_ok", "x2_ok", "stored"))
        first_in, rest_in, cleared = sem("first_in"), sem("rest_in"), sem("cleared")
        block = ctx.enter_context(nc.Block())

        @block.sync
        def _(sp):
            sp.dma_start(gamma[:], row_of(w["L1_gnn_ln_gamma"])).then_inc(params, 16)
            sp.dma_start(beta[:], row_of(w["L1_gnn_ln_beta"])).then_inc(params, 16)
            gather_tiles(sp, sh, sums, AROW, x_all, sh.x1, first_in, rest_in)

            @each_batch(sp)
            def _(i):
                sp.wait_ge(x2_ok, i + 1)
                sp.dma_start(batch_rows(sh.x2, i), x_all[:, bass.ds(i * BT, BT), :]).then_inc(stored, 16)
            sp.wait_ge(stored, 16 * BATCHES)

        @block.gpsimd
        def _(pool):
            pool.partition_all_reduce(best_all[:], sh.best[:], P, bass.bass_isa.ReduceOp.max
                                      ).then_inc(best_ok, 1)
            pool.wait_ge(deg_mm, 1)
            pool.wait_ge(first_in, GATHERED)
            pool.wait_ge(rest_in, GATHERED)
            pool.memset(sh.acc[:], 0.0).then_inc(cleared, 1)
            pool.wait_ge(cleared, 1)

        @block.tensor
        def _(pe):
            for q in range(4):
                col = sh.acc[WIN:2 * WIN, :].rearrange("p (c q f) -> p c q f", q=4, f=AROW)[:, :, q, D]
                mm = pe.matmul(deg[:], sh.place[WIN:2 * WIN, q, :], col, start=q == 0, stop=q == 3)
            mm.then_inc(deg_mm, 1)

        @block.scalar
        def _(act):
            act.wait_ge(score_ok, 1)
            act.activation(small[:], score[:], ACT.Exp, bias=sh.minus_shift[:, 0:1]).then_inc(small_ok, 1)

            @each_batch(act)
            def _(i):
                norm_a.scalar(act, sh, i)
                act.wait_ge(in_gelu, i + 1)
                act.activation(act_out, y, ACT.Gelu).then_inc(gelu_ok, 1)
                norm_b.scalar(act, sh, i)

        @block.vector
        def _(v):
            once = Chain(v, small_link)
            v.wait_ge(best_ok, 1)
            v.scalar_tensor_tensor(out=score[:], in0=best_all[:], scalar=SLOPE, in1=best_all[:],
                                   op0=ALU.mult, op1=ALU.max).then_inc(score_ok, 1)
            v.wait_ge(small_ok, 1)
            once.then(v.tensor_scalar(small[:], small[:], 1e-6, None, op0=ALU.mult))
            v.wait_ge(deg_mm, 1)
            once.then(v.tensor_copy(sh.weight_sum[:], deg[:]))
            v.wait_ge(params, 32)

            @each_batch(v)
            def _(i):
                chain = Chain(v, link, i, 6 + 2 * NORM_LINKS)
                v.wait_ge(first_in if isinstance(i, int) else rest_in, GATHERED)
                out, x_rows = sums[:, bass.ds(i * BT, BT), :], x_all[:, bass.ds(i * BT, BT), :]
                chain.then(v.tensor_scalar(den[:], out[:, :, D], small[:, 0:1], None, op0=ALU.add))
                chain.then(v.reciprocal(inv[:], den[:]))
                for j in range(BT):
                    ins = v.scalar_tensor_tensor(out=y[:, j, :], in0=out[:, j, 0:D],
                                                 scalar=inv[:, j:j + 1], in1=x_rows[:, j, :],
                                                 op0=ALU.mult, op1=ALU.add)
                chain.then(ins)
                norm_a.vector(v, chain, y, i)
                chain.then(v.tensor_tensor(y, y, bcast_mid(gamma[:], BT), ALU.mult))
                chain.then(v.tensor_tensor(y, y, bcast_mid(beta[:], BT), ALU.add))
                v.sem_inc(in_gelu, 1)
                v.wait_ge(gelu_ok, i + 1)
                chain.then(v.tensor_tensor(x_rows, act_out, x_rows, ALU.add))
                norm_b.vector(v, chain, x_rows, i)
                v.sem_inc(x2_ok, 1)
                chain.close()


def relation_edges(nc, sh, w):
    with ExitStack() as ctx:
        sb, ps, sem = scope(nc, ctx)
        rows = sb("rows2", [P, RING, D])
        one_hot = sb("one_hot2", [P, GRP, WIN])
        S = sb("S2", [P, 2, GRP, BASES, WIN])
        types, type_hot = sb("types2", [GRP * RELS, 4, P]), sb("type_hot", [GRP * RELS, 2, P])
        rel_id = sb("rel_id", [GRP * RELS, 1])
        comp = sb("comp", [GRP * RELS, GRP * BASES])
        coef = sb("coef", [P, GRP, BASES])
        T = sb("T2", [P, 2, BASES, GRP, WIN])
        w_base = sb("w_base", [P, BASES, D])
        n_all = sb("n_all2", [P, TCOLS])
        per_base = ps("per_base", [P, 2, GRP, BASES * WIN])
        coef_ps = ps("coef_ps", [P, GRP * BASES])
        summed_ps = ps("summed_ps", [P, 2, 512])
        params, rel_ok, comp_zero = sem("params"), sem("rel_ok"), sem("comp_zero")
        index_ready, granted = sem("index_ready"), sem("granted")
        types_in = [sem(f"types_in{s}") for s in range(4)]
        type_ok, coef_mm, coef_ok, s_ready = sem("type_ok"), sem("coef_mm"), sem("coef_ok"), sem("s_ready")
        based, T_ok, summed = (sem(n) for n in ("based", "T_ok", "summed"))
        added = [sem(f"added{u}") for u in range(GRP)]
        block = ctx.enter_context(nc.Block())
        PARAMS = (2 + GRP) * 16
        assert GRP * RELS == P

        def load_types(sp, n, q):
            at_least(sp, type_ok, n - 3)
            tile_types = sh.type_rows[bass.ds(n * GRP, GRP), :]
            sp.dma_start(types[:, q, :],
                         tile_types.unsqueeze(1).to_broadcast([GRP, RELS, P])).then_inc(types_in[q], 16)

        @block.sync
        def _(sp):
            sp.dma_start(w_base[:], w["L2_gnn_weight"].rearrange("b d f -> d b f")).then_inc(params, 16)
            sp.wait_ge(comp_zero, 1)
            for u in range(GRP):
                sp.dma_start(comp[RELS * u:RELS * u + RELS, BASES * u:BASES * u + BASES],
                             w["L2_gnn_w_comp"]).then_inc(params, 16)
            sp.dma_start(n_all[:], sh.n_dram).then_inc(params, 16)
            for q in range(4):
                load_types(sp, q, q)
            with sp.Fori(1, GROUPS // 4) as i:
                for q in range(4):
                    load_types(sp, i * 4 + q, q)
            load_types(sp, GROUPS, 0)
            sp.wait_ge(params, PARAMS)
            for q in range(4):
                sp.wait_ge(types_in[q], 16 * (GROUPS // 4 + (q == 0)))

        @block.gpsimd
        def _(pool):
            for u in range(GRP):
                at_least(pool, rel_ok, u)
                pool.iota(rel_id[RELS * u:RELS * u + RELS, :], pattern=[[1, 1]], base=0,
                          channel_multiplier=1, allow_small_or_imprecise_dtypes=True).then_inc(rel_ok, 1)
            with pool.Fori(0, GROUPS // 4) as i:
                for q in range(4):
                    gather_rows(pool, sh.x2, rows, index_ready, granted, sh, i * 4 + q, q)

        @block.scalar
        def _(act):
            def step(i, q):
                n = i * 4 + q
                stage_indices(act, sh, index_ready, based, n + 2, (q + 2) % 4)
                act.wait_ge(based, n + 1)
                at_least(act, summed, n - 1)
                for u in range(GRP):
                    ins = act.copy(T[:, q % 2, :, u, :],
                                   per_base[:, q % 2, u, :].rearrange("p (b d) -> p b d", d=WIN))
                ins.then_inc(T_ok, 1)

            for q in range(2):
                stage_indices(act, sh, index_ready, based, q, q)
            for q in range(4):
                step(0, q)
            with act.Fori(1, GROUPS // 4) as i:
                for q in range(4):
                    step(i, q)

        @block.tensor
        def _(pe):
            def coefficients(n, b):
                pe.wait_ge(type_ok, n + 1)
                at_least(pe, coef_ok, n)
                pe.matmul(coef_ps[:], type_hot[:, b, :], comp[:], start=True,
                          stop=True).then_inc(coef_mm, 1)

            def over_bases(n, b):
                pe.wait_ge(T_ok, n + 1)
                at_least(pe, added[GRP - 1], n - 1)
                for k in range(BASES):
                    mm = pe.matmul(summed_ps[:, b, 0:GRP * WIN], w_base[:, k, :],
                                   T[:, b, k].rearrange("p u d -> p (u d)"),
                                   start=k == 0, stop=k == BASES - 1)
                mm.then_inc(summed, 1)

            def step(i, q, first=False):
                n = i * 4 + q
                b = q % 2
                pe.wait_ge(s_ready, n + 1)
                pe.wait_ge(sh.gathered[q], gathered_count(2, i))
                at_least(pe, T_ok, n - 1)
                for u in range(GRP):
                    mm = pe.matmul(per_base[:, b, u, :], rows[:, GRP * q + u, :],
                                   S[:, b, u].rearrange("p k d -> p (k d)"), start=True, stop=True)
                mm.then_inc(based, 1)
                coefficients(n + 1, 1 - b)
                if not first:
                    over_bases(n - 1, 1 - b)

            pe.wait_ge(params, PARAMS)
            coefficients(0, 0)
            for q in range(4):
                step(0, q, first=q == 0)
            with pe.Fori(1, GROUPS // 4) as i:
                for q in range(4):
                    step(i, q)
            over_bases(GROUPS - 1, 1)

        @block.vector
        def _(v):
            windows = TileWindows(v, sh, "l2")

            def type_one_hot(i, q):
                turn = i + q // 4
                v.wait_ge(types_in[q % 4], turn * 16 + 16)
                on(v.tensor_scalar(type_hot[:, q % 2], types[:, q % 4, :], rel_id[:, 0:1], None,
                                   op0=ALU.is_equal),
                   coef_mm, upto(v, i, q - 1)).then_inc(type_ok, 1)

            def add_up_two_ago(i, q):
                into = windows.of((q - 2) % 4)
                done, before = upto(v, i, q - 1), upto(v, i, q - 2)
                for u, window in enumerate(into):
                    to = window_slice(sh.acc, window, WIN)
                    if u == 0:
                        at_least(v, added[GRP - 1], before)
                    ins = v.tensor_tensor(to, to, summed_ps[:, q % 2, WIN * u:WIN * u + WIN], ALU.add)
                    if u == 0:
                        on(ins, summed, done)
                    else:
                        on(ins, added[u - 1], done)
                    ins.then_inc(added[u], 1)
                    yield

            def step(i, q, lag_ok=True):
                b = q % 2
                tiles = bass.ds((i * 4 + q) * GRP, GRP)
                adds = add_up_two_ago(i, q) if lag_ok else iter(())
                now, before, two_ago = (upto(v, i, q + k) for k in (1, 0, -1))
                on(v.tensor_tensor(one_hot[:], bcast_last(sh.rel_all[:, tiles], WIN),
                                   bcast_mid(sh.iota[:], GRP), ALU.is_equal), s_ready, before)
                on(v.tensor_tensor(coef[:], coef_ps[:].rearrange("p (u k) -> p u k", k=BASES),
                                   bcast_last(n_all[:, tiles], BASES), ALU.mult),
                   coef_mm, now).then_inc(coef_ok, 1)
                at_least(v, based, two_ago)
                on(v.tensor_tensor(S[:, b], one_hot[:].unsqueeze(2).to_broadcast([P, GRP, BASES, WIN]),
                                   coef[:].unsqueeze(3).to_broadcast([P, GRP, BASES, WIN]), ALU.mult),
                   coef_ok, now).then_inc(s_ready, 1)
                type_one_hot(i, q + 1)
                for _ in adds:
                    pass
                if q == 1:
                    windows.load_all(i)

            v.memset(comp[:], 0.0).then_inc(comp_zero, 1)
            v.wait_ge(rel_ok, GRP)
            v.wait_ge(params, PARAMS)
            type_one_hot(0, 0)
            for q in range(4):
                step(0, q, lag_ok=q >= 2)
            with v.Fori(1, GROUPS // 4) as i:
                for q in range(4):
                    step(i, q)
            for q in (GROUPS, GROUPS + 1):
                for _ in add_up_two_ago(0, q):
                    pass


def finish_relations(nc, sh, w):
    with ExitStack() as ctx:
        sb, ps, sem = scope(nc, ctx)
        x_all = sb("x_all3", [P, NODE_TILES, D])
        x_rows, y = tiles_of(sb("x_rows3", [P, BN])[:]), tiles_of(sb("y3", [P, BN])[:])
        xT, sums, x3T = sb("xT3", [P, BN]), sb("sums3", [P, BN]), sb("x3T", [P, BN])
        table = tiles_of(sb("table3", [P, BN])[:])
        w_loop, w3, bias = sb("w_loop", [P, D]), sb("w3", [P, D]), sb("bias3", [P, D])
        deg, above, root = sb("deg3", [P, NODE_TILES]), sb("above3", [P, NODE_TILES]), sb("root3", [P, NODE_TILES])
        norm = Norm(sb, sem, "norm3")
        psA, psB, psC, psD = (ps(f"ps3{c}", [P, 1024]) for c in "ABCD")
        params, setup, deg_ok, root_ok, dinv_ok = (
            sem(n) for n in ("params", "setup", "deg_ok", "root_ok", "dinv_ok"))
        x_T, xT_sb, sums_ok, mixed, y_ok, x3_ok, x3_T, x3T_sb, xw, table_ok, stored, x3_out, link = (
            sem(n) for n in ("x_T", "xT_sb", "sums_ok", "mixed", "y_ok", "x3_ok", "x3_T", "x3T_sb",
                             "xw", "table_ok", "stored", "x3_out", "link"))
        first_in, rest_in, x_apart, x3_kept, cleared = (
            sem(n) for n in ("first_in", "rest_in", "x_apart", "x3_kept", "cleared"))
        block = ctx.enter_context(nc.Block())

        @block.sync
        def _(sp):
            rows = sh.x2.rearrange("(c p) f -> p c f", p=P)
            sp.dma_start(x_all[:, 0:BT, :], rows[:, 0:BT, :]).then_inc(first_in, 16)
            sp.dma_start(w_loop[:], w["L2_gnn_loop_weight"]).then_inc(params, 16)
            sp.dma_start(w3[:], w["L3_gnn_W"]).then_inc(params, 16)
            sp.dma_start(bias[:], row_of(w["L2_gnn_h_bias"])).then_inc(params, 16)
            sp.dma_start(x_all[:, BT:NODE_TILES, :], rows[:, BT:NODE_TILES, :]).then_inc(rest_in, 16)

            @each_batch(sp)
            def _(i):
                sp.wait_ge(x3_kept, i + 1)
                sp.dma_start(batch_rows(sh.x3, i), x_all[:, bass.ds(i * BT, BT), :]).then_inc(x3_out, 16)
            sp.wait_ge(x3_out, 16 * BATCHES)

        @block.gpsimd
        def _(pool):
            def set_apart(i):
                at_least(pool, x_T, i)
                pool.tensor_copy(x_rows, x_all[:, bass.ds(i * BT, BT), :]).then_inc(x_apart, 1)

            def clear(i):
                pool.wait_ge(sums_ok, i + 1)
                pool.wait_ge(x_apart, BATCHES if isinstance(i, int) and i == BATCHES - 1 else i + 2)
                at_least(pool, x3_kept, i)
                set_zero(pool, sh, sh.acc[0:WIN, bass.ds(i * BN, BN)]).then_inc(cleared, 1)
                pool.wait_ge(cleared, i + 1)

            pool.wait_ge(first_in, 16)
            set_apart(0)
            pool.wait_ge(rest_in, 16)

            @staggered(pool)
            def _(i, more):
                if more:
                    set_apart(i + 1)
                clear(i)
                pool.wait_ge(x3_ok, i + 1)
                pool.tensor_copy(x_all[:, bass.ds(i * BT, BT), :], y).then_inc(x3_kept, 1)

        @block.tensor
        def _(pe):
            pe.wait_ge(params, 48)

            def transpose_x(i):
                pe.wait_ge(x_apart, i + 1)
                at_least(pe, xT_sb, i)
                transpose_tiles(pe, psA, x_rows, sh.ident).then_inc(x_T, 1)

            def mix(i):
                pe.wait_ge(xT_sb, i + 1)
                pe.wait_ge(sums_ok, i + 1)
                at_least(pe, y_ok, i)
                for j in range(BT):
                    cols = slice(P * j, P * j + P)
                    pe.matmul(psB[:, cols], sums[:, cols], sh.ident[:], start=True, stop=False)
                    mm = pe.matmul(psB[:, cols], xT[:, cols], w_loop[:], start=False, stop=True)
                mm.then_inc(mixed, 1)

            transpose_x(0)
            mix(0)

            @staggered(pe)
            def _(i, more):
                if more:
                    transpose_x(i + 1)
                    mix(i + 1)
                pe.wait_ge(x3_ok, i + 1)
                at_least(pe, x3T_sb, i)
                transpose_tiles(pe, psC, y, sh.ident).then_inc(x3_T, 1)
                pe.wait_ge(x3T_sb, i + 1)
                at_least(pe, table_ok, i)
                for j in range(BT):
                    cols = slice(P * j, P * j + P)
                    mm = pe.matmul(psD[:, cols], x3T[:, cols], w3[:], start=True, stop=True)
                mm.then_inc(xw, 1)

        @block.scalar
        def _(act):
            act.wait_ge(deg_ok, 1)
            act.activation(root[:], deg[:], ACT.Sqrt).then_inc(root_ok, 1)

            def copy_sums(i):
                at_least(act, mixed, i)
                act.copy(sums[:], sh.acc[:, bass.ds(i * BN, BN)]).then_inc(sums_ok, 1)

            copy_sums(0)
            act.wait_ge(dinv_ok, 1)

            @staggered(act)
            def _(i, more):
                if more:
                    copy_sums(i + 1)
                norm.scalar(act, sh, i)
                act.wait_ge(x3_T, i + 1)
                at_least(act, xw, i)
                act.copy(x3T[:], psC[:, 0:BN]).then_inc(x3T_sb, 1)
                act.wait_ge(xw, i + 1)
                at_least(act, stored, 16 * i)
                for j in range(BT):
                    ins = act.activation(table[:, j, :], psD[:, P * j:P * j + P], ACT.Copy,
                                         scale=sh.dinv[:, bass.ds(i * BT + j, 1)])
                ins.then_inc(table_ok, 1)
                act.wait_ge(table_ok, i + 1)
                act.dma_start(batch_rows(sh.table3, i), table).then_inc(stored, 16)
            act.wait_ge(stored, 16 * BATCHES)

        @block.vector
        def _(v):
            once = Chain(v, setup)
            once.then(v.tensor_scalar(deg[:], sh.weight_sum[:], 1.0, None, op0=ALU.add))
            once.then(v.tensor_scalar(above[:], deg[:], 0.0, None, op0=ALU.is_gt))
            v.tensor_scalar(deg[:], deg[:], 1e-35, None, op0=ALU.max).then_inc(deg_ok, 1)
            v.wait_ge(root_ok, 1)
            once.then(v.reciprocal(root[:], root[:]))
            v.tensor_tensor(sh.dinv[:], root[:], above[:], ALU.mult).then_inc(dinv_ok, 1)
            v.wait_ge(params, 48)
            v.wait_ge(first_in, 16)

            def copy_xT(i):
                v.wait_ge(x_T, i + 1)
                at_least(v, mixed, i)
                v.tensor_copy(xT[:], psA[:, 0:BN]).then_inc(xT_sb, 1)

            copy_xT(0)

            @staggered(v)
            def _(i, more):
                chain = Chain(v, link, i, 2 + NORM_LINKS)
                x_rows = x_all[:, bass.ds(i * BT, BT), :]
                v.wait_ge(mixed, i + 1)
                at_least(v, x3_T, i)
                at_least(v, x3_kept, i)
                chain.then(v.tensor_tensor(y, tiles_of(psB[:, 0:BN]), bcast_mid(bias[:], BT), ALU.add))
                v.sem_inc(y_ok, 1)
                if not isinstance(i, int) or i > 0:
                    v.wait_ge(rest_in, 16)
                chain.then(v.scalar_tensor_tensor(out=y, in0=y, scalar=0.0, in1=x_rows,
                                                  op0=ALU.max, op1=ALU.add))
                norm.moments(v, chain, y)
                if more:
                    copy_xT(i + 1)
                norm.apply(v, chain, y, i)
                v.sem_inc(x3_ok, 1)
                chain.close()


def convolution_edges(nc, sh):
    with ExitStack() as ctx:
        sb, ps, sem = scope(nc, ctx)
        rows = sb("rows3", [P, RING, D])
        one_hot = sb("one_hot3", [P, 2, GRP, WIN])
        S = sb("S3", [P, 2, GRP, WIN])
        w_all = sb("w_all3", [P, TCOLS])
        out = ps("out3", [P, 2, GRP, 256])
        index_ready, granted, w_in = sem("index_ready"), sem("granted"), sem("w_in")
        link, s_ready = sem("link"), sem("s_ready")
        summed = sem("summed")
        added = [sem(f"added{u}") for u in range(GRP)]
        block = ctx.enter_context(nc.Block())

        @block.sync
        def _(sp):
            sp.dma_start(w_all[:], sh.w_dram).then_inc(w_in, 16)
            sp.wait_ge(w_in, 16)

        @block.gpsimd
        def _(pool):
            with pool.Fori(0, GROUPS // 4) as i:
                for q in range(4):
                    gather_rows(pool, sh.table3, rows, index_ready, granted, sh, i * 4 + q, q)

        @block.scalar
        def _(act):
            for q in range(4):
                stage_indices(act, sh, index_ready, summed, q, q)
            with act.Fori(1, GROUPS // 4) as i:
                for q in range(4):
                    stage_indices(act, sh, index_ready, summed, i * 4 + q, q)

        @block.tensor
        def _(pe):
            def step(i, q):
                n = i * 4 + q
                pe.wait_ge(s_ready, n + 1)
                at_least(pe, added[GRP - 1], n - 1)
                pe.wait_ge(sh.gathered[q], gathered_count(3, i))
                for u in range(GRP):
                    mm = pe.matmul(out[0:WIN, q % 2, u, 0:D], S[:, q % 2, u, :],
                                   rows[:, GRP * q + u, :], start=True, stop=True)
                mm.then_inc(summed, 1)

            for q in range(4):
                step(0, q)
            with pe.Fori(1, GROUPS // 4) as i:
                for q in range(4):
                    step(i, q)

        @block.vector
        def _(v):
            windows = TileWindows(v, sh, "l3")

            def step(i, q, first=False):
                b = q % 2
                tiles = bass.ds((i * 4 + q) * GRP, GRP)
                now, two_ago = upto(v, i, q + 1), upto(v, i, q - 1)
                on(v.tensor_tensor(one_hot[:, b], bcast_last(sh.rel_all[:, tiles], WIN),
                                   bcast_mid(sh.iota[:], GRP), ALU.is_equal),
                   summed, two_ago).then_inc(link, 1)
                on(v.tensor_tensor(S[:, b], one_hot[:, b], bcast_last(w_all[:, tiles], WIN), ALU.mult),
                   link, now).then_inc(s_ready, 1)
                if not first:
                    for _ in add_up(v, sh, windows, out, summed, added, i, q, WIN, D):
                        pass
                windows.load(i, q)

            v.wait_ge(w_in, 16)
            for q in range(4):
                step(0, q, first=q == 0)
            with v.Fori(1, GROUPS // 4) as i:
                for q in range(4):
                    step(i, q)
            for _ in add_up(v, sh, windows, out, summed, added, 0, GROUPS, WIN, D):
                pass


def finish_convolution(nc, sh, w, result):
    with ExitStack() as ctx:
        sb, ps, sem = scope(nc, ctx)
        own = sb("own4", [P, NODE_TILES, D])
        y = sb("y4", [P, NODE_TILES, D])
        x3 = sh.acc[:, 0:NODE_TILES * D].rearrange("p (c f) -> p c f", f=D)
        bias, gamma, beta = sb("bias4", [P, D]), sb("gamma4", [P, D]), sb("beta4", [P, D])
        real = sb("real4", [P, 1])
        mean, scale = sb("mean4", [P, D]), sb("scale4", [P, D])
        norm = Norm(sb, sem, "norm4")
        total = ps("total4", [P, 2, 512])
        params, real_ok, first_in, rest_in, link1, link2, link3, link4 = (
            sem(n) for n in ("params", "real_ok", "first_in", "rest_in", "link1", "link2", "link3", "link4"))
        y_ok, centred, squared, total_ok, var_in, root_ok, x_in, done, stored = (
            sem(n) for n in ("y_ok", "centred", "squared", "total_ok", "var_in", "root_ok", "x_in",
                             "done", "stored"))
        block = ctx.enter_context(nc.Block())
        FULL = NODE_TILES - 1

        @block.sync
        def _(sp):
            sp.dma_start(bias[:], row_of(w["L3_gnn_b"])).then_inc(params, 16)
            sp.dma_start(gamma[:], row_of(w["L3_gnn_gamma"])).then_inc(params, 16)
            sp.dma_start(beta[:], row_of(w["L3_gnn_beta"])).then_inc(params, 16)
            gather_tiles(sp, sh, y, D, own, sh.table3, first_in, rest_in)
            sp.wait_ge(first_in, GATHERED)
            sp.wait_ge(rest_in, GATHERED)
            sp.dma_start(x3, sh.x3.rearrange("(c p) f -> p c f", p=P)).then_inc(x_in, 16)

            @staggered(sp)
            def _(i, more):
                sp.wait_ge(done, i + 1)
                if more:
                    sp.dma_start(batch_rows(result, i), y[:, bass.ds(i * BT, BT), :]).then_inc(stored, 16)
            sp.dma_start(result[BN * (BATCHES - 1):FULL * P, :].rearrange("(c p) f -> p c f", p=P),
                         y[:, NODE_TILES - BT:FULL, :]).then_inc(stored, 16)
            sp.dma_start(result[FULL * P:N, :], y[0:N - FULL * P, FULL, :]).then_inc(stored, 16)
            sp.wait_ge(stored, 16 * (BATCHES + 1))

        @block.gpsimd
        def _(pool):
            pool.affine_select(out=real[:], in_=sh.ones[:, 0:1], compare_op=ALU.is_gt, fill=0.0,
                               base=N - FULL * P, pattern=[[0, 1]], channel_multiplier=-1
                               ).then_inc(real_ok, 1)

        @block.tensor
        def _(pe):
            for k, (of, ready) in enumerate(((y, y_ok), (own, squared))):
                @staggered(pe)
                def _(i, more):
                    pe.wait_ge(ready, i + 1)
                    for j in range(BT):
                        row = of[:, bass.ds(i * BT + j, 1), :].rearrange("p a f -> p (a f)")
                        mm = pe.matmul(total[:, k, 0:D], sh.ones[:], row,
                                       start=isinstance(i, int) and i + j == 0,
                                       stop=not more and j == BT - 1)
                    mm.then_inc(total_ok, 1)

        @block.scalar
        def _(act):
            @each_batch(act)
            def _(i):
                rows = bass.ds(i * BT, BT)
                act.wait_ge(centred, i + 1)
                act.activation(own[:, rows, :], y[:, rows, :], ACT.Square).then_inc(squared, 1)
            act.wait_ge(var_in, 1)
            act.activation(scale[:], scale[:], ACT.Sqrt, bias=sh.eps[:, 0:1]).then_inc(root_ok, 1)

            @each_batch(act)
            def _(i):
                norm.scalar(act, sh, i)

        @block.vector
        def _(v):
            def mask_padding(chain, i):
                if isinstance(i, int) and i > 0:
                    chain.then(v.tensor_scalar(y[:, FULL, :], y[:, FULL, :], real[:, 0:1], None,
                                               op0=ALU.mult))

            v.wait_ge(real_ok, 1)
            v.wait_ge(params, 48)

            @staggered(v)
            def _(i, more):
                chain = Chain(v, link1, i, 3)
                rows = bass.ds(i * BT, BT)
                v.wait_ge(first_in if isinstance(i, int) and i == 0 else rest_in, GATHERED)
                chain.then(v.tensor_tensor(y[:, rows, :], y[:, rows, :], own[:, rows, :], ALU.add))
                chain.then(v.tensor_tensor(y[:, rows, :], y[:, rows, :],
                                           bcast_last(sh.dinv[:, rows], D), ALU.mult))
                chain.then(v.tensor_tensor(y[:, rows, :], y[:, rows, :], bcast_mid(bias[:], BT), ALU.add))
                chain.close()
                mask_padding(chain, i)
                v.sem_inc(y_ok, 1)
            once = Chain(v, link2)
            v.wait_ge(total_ok, BATCHES)
            once.then(v.tensor_scalar(mean[:], total[:, 0, 0:D], 1.0 / N, None, op0=ALU.mult))

            @staggered(v)
            def _(i, more):
                chain = Chain(v, link3, i, 1)
                rows = bass.ds(i * BT, BT)
                chain.then(v.tensor_tensor(y[:, rows, :], y[:, rows, :], bcast_mid(mean[:], BT),
                                           ALU.subtract))
                chain.close()
                mask_padding(chain, i)
                v.sem_inc(centred, 1)
            v.wait_ge(total_ok, 2 * BATCHES)
            v.tensor_scalar(scale[:], total[:, 1, 0:D], 1.0 / N, None, op0=ALU.mult).then_inc(var_in, 1)
            v.wait_ge(root_ok, 1)
            once.then(v.reciprocal(scale[:], scale[:]))
            once.then(v.tensor_tensor(scale[:], scale[:], gamma[:], ALU.mult))
            v.wait_ge(x_in, 16)

            @each_batch(v)
            def _(i):
                chain = Chain(v, link4, i, 3 + NORM_LINKS)
                rows = y[:, bass.ds(i * BT, BT), :]
                chain.then(v.tensor_tensor(rows, rows, bcast_mid(scale[:], BT), ALU.mult))
                chain.then(v.tensor_tensor(rows, rows, bcast_mid(beta[:], BT), ALU.add))
                chain.then(v.scalar_tensor_tensor(out=rows, in0=rows, scalar=0.0,
                                                  in1=x3[:, bass.ds(i * BT, BT), :],
                                                  op0=ALU.max, op1=ALU.add))
                norm.vector(v, chain, rows, i)
                v.sem_inc(done, 1)
                chain.close()


def build(nc, w, result):
    def dram(name, shape, dt=F32):
        return nc.dram_tensor(name, shape, dt, kind="Internal").ap()

    with ExitStack() as ctx:
        sb, _, _ = scope(nc, ctx)
        sh = Shared()
        _, _, sem = scope(nc, ctx)
        sh.rows_in = sem("rows_in")
        sh.fetched = [[sem(f"fetched{b}{k}") for k in range(5)] for b in range(2)]
        sh.gathered = [sem(f"gathered{q}") for q in range(4)]
        sh.first_sem = sh.gathered[-1].num + 1
        sh.ident, sh.iota, sh.ones = sb("ident", [P, P]), sb("iota", [P, WIN]), sb("ones", [P, P])
        sh.eps, sh.place = sb("eps", [P, 1]), sb("place", [P, 4, P])
        sh.zero = sb("zero", [P, 1])
        sh.src_all, sh.rel_all = sb("src_all", [P, TCOLS], U16), sb("rel_all", [P, TCOLS], BF16)
        sh.win_all, sh.index = sb("win_all", [1, TCOLS], U8), sb("index", [P, RING], I32)
        sh.minus_shift, sh.best = sb("minus_shift", [P, 1]), sb("best_edge", [P, 1])
        sh.weight_sum, sh.dinv = sb("weight_sum", [P, NODE_TILES]), sb("dinv", [P, NODE_TILES])
        sh.acc = sb("acc", [P, WINDOWS * AROW])
        sh.xpad, sh.x1, sh.x2, sh.x3 = (dram(n, (NPAD, D)) for n in ("xpad", "x1", "x2", "x3"))
        sh.table, sh.table1 = dram("table0", (NPAD, TROW)), dram("table1_rows", (NPAD, TROW))
        sh.table3 = dram("table3_rows", (NPAD, D))
        fields = [dram(f"edge_{n}", (EPAD,), dt) for n, dt in
                  (("src", I32), ("dst", I32), ("type", I32), ("weight", F32), ("norm", F32))]
        win_dram = dram("win_dram", (TCOLS,), U8)
        sh.type_rows = dram("types_tiled", (TCOLS, P))
        sh.w_dram, sh.n_dram = dram("weights_tiled", (P, TCOLS)), dram("norms_tiled", (P, TCOLS))

        build_constants(nc, sh)
        zero_semaphores(nc, sh)
        with nc.sbuf_tensor("dst_terms", [P, WINDOWS * 3 * WIN], F32) as sh.dst_terms:
            build_tiles_and_tables(
                nc, sh, w, [w[n] for n in ("src", "dst", "edge_type_32", "edge_weight", "edge_weight1")],
                fields, sh.type_rows, win_dram)
            zero_semaphores(nc, sh)
            attention_edges(nc, sh)
            zero_semaphores(nc, sh)
        with (nc.sbuf_tensor("dst_terms1", [P, NPAD], F32) as sh.dst_terms1,
              nc.sbuf_tensor("src_terms1", [P, NODE_TILES], F32) as sh.src_terms1):
            finish_attention(nc, sh, w)
            zero_semaphores(nc, sh)
            softmax_edges(nc, sh)
            zero_semaphores(nc, sh)
        finish_softmax(nc, sh, w)
        zero_semaphores(nc, sh)
        relation_edges(nc, sh, w)
        zero_semaphores(nc, sh)
        finish_relations(nc, sh, w)
        zero_semaphores(nc, sh)
        convolution_edges(nc, sh)
        zero_semaphores(nc, sh)
        finish_convolution(nc, sh, w, result)


def kernel(**inputs):
    import concourse.bacc as bacc
    from concourse.bass_utils import run_bass_kernel_spmd

    nc = bacc.Bacc("TRN2", target_bir_lowering=False, num_devices=1)
    arrays = {name: np.ascontiguousarray(a) for name, a in inputs.items()}
    arrays["edge_weight1"] = arrays["edge_weight1"].reshape(-1)
    w = {name: nc.dram_tensor(f"in_{name}", a.shape, mybir.dt.from_np(a.dtype), kind="ExternalInput").ap()
         for name, a in arrays.items()}
    result = nc.dram_tensor("out_0", (N, D), F32, kind="ExternalOutput").ap()
    build(nc, w, result)
    r = run_bass_kernel_spmd(nc, [{f"in_{name}": a for name, a in arrays.items()}], core_ids=[0])
    return r.results[0]["out_0"]
```
